# Optimizing a Trainium2 kernel written in Bass

```python
import numpy as np
import jax
import jax.numpy as jnp

def _softmax(x, axis=-1):
    return jax.nn.softmax(x, axis=axis)

def _gelu(x):
    return jax.nn.gelu(x, approximate=True)

def _silu(x):
    return jax.nn.silu(x)

def _sigmoid(x):
    return jax.nn.sigmoid(x)

def _layernorm(x, axis=-1, eps=1e-05):
    m = jnp.mean(x, axis=axis, keepdims=True)
    v = jnp.var(x, axis=axis, keepdims=True)
    return (x - m) / jnp.sqrt(v + eps)

def _scatter_add(tgt, idx, src, axis=0):
    return tgt.at[idx].add(src)

def _segment_sum(src, seg, n):
    return jax.ops.segment_sum(src, seg, n)
kernel_name = 'mk_adaln_d1_jaxref_r8_e9f245'

def setup_inputs(seed: int=0):
    np.random.seed(seed)
    _w = jnp.asarray

    def _L0_attn_setup():
        import jax, jax.numpy as jnp
        import numpy as np
        B, T, D, H = (2, 256, 128, 16)
        DH = D // H
        key = jax.random.key(seed)
        k1, k2, k3 = jax.random.split(key, 3)
        x = jax.random.normal(k1, (B, T, D), dtype=jnp.float32)
        Wqkv = jax.random.normal(k2, (D, 3 * D), dtype=jnp.float32) * (1.0 / np.sqrt(D))
        Wproj = jax.random.normal(k3, (D, D), dtype=jnp.float32) * (1.0 / np.sqrt(D))
        return {'x': x, 'Wqkv': Wqkv, 'Wproj': Wproj}
    _L0_attn_in = _L0_attn_setup()

    def _L0_ffn_setup():
        import jax, jax.numpy as jnp
        import numpy as np
        B, T, D, DFF, E = (4, 256, 128, 512, 8)
        key = jax.random.key(seed)
        ks = jax.random.split(key, 4)
        s_in = 1.0 / np.sqrt(D)
        s_ff = 1.0 / np.sqrt(DFF)
        return {'x': jax.random.normal(ks[0], (B, T, D), dtype=jnp.float32), 'gate_W': jax.random.normal(ks[1], (D, E), dtype=jnp.float32) * s_in, 'gate_b': jnp.zeros((E,), dtype=jnp.float32), 'W1': jax.random.normal(ks[2], (E, D, DFF), dtype=jnp.float32) * s_in, 'b1': jnp.zeros((E, DFF), dtype=jnp.float32), 'W2': jax.random.normal(ks[3], (E, DFF, D), dtype=jnp.float32) * s_ff, 'b2': jnp.zeros((E, D), dtype=jnp.float32)}
    _L0_ffn_in = _L0_ffn_setup()
    _L0_c = _w((lambda *s: np.random.randn(*s).astype(np.float32) * 0.05)(16, 128))
    _L0_wmod = _w((lambda *s: np.random.randn(*s).astype(np.float32) * 0.05)(128, 6 * 128) * 128 ** (-0.5))
    _d = {'L0_attn_x': _L0_attn_in['x'], 'L0_attn_Wqkv': _L0_attn_in['Wqkv'], 'L0_attn_Wproj': _L0_attn_in['Wproj'], 'L0_ffn_gate_W': _L0_ffn_in['gate_W'], 'L0_ffn_gate_b': _L0_ffn_in['gate_b'], 'L0_ffn_W1': _L0_ffn_in['W1'], 'L0_ffn_b1': _L0_ffn_in['b1'], 'L0_ffn_W2': _L0_ffn_in['W2'], 'L0_ffn_b2': _L0_ffn_in['b2'], 'L0_c': _L0_c, 'L0_wmod': _L0_wmod}
    _x0 = _d['L0_attn_x']
    _d['L0_attn_x'] = jax.random.normal(jax.random.fold_in(jax.random.key(seed), 1), (16, 512, 128), dtype=_x0.dtype)
    del _x0
    return _d

def reference(L0_attn_x, L0_attn_Wqkv, L0_attn_Wproj, L0_ffn_gate_W, L0_ffn_gate_b, L0_ffn_W1, L0_ffn_b1, L0_ffn_W2, L0_ffn_b2, L0_c, L0_wmod):

    def _L0_attn_ref(x, Wqkv, Wproj):
        import jax, jax.numpy as jnp
        import numpy as np
        B, T, D, H = (2, 256, 128, 16)
        DH = D // H
        Bx, Tx, C = x.shape
        qkv = x @ Wqkv
        q, k, v = jnp.split(qkv, 3, axis=-1)

        def rs(t):
            return t.reshape(Bx, Tx, H, DH).transpose(0, 2, 1, 3)
        q, k, v = (rs(q), rs(k), rs(v))
        scale = 1.0 / jnp.sqrt(jnp.asarray(DH, dtype=x.dtype))
        att = jnp.einsum('bhqd,bhkd->bhqk', q, k) * scale
        causal = jnp.tril(jnp.ones((Tx, Tx), dtype=bool))
        att = jnp.where(causal[None, None, :, :], att, jnp.asarray(-jnp.inf, dtype=att.dtype))
        att = jax.nn.softmax(att, axis=-1)
        out = jnp.einsum('bhqk,bhkd->bhqd', att, v)
        out = out.transpose(0, 2, 1, 3).reshape(Bx, Tx, C)
        return out @ Wproj

    def _L0_ffn_ref(x, gate_W, gate_b, W1, b1, W2, b2):
        import jax, jax.numpy as jnp
        import numpy as np
        B, T, D, DFF, E = (4, 256, 128, 512, 8)
        b, t, d = x.shape
        num_experts = gate_W.shape[-1]
        logits = jnp.einsum('btd,de->bte', x, gate_W) + gate_b
        top1 = jnp.argmax(logits, axis=-1).reshape(-1)
        flat_x = x.reshape(b * t, d)
        out = jnp.zeros_like(flat_x)
        for e in range(num_experts):
            mask = (top1 == e).astype(x.dtype)[:, None]
            h = jax.nn.gelu(flat_x * mask @ W1[e] + b1[e], approximate=False)
            out = out + (h @ W2[e] + b2[e]) * mask
        return out.reshape(b, t, d)
    x = L0_attn_x
    mod = (_silu(L0_c) @ L0_wmod).reshape(L0_c.shape[0], 6, 1, -1)
    sa, ca, ga, sb, cb, gb = (mod[:, 0], mod[:, 1], mod[:, 2], mod[:, 3], mod[:, 4], mod[:, 5])
    ga = (2 * (ga >= 0) - 1) * jnp.maximum(jnp.abs(ga), 0.25)
    gb = (2 * (gb >= 0) - 1) * jnp.maximum(jnp.abs(gb), 0.25)
    h = _layernorm(x, axis=-1) * (1 + ca) + sa
    x = x + ga * _L0_attn_ref(h, L0_attn_Wqkv, L0_attn_Wproj)
    h = _layernorm(x, axis=-1) * (1 + cb) + sb
    x = x + gb * _L0_ffn_ref(h, L0_ffn_gate_W, L0_ffn_gate_b, L0_ffn_W1, L0_ffn_b1, L0_ffn_W2, L0_ffn_b2)
    return x

_drawn_inputs = setup_inputs


def setup_inputs(seed=0):
    import zlib

    import numpy as np

    out = dict(_drawn_inputs(seed))
    spreads = {'L0_ffn_gate_b': (0.0, 0.1), 'L0_ffn_b1': (0.0, 0.483), 'L0_ffn_b2': (0.0, 0.333)}
    factors = {}
    for name, (base, spread) in spreads.items():
        noise = np.random.default_rng([zlib.crc32(name.encode()), seed]).standard_normal(out[name].shape)
        drawn = base * np.exp(spread * noise) if base else spread * noise
        out[name] = jnp.asarray(drawn.astype(out[name].dtype))
    for name, factor in factors.items():
        out[name] = (out[name] * factor).astype(out[name].dtype)
    return out
```

```python
from contextlib import ExitStack

import concourse.bass as bass
from concourse import mybir

ALU = mybir.AluOpType
ACT = mybir.ActivationFunctionType
F32 = mybir.dt.float32
BF16 = mybir.dt.bfloat16
I32 = mybir.dt.int32
U32 = mybir.dt.uint32
AX_X = mybir.AxisListType.X

P = 128
PARTS = 3
MAX_ROW = 96
NEG = -1e30
BANK = 512
EPS = 1e-5

SLOTS = 40
GROUP_SLOTS = 10
PE_XT, PE_Q, PE_K, PE_V = 4, 7, 11, 13
PE_AT, PE_PROJ, PE_H2T, PE_LOGIT, PE_LOGIT_T, PE_RANK, PE_MAX_T = 15, 17, 24, 26, 28, 32, 36
PV_SLOTS = (3, 5, 7, 9)


def sn_units_at(q):
    return range(min(SLOTS, 5 * q // 4), min(SLOTS, 5 * (q + 1) // 4))


def block_kernel(nc, x, Wqkv, Wproj, gate_W, gate_b, W1, b1, W2, b2, c, wmod, out):
    NB, T, D = x.shape
    E = gate_W.shape[1]
    DFF = W1.shape[2]
    H = 16
    DH = D // H
    NT = T // P
    NG = H // 4
    N = NB * T
    SCALE = float(DH) ** -0.5
    ROWS = PARTS * PARTS * DH
    CAP = N + P
    SPARE = E * CAP
    RW = 388
    IDX = 3 * D
    TILES = N // P + E
    FC = DFF // P
    RING = 4
    NO_TOKEN = float(2 * N)
    assert T == BANK and D == P and NT == 4 and NG == 4 and NB % 2 == 0 and NB >= 6 and TILES % RING == 0

    parts_d = nc.dram_tensor("parts_d", [2, PARTS, DH, H, T], BF16).ap()
    mod_d = nc.dram_tensor("mod_d", [NB, 4, D], F32).ap()
    rows_d = nc.dram_tensor("rows_d", [E * CAP + P, RW], F32).ap()
    b1_d = nc.dram_tensor("b1_d", [PARTS, E * DFF], BF16).ap()
    b2_d = nc.dram_tensor("b2_d", [PARTS, E * D], BF16).ap()

    ctx = ExitStack()
    with ctx:
        def sb(name, shape, dt=F32):
            return ctx.enter_context(nc.sbuf_tensor(name, shape, dt))

        def psum(name, shape, dt=F32):
            return ctx.enter_context(nc.psum_tensor(name, shape, dt))

        def sem(name):
            return ctx.enter_context(nc.semaphore(name))

        sn_ps = psum("sn_ps", [P, 3, BANK])
        st_ps = psum("st_ps", [P, 2, BANK])
        pv_ps = psum("pv_ps", [P, BANK])
        m0_ps = psum("m0_ps", [P, BANK])
        m1_ps = psum("m1_ps", [P, BANK])

        ident = sb("ident", [P, P])
        ident_b = sb("ident_b", [P, P], BF16)
        causal = sb("causal", [P, P], BF16)
        before = sb("before", [P, P], BF16)
        ones_b = sb("ones_b", [P, P], BF16)
        wqkv = sb("wqkv", [P, 3 * D])
        wproj = sb("wproj", [P, D])
        gate_w = sb("gate_w", [P, 32])
        gate_bias = sb("gate_bias", [P, E])
        rank_of_e = sb("rank_of_e", [P, E])
        w1 = sb("w1", [P, E * DFF])
        ones3 = sb("ones3", [PARTS, P], BF16)
        eps = sb("eps", [P, NT])
        half = sb("half", [P, NT])
        modT = sb("modT", [P, 6, NB])
        c_in = sb("c_in", [NB, D])
        c_exp = sb("c_exp", [NB, D])
        c_silu = sb("c_silu", [NB, D])
        c_T = sb("c_T", [P, NB])
        wmod_sb = sb("wmod_sb", [P, 6 * D])
        mod_n = sb("mod_n", [NB, 6, D])
        mod_out = sb("mod_out", [NB, 4, D])
        mod_t0 = sb("mod_t0", [NB, D])
        mod_t1 = sb("mod_t1", [NB, D])
        NBIAS = (E * DFF + E * D) // P
        bias_in = sb("bias_in", [P, NBIAS])
        bias_r = sb("bias_r", [P, NBIAS])
        bias_parts = sb("bias_parts", [P, PARTS, NBIAS], BF16)
        xin = sb("xin", [P, 2, NT, D])
        stats1 = sb("stats1", [P, NT, 6])
        mv1 = sb("mv1", [P, NT, 2])
        var1 = sb("var1", [P, NT])
        rstd1 = sb("rstd1", [P, NT])
        xhat = sb("xhat", [P, NT, D])
        hT = sb("hT", [P, 2, T])
        qk_f = sb("qk_f", [P, 2, T])
        qk_r = sb("qk_r", [P, 2, T])
        qk_parts = sb("qk_parts", [P, 2, PARTS, T], BF16)
        qst = [sb(f"qst{i}", [P, H, T], BF16) for i in range(2)]
        kst = [sb(f"kst{i}", [P, H, T], BF16) for i in range(2)]
        vaug = [sb(f"vaug{i}", [P, NT, H, DH + 1]) for i in range(2)]
        bmax = sb("bmax", [P, H // 2, 5, 4])
        rmax = sb("rmax", [P, NT, H])
        neg_r = sb("neg_r", [P, NT, H])
        neg_parts = sb("neg_parts", [P, NT, PARTS, H], BF16)
        neg_T = sb("neg_T", [PARTS * H, T], BF16)
        probs = [sb(f"probs{i}", [P, 10, T]) for i in range(2)]
        pvs = sb("pvs", [P, 2, T])
        rsum = sb("rsum", [P, NT, 4])
        attn = sb("attn", [P, NT, H, DH])
        attnT = sb("attnT", [P, T])
        wpg = sb("wpg", [P, D])
        xres = sb("xres", [P, 2, NT, D])
        modb = sb("modb", [P, 2, 3, D])
        pack = [sb(f"pack{i}", [P, NT, RW]) for i in range(2)]
        stats2 = sb("stats2", [P, NT, 6])
        mv2 = sb("mv2", [P, NT, 2])
        var2 = sb("var2", [P, NT])
        rstd2 = sb("rstd2", [P, NT])
        xhat2 = sb("xhat2", [P, NT, D])
        h2m = sb("h2m", [P, NT, D])
        h2T = sb("h2T", [P, T])
        logitT = sb("logitT", [P, P])
        logit = sb("logit", [P, NT, E])
        lmax = sb("lmax", [P, NT])
        first = sb("first", [P, NT, E])
        fmax = sb("fmax", [P, NT])
        onehot = sb("onehot", [P, NT, E], BF16)
        posm = sb("posm", [P, NT, E])
        pos = sb("pos", [P, NT])
        pos_u = sb("pos_u", [P, 2, NT], U32)
        base = sb("base", [P, E])
        e_cap = sb("e_cap", [1, E])
        m_128 = sb("m_128", [1, N // P])
        t_iota = sb("t_iota", [1, TILES])
        low_e = sb("low_e", [1, E, E])
        cnt = sb("cnt", [1, E])
        nt_cmp = qk_r[0:1, 0, :].rearrange("p (e n) -> p e n", e=E)[:, :, 0:N // P]
        nt_e = sb("nt_e", [1, E])
        nt_m = sb("nt_m", [1, E, E])
        nt_end = sb("nt_end", [1, E])
        t_ge = hT[0:1, :, :].rearrange("p a t -> p (a t)")[:, 0:TILES * E].rearrange("p (k e) -> p k e", e=E)
        t_gn = qk_f[0:1, :, :].rearrange("p a t -> p (a t)")[:, 0:TILES * E].rearrange("p (k e) -> p k e", e=E)
        t_e = sb("t_e", [1, TILES])
        t_b = sb("t_b", [1, TILES])
        t_row = sb("t_row", [1, TILES])
        t_row1 = sb("t_row1", [1, TILES])
        t_row_i = sb("t_row_i", [1, TILES], I32)
        t_e_i = sb("t_e_i", [1, TILES], I32)
        base_i = sb("base_i", [1, E], I32)
        pad = sb("pad", [P, RW])

        stack_f = qst[0][:, :, :].rearrange("p h t -> p (h t)").bitcast(F32)
        stack_g = qst[1][:, :, :].rearrange("p h t -> p (h t)").bitcast(F32)
        rows = [stack_f[:, i * RW:(i + 1) * RW] for i in range(RING)]
        h2T_b = [stack_f[:, 2048 + i * P:2048 + (i + 1) * P] for i in range(2)]
        y_b = [stack_f[:, 2560 + i * D:2560 + (i + 1) * D] for i in range(RING)]
        ygb = [stack_f[:, 3200 + i * D:3200 + (i + 1) * D] for i in range(2)]
        hg = [stack_g[:, i * DFF:(i + 1) * DFF] for i in range(2)]
        hgT = [stack_g[:, 1024 + i * DFF:1024 + (i + 1) * DFF] for i in range(2)]
        idx_u = sb("idx_u", [P, RING], U32)
        h_ps, gT_ps = sn_ps, st_ps
        y_ps = [sn_ps[:, 2, :], pv_ps[:, :]]
        hT_ps = [m0_ps, m1_ps]
        w2 = kst[0][:, :, :].rearrange("p h t -> p (h t)").bitcast(F32)[:, 0:E * FC * D]
        bias_rows = probs[0][:, :, :].rearrange("p u t -> p (u t)").bitcast(BF16)
        b1p = bias_rows[0:PARTS, 0:E * DFF]
        b2p = bias_rows[0:PARTS, E * DFF:E * (DFF + D)]

        names = """passed const_done ident_done gate_w_zero w_loaded c_loaded c_exp_done silu_done cT_ready cT_done
            modps_ready modn_done modT_ready modT_done modout_done mod_stored bias_loaded bias_step
            bias_stored bias_rows_loaded stacks_zero stacks_ones vaug_ones pv_zero setup_dve
            pad_done wffn_loaded""".split()
        names += """x_loaded ln1_stat ln1_mv rstd1_add rstd1_done xhat_done xT_ready hT_done qk_ready qk_copied
            r1_done qm_done ql_done v_ready v_copied""".split()
        names += """sn_ready sn_read rmax_done neg_hi neg_rest neg_mid neg_done maxT_ready neg_copied
            max_loaded""".split()
        names += """st_ready exp_done masked pv_ready pv_copied pvT_ready rsum_done pvn_done""".split()
        names += """res_loaded wpg_done aT_ready aT_copied proj_ready x1_done ln2_stat ln2_mv rstd2_add rstd2_done
            xhat2_done h2m_done h2_done h2T_ready h2T_copied lgT_ready lgT_copied lg_ready lg_read lmax_done
            first_done fmax_done onehot_done rank_ready posm_done posm_sel pos_done base_done pos_u_done idx_moved
            """.split()
        names += """tab_step tab_done pads_stored tB_ready tB_copied hB_ready gelu_done gT_ready gT_copied yB_ready
            ygb_done y_done idx_done""".split()
        S = {n: sem(n) for n in names}
        parts_stored = [sem(f"parts_stored{i}") for i in range(2)]
        stack_loaded = [sem(f"stack_loaded{g}") for g in range(NG)]
        scattered = [sem(f"scattered{i}") for i in range(2)]
        row_loaded = [sem(f"row_loaded{i}") for i in range(RING)]
        out_stored = [sem(f"out_stored{i}") for i in range(RING)]

        def after(eng, name, per, b, k):
            s = S[name] if isinstance(name, str) else name
            v = per * b + k
            if isinstance(v, int) and v <= 0:
                return
            eng.wait_ge(s, v)

        def stand(eng):
            eng.sem_inc(S["passed"], 1)

        def after_scatter(eng, b, par):
            after(eng, scattered[par], 32, b - par, 64)

        STACK_DMAS = 4
        block = ctx.enter_context(nc.Block())

        def steps(eng, step):
            for s in range(4):
                step(s, s % 2, s < NB, 1 <= s <= NB, s >= 2, s >= 3)
            with eng.Fori(2, NB // 2) as i:
                step(2 * i, 0, True, True, True, True)
                step(2 * i + 1, 1, True, True, True, True)
            for s in range(NB, NB + 3):
                step(s, s % 2, False, s <= NB, s <= NB + 1, True)

        @block.sync
        def _(sp):
            sp.dma_start(c_in[:, :], c).then_inc(S["c_loaded"], 16)
            sp.dma_start(wmod_sb[:, :], wmod).then_inc(S["c_loaded"], 16)
            sp.dma_start(xin[:, 0, :, :], x[0].rearrange("(t p) d -> p t d", p=P)).then_inc(S["x_loaded"], 16)
            sp.wait_ge(S["gate_w_zero"], 1)
            sp.dma_start(gate_w[:, 0:E], gate_W).then_inc(S["w_loaded"], 16)
            sp.dma_start(wqkv[:, :], Wqkv).then_inc(S["w_loaded"], 16)
            sp.dma_start(wproj[:, :], Wproj).then_inc(S["w_loaded"], 16)
            sp.dma_start(gate_bias[:, :], gate_b.partition_broadcast(P)).then_inc(S["w_loaded"], 16)
            nb1 = E * DFF // P
            sp.dma_start(bias_in[:, 0:nb1], b1.rearrange("e (a n) -> (e a) n", n=nb1)).then_inc(S["bias_loaded"], 16)
            sp.dma_start(bias_in[:, nb1:NBIAS], b2.rearrange("e (a n) -> (e a) n", n=E * D // P))\
                .then_inc(S["bias_loaded"], 16)
            sp.wait_ge(S["bias_step"], 5)
            sp.dma_start(b1_d.rearrange("i (p n) -> p i n", p=P), bias_parts[:, :, 0:nb1])\
                .then_inc(S["bias_stored"], 16)
            sp.dma_start(b2_d.rearrange("i (p n) -> p i n", p=P), bias_parts[:, :, nb1:NBIAS])\
                .then_inc(S["bias_stored"], 16)
            sp.wait_ge(S["modout_done"], 1)
            sp.dma_start(mod_d, mod_out[:, :, :]).then_inc(S["mod_stored"], 16)
            sp.wait_ge(S["mod_stored"], 16)

            def step(s, p, qkv, mx, soft, close):
                b = s
                if not isinstance(s, int) or s + 1 < NB:
                    after(sp, "xhat_done", NT, b - 1, NT)
                    nxt = s + 1 if isinstance(s, int) or p == 0 else (s + 1) % NB
                    after(sp, "x_loaded", 16, b, 16)
                    sp.dma_start(xin[:, 1 - p, :, :], xt_d(nxt)).then_inc(S["x_loaded"], 16)
                if qkv:
                    for i in range(2):
                        for g in range(NG):
                            after(sp, stack_loaded[g], 16 * STACK_DMAS, b - 1, 16 * STACK_DMAS) if i == 0 else None
                        after(sp, "ql_done", 2, b, i + 1)
                        for j in range(PARTS):
                            sp.dma_start(parts_d[i, j].rearrange("d h n -> h d n"), qk_parts[:, i, j, :])\
                                .then_inc(parts_stored[i], 16)
                    for i in range(2):
                        after(sp, parts_stored[i], 16 * PARTS, b, 16 * PARTS)
                    if isinstance(s, int) and s == 0:
                        sp.wait_ge(S["stacks_zero"], 8)
                for g in range(NG):
                    if g == NG - 1 and mx:
                        after(sp, "neg_copied", 1, s - 1, 1)
                        sp.dma_start(qst[1 - p][MAX_ROW:MAX_ROW + PARTS, :, :], neg_T[:, :])\
                            .then_inc(S["max_loaded"], 16)
                    if qkv:
                        after(sp, "st_ready", SLOTS, b - 2, GROUP_SLOTS * (g + 1))
                        q_d = parts_d[0].rearrange("i d h n -> (i d) (h n)")[:, 4 * g * T:4 * (g + 1) * T]
                        k_d = parts_d[1].rearrange("i d h n -> i d (h n)")[:, :, 4 * g * T:4 * (g + 1) * T]
                        rows_q = PARTS * DH
                        sp.dma_start(qst[p][0:ROWS, 4 * g:4 * g + 4, :],
                                     q_d.unsqueeze(0).to_broadcast([PARTS, rows_q, 4 * T]))\
                            .then_inc(stack_loaded[g], 16)
                        for j in range(PARTS):
                            sp.dma_start(kst[p][j * rows_q:(j + 1) * rows_q, 4 * g:4 * g + 4, :],
                                         k_d[j].unsqueeze(0).to_broadcast([PARTS, DH, 4 * T]))\
                                .then_inc(stack_loaded[g], 16)
                if soft and (not isinstance(s, int) or s - 2 < NB):
                    cb = s - 2
                    after(sp, "res_loaded", 48, cb - 1, 48)
                    after(sp, "x1_done", 1, cb - 2, 1)
                    sp.dma_start(xres[:, p, :, :], xt_d(cb)).then_inc(S["res_loaded"], 16)
                    after(sp, "h2_done", 1, cb - 2, 1)
                    after(sp, "wpg_done", 1, cb - 2, 1)
                    sp.dma_start(modb[:, p, :, :], mod_row(cb)[0:3, :].partition_broadcast(P))\
                        .then_inc(S["res_loaded"], 16)
                    after_scatter(sp, cb - 2, p)
                    sp.dma_start(pack[p][:, :, 2 * D:3 * D],
                                 mod_row(cb)[3, :].partition_broadcast(P).unsqueeze(1).to_broadcast([P, NT, D]))\
                        .then_inc(S["res_loaded"], 16)

            def xt_d(b):
                return x[b].rearrange("(t p) d -> p t d", p=P)

            def mod_row(b):
                return mod_d[b]

            sp.dma_start(w1[:, :].rearrange("p (e f) -> p e f", e=E), W1.rearrange("e p f -> p e f"))\
                .then_inc(S["wffn_loaded"], 16)

            steps(sp, step)

            sp.wait_ge(S["st_ready"], SLOTS * (NB - 1))
            sp.dma_start(w2.rearrange("p (e c d) -> p e c d", e=E, c=FC),
                         W2.rearrange("e (c p) d -> p e c d", p=P)).then_inc(S["wffn_loaded"], 16)

            sp.wait_ge(S["pv_ready"], NG * NB)
            sp.wait_ge(S["bias_stored"], 32)
            sp.dma_start(b1p, b1_d).then_inc(S["bias_rows_loaded"], 16)
            sp.dma_start(b2p, b2_d).then_inc(S["bias_rows_loaded"], 16)
            sp.wait_ge(S["tab_done"], 1)
            for i in range(2):
                after_scatter(sp, NB - 2 + i, i)
            for e in range(E):
                row = sp.value_load(base_i[0:1, e:e + 1], min_val=0, max_val=SPARE - P)
                sp.dma_start(rows_d[bass.ds(row, P), :], pad[:, :]).then_inc(S["pads_stored"], 16)
            sp.dma_start(rows_d[SPARE:SPARE + P, :], pad[:, :]).then_inc(S["pads_stored"], 16)
            sp.wait_ge(S["pads_stored"], 16 * (E + 1))

            def load(k, r, n):
                if not (isinstance(n, int) and n == 0):
                    after(sp, out_stored[r], 16, n - 1, 16)
                row = sp.value_load(t_row_i[0:1, bass.ds(k, 1)], min_val=0, max_val=SPARE)
                sp.dma_start(rows[r], rows_d[bass.ds(row, P), :]).then_inc(row_loaded[r], 16)

            for r in range(RING):
                load(r, r, 0)
            with sp.Fori(1, TILES // RING) as n:
                for r in range(RING):
                    load(RING * n + r, r, n)

        @block.gpsimd
        def _(pool):
            g = nc.gpsimd

            for m in (ident, ident_b):
                g.memset(m[:, :], 0.0).then_inc(S["ident_done"], 1)
            g.memset(causal[:, :], 0.0).then_inc(S["ident_done"], 1)
            g.memset(before[:, :], 1.0).then_inc(S["ident_done"], 1)
            g.memset(gate_w[:, :], 0.0).then_inc(S["gate_w_zero"], 1)
            pool.wait_ge(S["ident_done"], 4)
            for m in (ident, ident_b):
                g.affine_select(out=m[:, :], in_=m[:, :], compare_op=ALU.not_equal, fill=1.0, base=0,
                                pattern=[[-1, P]], channel_multiplier=1).then_inc(S["const_done"], 1)
            g.affine_select(out=causal[:, :], in_=causal[:, :], compare_op=ALU.is_ge, fill=NEG, base=0,
                            pattern=[[-1, P]], channel_multiplier=1).then_inc(S["const_done"], 1)
            g.affine_select(out=before[:, :], in_=before[:, :], compare_op=ALU.is_gt, fill=0.0, base=0,
                            pattern=[[1, P]], channel_multiplier=-1).then_inc(S["const_done"], 1)
            g.memset(ones_b[:, :], 1.0).then_inc(S["const_done"], 1)
            g.memset(ones3[:, :], 1.0).then_inc(S["const_done"], 1)
            g.memset(eps[:, :], EPS).then_inc(S["const_done"], 1)
            g.memset(half[:, :], -0.5).then_inc(S["const_done"], 1)
            g.iota(rank_of_e[:, :], pattern=[[-1, E]], base=E, channel_multiplier=0,
                   allow_small_or_imprecise_dtypes=True).then_inc(S["const_done"], 1)
            g.iota(base[:, :], pattern=[[CAP, E]], base=0, channel_multiplier=0,
                   allow_small_or_imprecise_dtypes=True).then_inc(S["const_done"], 1)
            g.iota(e_cap[:, :], pattern=[[CAP, E]], base=0, channel_multiplier=0,
                   allow_small_or_imprecise_dtypes=True).then_inc(S["const_done"], 1)
            g.iota(m_128[:, :], pattern=[[P, N // P]], base=0, channel_multiplier=0,
                   allow_small_or_imprecise_dtypes=True).then_inc(S["const_done"], 1)
            g.iota(t_iota[:, :], pattern=[[1, TILES]], base=0, channel_multiplier=0,
                   allow_small_or_imprecise_dtypes=True).then_inc(S["const_done"], 1)
            g.memset(low_e[:, :, :], 1.0).then_inc(S["ident_done"], 1)
            pool.wait_ge(S["ident_done"], 5)
            g.affine_select(out=low_e[:, :, :], in_=low_e[:, :, :], compare_op=ALU.is_ge, fill=0.0, base=0,
                            pattern=[[1, E], [-1, E]], channel_multiplier=0).then_inc(S["const_done"], 1)
            for i in range(2):
                g.memset(pack[i][:, :, IDX:RW], 0.0).then_inc(S["ident_done"], 1)
                pool.wait_ge(S["ident_done"], 6 + i)
                g.iota(pack[i][:, :, IDX:IDX + 1], pattern=[[P, NT], [0, 1]], base=(i - 2) * T, channel_multiplier=1,
                       allow_small_or_imprecise_dtypes=True).then_inc(S["const_done"], 1)
            g.memset(pad[:, :], 0.0).then_inc(S["ident_done"], 1)
            pool.wait_ge(S["ident_done"], 8)
            g.memset(pad[:, IDX:IDX + 1], NO_TOKEN).then_inc(S["pad_done"], 1)
            for i in range(2):
                g.memset(vaug[i][:, :, :, DH:DH + 1], 1.0).then_inc(S["vaug_ones"], 1)
            pool.wait_ge(S["const_done"], 16)

            def rstd(mv, var, r, add, done, b):
                g.tensor_tensor(var[:, :], mv[:, :, 1], eps[:, :], op=ALU.add).then_inc(S[add], 1)
                after(pool, add, 1, b, 1)
                g.tensor_tensor(r[:, :], var[:, :], half[:, :], op=ALU.pow).then_inc(S[done], 1)

            def split(b, i):
                after(pool, "qk_copied", 4, b, 2 * i + 2)
                g.tensor_tensor(qk_r[:, i, :], qk_f[:, i, :], qk_parts[:, i, 0, :], op=ALU.subtract)\
                    .then_inc(S["r1_done"], 1)

            def split_last(b, i):
                after(pool, "qm_done", 2, b, i + 1)
                g.tensor_tensor(qk_parts[:, i, 2, :], qk_r[:, i, :], qk_parts[:, i, 1, :], op=ALU.subtract)\
                    .then_inc(S["ql_done"], 1)

            def mask(b, pair):
                after(pool, "exp_done", SLOTS, b, 5 * (pair + 1))
                stand(pool)
                v = probs[pair // 2 % 2][:, 5 * (pair % 2):5 * (pair % 2) + 5, :]
                for blocks, n in ((v[:, 0:4:2, 0:P], (2, 1)),
                                  (v[:, 1:5:2, 0:2 * P].rearrange("p a (b n) -> p a b n", b=2), (2, 2)),
                                  (v[:, 4, :].rearrange("p (a n) -> p a n", a=2)[:, :, 0:P], (2, 1))):
                    pat = [[0, n[0]], [0, n[1]], [1, P]] if n[1] > 1 else [[0, n[0]], [1, P]]
                    last = g.affine_select(out=blocks, in_=blocks, compare_op=ALU.is_ge, fill=0.0, base=0,
                                           pattern=pat, channel_multiplier=-1)
                last.then_inc(S["masked"], 1)

            def step(s, p, qkv, mx, soft, close):
                for q in range(SLOTS):
                    if soft and q % 5 == 1 and q > 1:
                        mask(s - 2, q // 5 - 1)
                    if qkv and q == 1:
                        after(pool, "ln1_mv", NT, s, NT)
                        after(pool, "xhat_done", NT, s - 1, NT)
                        rstd(mv1, var1, rstd1, "rstd1_add", "rstd1_done", s)
                    if close and q == 2:
                        b = s - 3
                        after(pool, "res_loaded", 48, b, 48)
                        after(pool, "proj_ready", 1, b - 1, 1)
                        g.tensor_tensor(wpg[:, :], wproj[:, :], modb[:, 1 - p, 0, :], op=ALU.mult)\
                            .then_inc(S["wpg_done"], 1)
                        after_scatter(pool, b - 2, 1 - p)
                        stand(pool)
                        col = pack[1 - p][:, :, IDX:IDX + 1]
                        g.tensor_scalar(col, col, float(2 * T), None, op0=ALU.add).then_inc(S["idx_moved"], 1)
                    if qkv and q == 9:
                        if not (isinstance(s, int) and s == 0):
                            pass
                        split(s, 0)
                    if qkv and q == 12:
                        split_last(s, 0)
                    if qkv and q == 13:
                        split(s, 1)
                    if qkv and q == 15:
                        split_last(s, 1)
                    if close and q == PE_PROJ + 2:
                        after(pool, "ln2_mv", NT, s - 3, NT)
                        after(pool, "xhat2_done", NT, s - 4, NT)
                        rstd(mv2, var2, rstd2, "rstd2_add", "rstd2_done", s - 3)
                    if close and q == PE_PROJ + 4:
                        b = s - 3
                        mb = modb[:, 1 - p, :, :]
                        after(pool, "xhat2_done", NT, b, NT)
                        g.tensor_tensor(h2m[:, :, :], xhat2[:, :, :],
                                        mb[:, 1, :].unsqueeze(1).to_broadcast([P, NT, D]), op=ALU.mult)\
                            .then_inc(S["h2m_done"], 1)
                        after(pool, "h2m_done", 1, b, 1)
                        g.tensor_tensor(pack[1 - p][:, :, 0:D], h2m[:, :, :],
                                        mb[:, 2, :].unsqueeze(1).to_broadcast([P, NT, D]), op=ALU.add)\
                            .then_inc(S["h2_done"], 1)
                    if close and q == PE_RANK + 2:
                        b = s - 3
                        after(pool, "pos_u_done", 1, b, 1)
                        after(pool, "x1_done", 1, b, 1)
                        after(pool, "h2_done", 1, b, 1)
                        after(pool, "idx_moved", 1, b, 1)
                        stand(pool)
                        for t in range(NT):
                            g.indirect_dma_start(
                                out=rows_d, out_offset=bass.IndirectOffsetOnAxis(ap=pos_u[:, 1 - p, t:t + 1], axis=0),
                                in_=pack[1 - p][:, t, :], in_offset=None, bounds_check=E * CAP - 1, oob_is_err=False)\
                                .then_inc(scattered[1 - p], 16)
                if soft:
                    mask(s - 2, 7)

            steps(pool, step)

            def store(k, r, n):
                after(pool, row_loaded[r], 16, n, 16)
                stand(pool)
                g.tensor_copy(idx_u[:, r:r + 1], rows[r][:, IDX:IDX + 1]).then_inc(S["idx_done"], 1)
                pool.wait_ge(S["idx_done"], k + 1)
                pool.wait_ge(S["y_done"], k + 1)
                stand(pool)
                g.indirect_dma_start(
                    out=out.rearrange("b t d -> (b t) d"),
                    out_offset=bass.IndirectOffsetOnAxis(ap=idx_u[:, r:r + 1], axis=0),
                    in_=y_b[r], in_offset=None, bounds_check=N - 1, oob_is_err=False).then_inc(out_stored[r], 16)

            with pool.Fori(0, TILES // RING) as n:
                for r in range(RING):
                    store(RING * n + r, r, n)
            for r in range(RING):
                pool.wait_ge(out_stored[r], 16 * (TILES // RING))

        @block.scalar
        def _(act):
            a = nc.scalar
            act.wait_ge(S["c_loaded"], 32)
            a.activation(c_exp[:, :], c_in[:, :], ACT.Exp, scale=-1.0).then_inc(S["c_exp_done"], 1)
            act.wait_ge(S["modT_done"], 2)

            def copy_out(dst, src, name):
                a.activation(dst, src, ACT.Copy).then_inc(S[name], 1)

            def exp(b, q):
                gr = q // GROUP_SLOTS
                if q % GROUP_SLOTS == 0:
                    after(act, "pv_ready", NG, b, gr - 1)
                after(act, "st_ready", SLOTS, b, q + 1)
                a.activation(probs[gr % 2][:, q % GROUP_SLOTS, :], st_ps[:, q % 2, :], ACT.Exp, scale=SCALE)\
                    .then_inc(S["exp_done"], 1)

            def pv_copy(b, gr):
                after(act, "pv_ready", NG, b, gr + 1)
                after(act, "pvT_ready", NG, b, gr - 1)
                copy_out(pvs[:, gr % 2, :], pv_ps[:, :], "pv_copied")

            def step(s, p, qkv, mx, soft, close):
                for q in range(SLOTS):
                    if close and q == 0:
                        pv_copy(s - 3, 2)
                    if close and q == 10:
                        pv_copy(s - 3, 3)
                    if soft and q == 20:
                        pv_copy(s - 2, 0)
                    if soft and q == 30:
                        pv_copy(s - 2, 1)
                    if qkv and q == PE_XT + 1:
                        after(act, "xT_ready", 1, s, 1)
                        after(act, "v_ready", 1, s - 2, 1)
                        a.activation(hT[:, p, :], m0_ps[:, :], ACT.Identity, bias=modT[:, 0, bass.ds(s, 1)],
                                     scale=modT[:, 1, bass.ds(s, 1)]).then_inc(S["hT_done"], 1)
                    for i, at in ((0, PE_Q + 1), (1, PE_K + 1)):
                        if qkv and q == at:
                            after(act, "qk_ready", 2, s, i + 1)
                            after(act, parts_stored[i], 16 * PARTS, s - 1, 16 * PARTS)
                            copy_out(qk_f[:, i, :], m0_ps[:, :], "qk_copied")
                            copy_out(qk_parts[:, i, 0, :], m0_ps[:, :], "qk_copied")
                    if mx and q == PE_V + 1:
                        b = s - 1
                        after(act, "v_ready", 1, b, 1)
                        after(act, "pv_ready", NG, b - 2, NG)
                        a.activation(vaug[1 - p][:, :, :, 0:DH],
                                     m1_ps[:, :].rearrange("p (t h d) -> p t h d", t=NT, h=H), ACT.Copy)\
                            .then_inc(S["v_copied"], 1)
                    if mx and q == PE_MAX_T + 1:
                        after(act, "maxT_ready", 1, s - 1, 1)
                        after(act, "max_loaded", 16, s - 2, 16)
                        copy_out(neg_T[:, :], m1_ps[0:PARTS * H, :].bitcast(BF16)[:, 0:T], "neg_copied")
                    if close and q == PE_AT + 1:
                        after(act, "aT_ready", 1, s - 3, 1)
                        after(act, "proj_ready", 1, s - 4, 1)
                        copy_out(attnT[:, :], m0_ps[:, :], "aT_copied")
                    if close and q == PE_H2T + 1:
                        after(act, "h2T_ready", 1, s - 3, 1)
                        after(act, "lgT_ready", 1, s - 4, 1)
                        copy_out(h2T[:, :], m0_ps[:, :], "h2T_copied")
                    if close and q == PE_LOGIT + 1:
                        after(act, "lgT_ready", 1, s - 3, 1)
                        after(act, "lg_ready", 1, s - 4, 1)
                        copy_out(logitT[:, :], m0_ps[:, 0:P], "lgT_copied")
                    if soft:
                        exp(s - 2, q)

            steps(act, step)

            def gelu(k, r):
                act.wait_ge(S["hB_ready"], k + 1)
                if not (isinstance(k, int) and k < 2):
                    after(act, "gT_ready", 1, k, -1)
                a.activation(hg[r], h_ps[:, r, :], ACT.Gelu).then_inc(S["gelu_done"], 1)

            gelu(0, 0)
            gelu(1, 1)
            with act.Fori(1, TILES // 2) as n:
                gelu(2 * n, 0)
                gelu(2 * n + 1, 1)

        @block.tensor
        def _(pe):
            t_ = nc.tensor

            def mm(o, l, r, start=True, stop=True):
                return t_.matmul(o, l, r, start=start, stop=stop, skip_group_check=True)

            pe.wait_ge(S["const_done"], 16)
            pe.wait_ge(S["silu_done"], 1)
            t_.transpose(m0_ps[:, 0:NB], c_silu[:, :], ident[0:NB, 0:NB]).then_inc(S["cT_ready"], 1)
            pe.wait_ge(S["cT_done"], 1)
            mm(m0_ps[0:NB, :], c_T[:, :], wmod_sb[:, 0:BANK])
            mm(m1_ps[0:NB, 0:6 * D - BANK], c_T[:, :], wmod_sb[:, BANK:6 * D]).then_inc(S["modps_ready"], 1)
            for i in range(6):
                last = mm(pv_ps[:, i * NB:(i + 1) * NB], wmod_sb[:, i * D:(i + 1) * D], c_T[:, :])
            last.then_inc(S["modT_ready"], 1)
            pe.wait_ge(S["modn_done"], 2)
            pe.wait_ge(S["modT_done"], 2)
            pe.wait_ge(S["w_loaded"], 64)
            pe.wait_ge(S["stacks_zero"], 8)
            pe.wait_ge(S["stacks_ones"], 2)
            pe.wait_ge(S["vaug_ones"], 2)
            pe.wait_ge(S["pv_zero"], 1)

            def sn_unit(b, par, u):
                gr, pair, k = u // GROUP_SLOTS, u // 5, u % 5
                if u % GROUP_SLOTS == 0:
                    after(pe, stack_loaded[gr], 16 * STACK_DMAS, b, 16 * STACK_DMAS)
                after(pe, "sn_read", SLOTS, b, max(u - 2, 0))
                o = sn_ps[:, u % 3, :]
                parts = {0: [(0, 3, 0)], 1: [(0, 0, 0), (0, 2, P)], 2: [(1, 3, 0)], 3: [(1, 0, 0), (1, 2, P)],
                         4: [(0, 1, 0), (1, 1, 2 * P)]}[k]
                for hd, t, col in parts:
                    h = 2 * pair + hd
                    mm(o[:, col:col + (t + 1) * P], qst[par][0:ROWS, h, t * P:(t + 1) * P],
                       kst[par][0:ROWS, h, 0:(t + 1) * P], stop=False)
                    last = mm(o[:, col + t * P:col + (t + 1) * P], ident_b[:, :], causal[:, :], start=False)
                last.then_inc(S["sn_ready"], 1)

            def st_unit(b, par, u):
                pair, k = u // 5, u % 5
                if u == 0:
                    after(pe, "max_loaded", 16, b, 16)
                after(pe, "exp_done", SLOTS, b, u - 1)
                o = st_ps[:, u % 2, :]
                parts = {0: [(0, 0, 0)], 1: [(0, 3, 0), (0, 1, P)], 2: [(1, 0, 0)], 3: [(1, 3, 0), (1, 1, P)],
                         4: [(0, 2, 0), (1, 2, 2 * P)]}[k]
                for hd, t, col in parts:
                    h = 2 * pair + hd
                    last = mm(o[:, col:col + T - t * P], kst[par][:, h, t * P:(t + 1) * P],
                              qst[par][:, h, t * P:T])
                last.then_inc(S["st_ready"], 1)

            def pv(b, par, gr, j):
                if j == 0:
                    after(pe, "masked", H // 2, b, 2 * gr + 2)
                    after(pe, "pv_copied", NG, b, gr)
                    after(pe, "v_copied", 1, b, 1)
                for hd in range(4):
                    base_u, X = 5 * (hd // 2), hd % 2
                    u, col = {0: (2 * X, 0), 1: (2 * X + 1, P), 2: (4, 2 * P * X), 3: (2 * X + 1, 0)}[j]
                    last = mm(pv_ps[32 * hd:32 * hd + DH + 1, j * P:T], vaug[par][:, j, 4 * gr + hd, :],
                              probs[gr % 2][:, base_u + u, col:col + T - j * P], start=j == 0, stop=j == NT - 1)
                if j == NT - 1:
                    last.then_inc(S["pv_ready"], 1)

            def pv_transpose(b, gr):
                after(pe, "pv_copied", NG, b, gr + 1)
                for t in range(NT):
                    last = t_.transpose(m1_ps[:, t * P:(t + 1) * P], pvs[:, gr % 2, t * P:(t + 1) * P], ident[:, :])
                last.then_inc(S["pvT_ready"], 1)

            def four_transposes(ps, src, name):
                for t in range(NT):
                    last = t_.transpose(ps[:, t * P:(t + 1) * P], src[:, t, :], ident[:, :])
                last.then_inc(S[name], 1)

            def step(s, p, qkv, mx, soft, close):
                for q in range(SLOTS):
                    if close and q == 1:
                        after(pe, "neg_copied", 1, s - 2, 1) if (not isinstance(s, int) or s - 2 < NB) else None
                        after(pe, "pvn_done", NG, s - 3, 2)
                        pv_transpose(s - 3, 2)
                    if close and q == 11:
                        after(pe, "pvn_done", NG, s - 3, 3)
                        pv_transpose(s - 3, 3)
                    if soft and q == 21:
                        if s - 1 < NB if isinstance(s, int) else True:
                            after(pe, "v_copied", 1, s - 1, 1)
                        after(pe, "pvn_done", NG, s - 3, NG)
                        pv_transpose(s - 2, 0)
                    if soft and q == 31:
                        after(pe, "pvn_done", NG, s - 2, 1)
                        pv_transpose(s - 2, 1)
                    if qkv and q == PE_XT:
                        after(pe, "xhat_done", NT, s, NT)
                        after(pe, "qk_copied", 4, s - 1, 4)
                        after(pe, "base_done", 1, s - 4, 1)
                        four_transposes(m0_ps, xhat, "xT_ready")
                    for i, at in ((0, PE_Q), (1, PE_K)):
                        if qkv and q == at:
                            after(pe, "hT_done", 1, s, 1)
                            after(pe, "qk_copied", 4, s, 2 * i)
                            mm(m0_ps[:, :], wqkv[:, i * D:(i + 1) * D], hT[:, p, :]).then_inc(S["qk_ready"], 1)
                    if mx and q == PE_V:
                        after(pe, "hT_done", 1, s - 1, 1)
                        after(pe, "neg_copied", 1, s - 2, 1)
                        after(pe, "pvn_done", NG, s - 3, NG)
                        for t in range(NT):
                            last = mm(m1_ps[:, t * P:(t + 1) * P], hT[:, 1 - p, t * P:(t + 1) * P],
                                      wqkv[:, 2 * D:3 * D])
                        last.then_inc(S["v_ready"], 1)
                    if mx and q == PE_MAX_T:
                        after(pe, "neg_done", 1, s - 1, 1)
                        after(pe, "v_copied", 1, s - 1, 1)
                        after(pe, "pvn_done", NG, s - 2, 2)
                        stand(pe)
                        for t in range(NT):
                            last = t_.transpose(
                                m1_ps[0:PARTS * H, :].bitcast(BF16)[:, t * P:(t + 1) * P],
                                neg_parts[:, t, :, :].rearrange("p i h -> p (i h)"), ident_b[:, :])
                        last.then_inc(S["maxT_ready"], 1)
                    if close:
                        b = s - 3
                        if q == PE_AT:
                            after(pe, "pvn_done", NG, b, NG)
                            if qkv:
                                after(pe, "qk_copied", 4, s, 4)
                            else:
                                after(pe, "base_done", 1, b - 1, 1)
                            four_transposes(m0_ps, attn[:, :, :, :].rearrange("p t h d -> p t (h d)"), "aT_ready")
                        if q == PE_PROJ:
                            after(pe, "aT_copied", 1, b, 1)
                            after(pe, "wpg_done", 1, b, 1)
                            for t in range(NT):
                                last = mm(m0_ps[:, t * P:(t + 1) * P], attnT[:, t * P:(t + 1) * P], wpg[:, :])
                            last.then_inc(S["proj_ready"], 1)
                        if q == PE_H2T:
                            after(pe, "x1_done", 1, b, 1)
                            after(pe, "h2_done", 1, b, 1)
                            four_transposes(m0_ps, pack[1 - p][:, :, 0:D], "h2T_ready")
                        if q == PE_LOGIT:
                            after(pe, "h2T_copied", 1, b, 1)
                            for t in range(NT):
                                last = mm(m0_ps[32 * t:32 * t + 32, 0:P], gate_w[:, :], h2T[:, t * P:(t + 1) * P])
                            last.then_inc(S["lgT_ready"], 1)
                        if q == PE_LOGIT_T:
                            after(pe, "lgT_copied", 1, b, 1)
                            t_.transpose(m0_ps[:, 0:P], logitT[:, :], ident[:, :]).then_inc(S["lg_ready"], 1)
                        if q == PE_RANK:
                            after(pe, "onehot_done", 1, b, 1)
                            after(pe, "lg_read", 1, b, 1)
                            for t in range(NT + 1):
                                o = m0_ps[:, t * E:(t + 1) * E]
                                for u in range(min(t, NT)):
                                    last = mm(o, ones_b[:, :], onehot[:, u, :], start=u == 0, stop=u == NT - 1)
                                if t < NT:
                                    last = mm(o, before[:, :], onehot[:, t, :], start=t == 0)
                            last.then_inc(S["rank_ready"], 1)
                    if mx:
                        for u in sn_units_at(q):
                            sn_unit(s - 1, 1 - p, u)
                    if soft:
                        st_unit(s - 2, p, q)
                    if q % GROUP_SLOTS in PV_SLOTS:
                        j = PV_SLOTS.index(q % GROUP_SLOTS)
                        gr = q // GROUP_SLOTS - 1
                        if gr < 0 and close:
                            pv(s - 3, 1 - p, 3, j)
                        if gr >= 0 and soft:
                            pv(s - 2, p, gr, j)

            steps(pe, step)

            pe.wait_ge(S["wffn_loaded"], 32)
            pe.wait_ge(S["bias_rows_loaded"], 32)
            pe.wait_ge(S["tab_done"], 1)

            def load_expert(k):
                return pe.value_load(t_e_i[0:1, bass.ds(k, 1)], min_val=0, max_val=E - 1)

            def up(k, r4, n):
                r = r4 % 2
                after(pe, row_loaded[r4], 16, n, 16)
                if not (isinstance(k, int) and k < 2):
                    after(pe, "hB_ready", 1, k, -1)
                    after(pe, "tB_copied", 1, k, -1)
                t_.transpose(hT_ps[r][:, 0:P], rows[r4][:, 0:D], ident[:, :]).then_inc(S["tB_ready"], 1)
                e = load_expert(k)
                if not (isinstance(k, int) and k < 2):
                    after(pe, "gelu_done", 1, k, -1)
                mm(h_ps[:, r, :], ones3[:, :], b1p[:, bass.ds(e * DFF, DFF)], stop=False)
                after(pe, "tB_copied", 1, k, 1)
                mm(h_ps[:, r, :], h2T_b[r], w1[:, bass.ds(e * DFF, DFF)], start=False).then_inc(S["hB_ready"], 1)

            def down(k, r):
                after(pe, "gelu_done", 1, k, 1)
                if not (isinstance(k, int) and k < 2):
                    after(pe, "gT_copied", 1, k, -1)
                for f in range(FC):
                    last = t_.transpose(gT_ps[:, r, f * P:(f + 1) * P], hg[r][:, f * P:(f + 1) * P], ident[:, :])
                last.then_inc(S["gT_ready"], 1)
                e = load_expert(k)
                if not (isinstance(k, int) and k < 2):
                    after(pe, "ygb_done", 1, k, -1)
                mm(y_ps[r][:, 0:D], ones3[:, :], b2p[:, bass.ds(e * D, D)], stop=False)
                after(pe, "gT_copied", 1, k, 1)
                for f in range(FC):
                    last = mm(y_ps[r][:, 0:D], hgT[r][:, f * P:(f + 1) * P],
                              w2[:, bass.ds(e * (FC * D) + f * D, D)], start=False, stop=f == FC - 1)
                last.then_inc(S["yB_ready"], 1)

            up(0, 0, 0)
            for k in range(3):
                up(k + 1, k + 1, 0)
                down(k, k % 2)
            with pe.Fori(1, TILES // RING) as n:
                for r in range(RING):
                    up(RING * n + r, r, n)
                    down(RING * n + r - 1, (r + 1) % 2)
            down(TILES - 1, 1)

        @block.vector
        def _(dve):
            v = nc.vector

            for i in range(2):
                v.memset(qst[i][64:P, :, :].rearrange("p h t -> p (h t)").bitcast(U32), 0).then_inc(S["stacks_zero"], 2)
                v.memset(kst[i][64:P, :, :].rearrange("p h t -> p (h t)").bitcast(U32), 0).then_inc(S["stacks_zero"], 2)
            dve.wait_ge(S["stacks_zero"], 8)
            for i in range(2):
                v.memset(kst[i][MAX_ROW:MAX_ROW + PARTS, :, :], 1.0).then_inc(S["stacks_ones"], 1)
            dve.wait_ge(S["c_exp_done"], 1)
            dve.wait_ge(S["c_loaded"], 32)
            v.tensor_scalar(c_exp[:, :], c_exp[:, :], 1.0, None, op0=ALU.add).then_inc(S["setup_dve"], 1)
            dve.wait_ge(S["setup_dve"], 1)
            v.reciprocal(c_exp[:, :], c_exp[:, :]).then_inc(S["setup_dve"], 1)
            dve.wait_ge(S["setup_dve"], 2)
            v.tensor_tensor(c_silu[:, :], c_in[:, :], c_exp[:, :], op=ALU.mult).then_inc(S["silu_done"], 1)
            dve.wait_ge(S["cT_ready"], 1)
            v.tensor_copy(c_T[:, :], m0_ps[:, 0:NB]).then_inc(S["cT_done"], 1)
            dve.wait_ge(S["modps_ready"], 1)
            flat = mod_n[:, :, :].rearrange("b s d -> b (s d)")
            v.tensor_copy(flat[:, 0:BANK], m0_ps[0:NB, :]).then_inc(S["modn_done"], 1)
            v.tensor_copy(flat[:, BANK:6 * D], m1_ps[0:NB, 0:6 * D - BANK]).then_inc(S["modn_done"], 1)
            dve.wait_ge(S["modT_ready"], 1)
            v.tensor_copy(modT[:, :, :].rearrange("p s b -> p (s b)"), pv_ps[:, 0:6 * NB])\
                .then_inc(S["modT_done"], 1)
            dve.wait_ge(S["modT_done"], 1)
            v.tensor_scalar(modT[:, 1, :], modT[:, 1, :], 1.0, None, op0=ALU.add).then_inc(S["modT_done"], 1)
            v.memset(pv_ps[:, :], 0.0).then_inc(S["pv_zero"], 1)
            dve.wait_ge(S["modn_done"], 2)
            n0 = 2
            for src, dst in ((2, 0), (5, 3)):
                v.tensor_scalar(mod_t0[:, :], mod_n[:, src, :], 0.0, 2.0, op0=ALU.is_ge, op1=ALU.mult)\
                    .then_inc(S["setup_dve"], 1)
                v.scalar_tensor_tensor(out=mod_t1[:, :], in0=mod_n[:, src, :], scalar=-1.0, in1=mod_n[:, src, :],
                                       op0=ALU.mult, op1=ALU.max).then_inc(S["setup_dve"], 1)
                n0 += 2
                dve.wait_ge(S["setup_dve"], n0)
                v.tensor_scalar(mod_t1[:, :], mod_t1[:, :], 0.25, None, op0=ALU.max).then_inc(S["setup_dve"], 1)
                n0 += 1
                dve.wait_ge(S["setup_dve"], n0)
                v.scalar_tensor_tensor(out=mod_out[:, dst, :], in0=mod_t0[:, :], scalar=-1.0, in1=mod_t1[:, :],
                                       op0=ALU.add, op1=ALU.mult).then_inc(S["setup_dve"], 1)
                n0 += 1
                dve.wait_ge(S["setup_dve"], n0)
            v.tensor_scalar(mod_out[:, 1, :], mod_n[:, 4, :], 1.0, None, op0=ALU.add).then_inc(S["setup_dve"], 1)
            v.tensor_copy(mod_out[:, 2, :], mod_n[:, 3, :]).then_inc(S["setup_dve"], 1)
            dve.wait_ge(S["setup_dve"], n0 + 2)
            v.tensor_copy(mod_t0[:, :], mod_out[:, 2, :]).then_inc(S["modout_done"], 1)
            dve.wait_ge(S["bias_loaded"], 32)
            v.tensor_copy(bias_parts[:, 0, :], bias_in[:, :]).then_inc(S["bias_step"], 1)
            dve.wait_ge(S["bias_step"], 1)
            v.tensor_tensor(bias_r[:, :], bias_in[:, :], bias_parts[:, 0, :], op=ALU.subtract)\
                .then_inc(S["bias_step"], 1)
            dve.wait_ge(S["bias_step"], 2)
            v.tensor_copy(bias_parts[:, 1, :], bias_r[:, :]).then_inc(S["bias_step"], 1)
            dve.wait_ge(S["bias_step"], 3)
            v.tensor_tensor(bias_parts[:, 2, :], bias_r[:, :], bias_parts[:, 1, :], op=ALU.subtract)\
                .then_inc(S["bias_step"], 2)
            dve.wait_ge(S["const_done"], 16)
            dve.wait_ge(S["w_loaded"], 64)

            def layer_stats(src, stats, mv, stat, mvd, b):
                for t in range(NT):
                    v.bn_stats(stats[:, t, :], src(t)).then_inc(S[stat], 1)
                after(dve, stat, NT, b, NT)
                stand(dve)
                for t in range(NT):
                    v.bn_aggr(mv[:, t, :], stats[:, t, :]).then_inc(S[mvd], 1)

            def normalise(dst, src, mv, r, name):
                for t in range(NT):
                    v.tensor_scalar(dst[:, t, :], src(t), mv[:, t, 0:1], r[:, t:t + 1],
                                    op0=ALU.subtract, op1=ALU.mult).then_inc(S[name], 1)

            def divide(b, gr):
                after(dve, "pvT_ready", NG, b, gr + 1)
                m = m1_ps[:, :].rearrange("p (t h d) -> p t h d", t=NT, h=4)
                v.reciprocal(rsum[:, :, :], m[:, :, :, DH]).then_inc(S["rsum_done"], 1)
                after(dve, "rsum_done", NG, b, gr + 1)
                if gr == 0:
                    after(dve, "aT_ready", 1, b - 1, 1)
                v.tensor_tensor(attn[:, :, 4 * gr:4 * gr + 4, :], m[:, :, :, 0:DH],
                                rsum[:, :, :].unsqueeze(3).to_broadcast([P, NT, 4, DH]), op=ALU.mult)\
                    .then_inc(S["pvn_done"], 1)

            def row_maxima(b):
                after(dve, "sn_read", SLOTS, b, SLOTS)
                after(dve, "maxT_ready", 1, b - 1, 1)
                by_head = rmax[:, :, :].rearrange("p t (a x) -> p t a x", x=2)
                v.tensor_reduce(by_head[:, 3, :, :], bmax[:, :, 0:4:2, :], axis=AX_X, op=ALU.max)\
                    .then_inc(S["rmax_done"], 1)
                v.tensor_reduce(by_head[:, 2, :, :], bmax[:, :, 1:5:2, 1:4], axis=AX_X, op=ALU.max)\
                    .then_inc(S["rmax_done"], 1)
                v.tensor_reduce(by_head[:, 1, :, :], bmax[:, :, 4, :].rearrange("p a (x k) -> p a x k", x=2),
                                axis=AX_X, op=ALU.max).then_inc(S["rmax_done"], 1)
                v.tensor_copy(by_head[:, 0, :, :], bmax[:, :, 1:5:2, 0]).then_inc(S["rmax_done"], 1)
                after(dve, "rmax_done", 4, b, 4)
                v.tensor_scalar(neg_parts[:, :, 0, :], rmax[:, :, :], -1.0, None, op0=ALU.mult)\
                    .then_inc(S["neg_hi"], 1)
                after(dve, "neg_hi", 1, b, 1)
                v.scalar_tensor_tensor(out=neg_r[:, :, :], in0=rmax[:, :, :], scalar=-1.0, in1=neg_parts[:, :, 0, :],
                                       op0=ALU.mult, op1=ALU.subtract).then_inc(S["neg_rest"], 1)
                after(dve, "neg_rest", 1, b, 1)
                v.tensor_copy(neg_parts[:, :, 1, :], neg_r[:, :, :]).then_inc(S["neg_mid"], 1)
                after(dve, "neg_mid", 1, b, 1)
                v.tensor_tensor(neg_parts[:, :, 2, :], neg_r[:, :, :], neg_parts[:, :, 1, :], op=ALU.subtract)\
                    .then_inc(S["neg_done"], 1)

            def choose(b):
                after(dve, "lg_ready", 1, b, 1)
                m = m0_ps[:, 0:P].rearrange("p (t e) -> p t e", t=NT)[:, :, 0:E]
                v.tensor_tensor(logit[:, :, :], m, gate_bias[:, :].unsqueeze(1).to_broadcast([P, NT, E]), op=ALU.add)\
                    .then_inc(S["lg_read"], 1)
                after(dve, "lg_read", 1, b, 1)
                v.tensor_reduce(lmax[:, :], logit[:, :, :], axis=AX_X, op=ALU.max).then_inc(S["lmax_done"], 1)
                after(dve, "lmax_done", 1, b, 1)
                v.tensor_tensor(first[:, :, :], logit[:, :, :], lmax[:, :].unsqueeze(2).to_broadcast([P, NT, E]),
                                op=ALU.is_ge).then_inc(S["first_done"], 1)
                after(dve, "first_done", 2, b, 1)
                v.tensor_tensor(first[:, :, :], first[:, :, :], rank_of_e[:, :].unsqueeze(1).to_broadcast([P, NT, E]),
                                op=ALU.mult).then_inc(S["first_done"], 1)
                after(dve, "first_done", 2, b, 2)
                v.tensor_reduce(fmax[:, :], first[:, :, :], axis=AX_X, op=ALU.max).then_inc(S["fmax_done"], 1)
                after(dve, "fmax_done", 1, b, 1)
                after(dve, "rank_ready", 1, b - 1, 1)
                v.tensor_tensor(onehot[:, :, :], rank_of_e[:, :].unsqueeze(1).to_broadcast([P, NT, E]),
                                fmax[:, :].unsqueeze(2).to_broadcast([P, NT, E]), op=ALU.is_equal)\
                    .then_inc(S["onehot_done"], 1)

            def place(b, par):
                after(dve, "rank_ready", 1, b, 1)
                m = m0_ps[:, 0:(NT + 1) * E].rearrange("p (t e) -> p t e", t=NT + 1)
                after(dve, "base_done", 1, b - 1, 1)
                v.tensor_tensor(posm[:, :, :], m[:, 0:NT, :], base[:, :].unsqueeze(1).to_broadcast([P, NT, E]),
                                op=ALU.add).then_inc(S["posm_done"], 1)
                after(dve, "posm_done", 1, b, 1)
                v.tensor_tensor(base[:, :], m[:, NT, :], base[:, :], op=ALU.add).then_inc(S["base_done"], 1)
                v.tensor_tensor(posm[:, :, :], posm[:, :, :], onehot[:, :, :], op=ALU.mult).then_inc(S["posm_sel"], 1)
                after(dve, "posm_sel", 1, b, 1)
                v.tensor_reduce(pos[:, :], posm[:, :, :], axis=AX_X, op=ALU.add).then_inc(S["pos_done"], 1)
                after(dve, "pos_done", 1, b, 1)
                after_scatter(dve, b - 2, par)
                v.tensor_copy(pos_u[:, par, :], pos[:, :]).then_inc(S["pos_u_done"], 1)

            def step(s, p, qkv, mx, soft, close):
                b = s - 3
                xs = lambda t: xin[:, p, t, :]
                x1s = lambda t: pack[1 - p][:, t, D:2 * D]
                for q in range(SLOTS):
                    if qkv and q == 0:
                        after(dve, "x_loaded", 16, s, 16)
                        after(dve, "rstd1_add", 1, s - 1, 1)
                        layer_stats(xs, stats1, mv1, "ln1_stat", "ln1_mv", s)
                    if qkv and q == 2:
                        after(dve, "rstd1_done", 1, s, 1)
                        after(dve, "xT_ready", 1, s - 1, 1)
                        normalise(xhat, xs, mv1, rstd1, "xhat_done")
                    for i, at in ((0, PE_Q + 4), (1, PE_K + 3)):
                        if qkv and q == at:
                            after(dve, "r1_done", 2, s, i + 1)
                            v.tensor_copy(qk_parts[:, i, 1, :], qk_r[:, i, :]).then_inc(S["qm_done"], 1)
                    if close and q == 2:
                        divide(b, 2)
                    if close and q == 12:
                        divide(b, 3)
                    if soft and q == 22:
                        divide(s - 2, 0)
                    if soft and q == 32:
                        divide(s - 2, 1)
                    if close and q == PE_PROJ + 1:
                        after(dve, "proj_ready", 1, b, 1)
                        after(dve, "res_loaded", 48, b, 48)
                        after_scatter(dve, b - 2, 1 - p)
                        v.tensor_tensor(pack[1 - p][:, :, D:2 * D], m0_ps[:, :].rearrange("p (t d) -> p t d", t=NT),
                                        xres[:, 1 - p, :, :], op=ALU.add).then_inc(S["x1_done"], 1)
                        after(dve, "x1_done", 1, b, 1)
                        after(dve, "rstd2_add", 1, b - 1, 1)
                        layer_stats(x1s, stats2, mv2, "ln2_stat", "ln2_mv", b)
                    if close and q == PE_PROJ + 4:
                        after(dve, "rstd2_done", 1, b, 1)
                        after(dve, "h2m_done", 1, b - 1, 1)
                        normalise(xhat2, x1s, mv2, rstd2, "xhat2_done")
                    if mx:
                        for u in sn_units_at(q):
                            after(dve, "sn_ready", SLOTS, s - 1, u + 1)
                            v.tensor_reduce(bmax[:, u // 5, u % 5, :],
                                            sn_ps[:, u % 3, :].rearrange("p (k n) -> p k n", k=4),
                                            axis=AX_X, op=ALU.max).then_inc(S["sn_read"], 1)
                    if mx and q == 32:
                        row_maxima(s - 1)
                    if close and q == PE_LOGIT_T + 1:
                        choose(b)
                    if close and q == PE_RANK + 1:
                        place(b, 1 - p)

            steps(dve, step)

            dve.wait_ge(S["base_done"], NB)
            dve.wait_ge(S["const_done"], 16)
            n = [0]

            def link(ins):
                n[0] += 1
                ins.then_inc(S["tab_step"], 1)
                dve.wait_ge(S["tab_step"], n[0])

            link(v.tensor_copy(base_i[:, :], base[0:1, :]))
            link(v.tensor_tensor(cnt[:, :], base[0:1, :], e_cap[:, :], op=ALU.subtract))
            link(v.tensor_tensor(nt_cmp[:, :, :], cnt[:, :].unsqueeze(2).to_broadcast([1, E, N // P]),
                                 m_128[:, :].unsqueeze(1).to_broadcast([1, E, N // P]), op=ALU.is_gt))
            link(v.tensor_reduce(nt_e[:, :], nt_cmp[:, :, :], axis=AX_X, op=ALU.add))
            link(v.tensor_tensor(nt_m[:, :, :], low_e[:, :, :], nt_e[:, :].unsqueeze(1).to_broadcast([1, E, E]),
                                 op=ALU.mult))
            link(v.tensor_reduce(nt_end[:, :], nt_m[:, :, :], axis=AX_X, op=ALU.add))
            link(v.tensor_tensor(t_ge[:, :, :], t_iota[:, :].unsqueeze(2).to_broadcast([1, TILES, E]),
                                 nt_end[:, :].unsqueeze(1).to_broadcast([1, TILES, E]), op=ALU.is_ge))
            link(v.tensor_tensor(t_gn[:, :, :], t_ge[:, :, :], nt_e[:, :].unsqueeze(1).to_broadcast([1, TILES, E]),
                                 op=ALU.mult))
            link(v.tensor_reduce(t_e[:, :], t_ge[:, :, :], axis=AX_X, op=ALU.add))
            link(v.tensor_reduce(t_b[:, :], t_gn[:, :, :], axis=AX_X, op=ALU.add))
            link(v.tensor_tensor(t_row[:, :], t_iota[:, :], t_b[:, :], op=ALU.subtract))
            link(v.tensor_scalar(t_row[:, :], t_row[:, :], float(P), None, op0=ALU.mult))
            link(v.scalar_tensor_tensor(out=t_row1[:, :], in0=t_e[:, :], scalar=float(CAP), in1=t_row[:, :],
                                        op0=ALU.mult, op1=ALU.add))
            link(v.tensor_scalar(t_row_i[:, :], t_row1[:, :], float(SPARE), None, op0=ALU.min))
            link(v.tensor_scalar(t_e_i[:, :], t_e[:, :], float(E - 1), None, op0=ALU.min))
            v.tensor_copy(t_b[:, :], t_e[:, :]).then_inc(S["tab_done"], 1)

            def tile_in(k, r):
                dve.wait_ge(S["tB_ready"], k + 1)
                if not (isinstance(k, int) and k < 2):
                    after(dve, "hB_ready", 1, k, -1)
                v.tensor_copy(h2T_b[r], hT_ps[r][:, 0:P]).then_inc(S["tB_copied"], 1)

            def tile_out(k, r4):
                r = r4 % 2
                dve.wait_ge(S["gT_ready"], k + 1)
                if not (isinstance(k, int) and k < 2):
                    after(dve, "yB_ready", 1, k, -1)
                v.tensor_copy(hgT[r], gT_ps[:, r, :]).then_inc(S["gT_copied"], 1)

            def tile_close(k, r4, nn):
                r = r4 % 2
                dve.wait_ge(S["yB_ready"], k + 1)
                after(dve, row_loaded[r4], 16, nn, 16)
                v.tensor_tensor(ygb[r], y_ps[r][:, 0:D], rows[r4][:, 2 * D:3 * D], op=ALU.mult)\
                    .then_inc(S["ygb_done"], 1)
                dve.wait_ge(S["ygb_done"], k + 1)
                if not (isinstance(nn, int) and nn == 0):
                    after(dve, out_stored[r4], 16, nn - 1, 16)
                v.tensor_tensor(y_b[r4], ygb[r], rows[r4][:, D:2 * D], op=ALU.add).then_inc(S["y_done"], 1)

            tile_in(0, 0)
            for k in range(3):
                tile_in(k + 1, (k + 1) % 2)
                tile_out(k, k)
                if k >= 1:
                    tile_close(k - 1, k - 1, 0)
            with dve.Fori(1, TILES // RING) as nn:
                for r in range(RING):
                    k = RING * nn + r
                    tile_in(k, r % 2)
                    tile_out(k - 1, (r - 1) % RING)
                    tile_close(k - 2, (r - 2) % RING, nn if r >= 2 else nn - 1)
            tile_out(TILES - 1, RING - 1)
            for k in (TILES - 2, TILES - 1):
                tile_close(k, k % RING, TILES // RING - 1)


_INS = ["L0_attn_x", "L0_attn_Wqkv", "L0_attn_Wproj", "L0_ffn_gate_W", "L0_ffn_gate_b", "L0_ffn_W1", "L0_ffn_b1",
        "L0_ffn_W2", "L0_ffn_b2", "L0_c", "L0_wmod"]


def kernel(**inputs):
    import numpy as _np
    import concourse.bacc as _bacc
    from concourse import mybir as _mybir
    from concourse.bass_utils import run_bass_kernel_spmd as _run

    nc = _bacc.Bacc("TRN2", target_bir_lowering=False, num_devices=1)
    arrays, args = {}, []
    for name in _INS:
        a = _np.ascontiguousarray(inputs[name])
        arrays[f"in_{name}_dram"] = a
        args.append(nc.dram_tensor(f"in_{name}_dram", a.shape, _mybir.dt.from_np(a.dtype), kind="ExternalInput").ap())
    shape = inputs["L0_attn_x"].shape
    args.append(nc.dram_tensor("out_0_dram", shape, F32, kind="ExternalOutput").ap())
    block_kernel(nc, *args)
    r = _run(nc, [arrays], core_ids=[0])
    return r.results[0]["out_0_dram"]
```

```python
from contextlib import ExitStack

import concourse.bass as bass
from concourse import mybir

ALU = mybir.AluOpType
ACT = mybir.ActivationFunctionType
F32 = mybir.dt.float32
BF16 = mybir.dt.bfloat16
I32 = mybir.dt.int32
U32 = mybir.dt.uint32
AX_X = mybir.AxisListType.X

P = 128
PARTS = 3
MAX_ROW = 96
NEG = -1e30
BANK = 512
EPS = 1e-5

SLOTS = 40
GROUP_SLOTS = 10
PE_XT, PE_Q, PE_K, PE_V = 8, 11, 16, 17
PE_AT, PE_PROJ, PE_H2T, PE_LOGIT, PE_LOGIT_T, PE_RANK = 14, 19, 31, 33, 35, 38
PE_MAX_T = (29, 6)
PV_SLOTS = (4, 6, 8, 9)


def block_kernel(nc, x, Wqkv, Wproj, gate_W, gate_b, W1, b1, W2, b2, c, wmod, out):
    NB, T, D = x.shape
    E = gate_W.shape[1]
    DFF = W1.shape[2]
    H = 16
    DH = D // H
    NT = T // P
    NG = H // 4
    N = NB * T
    SCALE = float(DH) ** -0.5
    ROWS = PARTS * PARTS * DH
    CAP = N + P
    SPARE = E * CAP
    RW = 388
    IDX = 3 * D
    TILES = N // P + E
    FC = DFF // P
    RING = 8
    NO_TOKEN = float(2 * N)
    assert T == BANK and D == P and NT == 4 and NG == 4 and NB % 2 == 0 and NB >= 6 and TILES % RING == 0

    parts_d = nc.dram_tensor("parts_d", [2, PARTS, DH, H, T], BF16).ap()
    mod_d = nc.dram_tensor("mod_d", [NB, 4, D], F32).ap()
    rows_d = nc.dram_tensor("rows_d", [E * CAP + P, RW], F32).ap()
    b1_d = nc.dram_tensor("b1_d", [PARTS, E * DFF], BF16).ap()
    b2_d = nc.dram_tensor("b2_d", [PARTS, E * D], BF16).ap()

    ctx = ExitStack()
    with ctx:
        def sb(name, shape, dt=F32):
            return ctx.enter_context(nc.sbuf_tensor(name, shape, dt))

        def psum(name, shape, dt=F32):
            return ctx.enter_context(nc.psum_tensor(name, shape, dt))

        def sem(name):
            return ctx.enter_context(nc.semaphore(name))

        sn_ps = psum("sn_ps", [P, 3, BANK])
        st_ps = psum("st_ps", [P, 2, BANK])
        pv_ps = psum("pv_ps", [P, BANK])
        m0_ps = psum("m0_ps", [P, BANK])
        m1_ps = psum("m1_ps", [P, BANK])

        ident = sb("ident", [P, P])
        ident_b = sb("ident_b", [P, P], BF16)
        causal = sb("causal", [P, P], BF16)
        before = sb("before", [P, P], BF16)
        ones_b = sb("ones_b", [P, P], BF16)
        wqkv = sb("wqkv", [P, 3 * D])
        wproj = sb("wproj", [P, D])
        gate_w = sb("gate_w", [P, 32])
        gate_bias = sb("gate_bias", [P, E])
        rank_of_e = sb("rank_of_e", [P, E])
        w1 = sb("w1", [P, E * DFF])
        ones3 = sb("ones3", [PARTS, P], BF16)
        eps = sb("eps", [P, NT])
        half = sb("half", [P, NT])
        modT = sb("modT", [P, 6, NB])
        c_in = sb("c_in", [NB, D])
        c_exp = sb("c_exp", [NB, D])
        c_silu = sb("c_silu", [NB, D])
        c_T = sb("c_T", [P, NB])
        wmod_sb = sb("wmod_sb", [P, 6 * D])
        mod_n = sb("mod_n", [NB, 6, D])
        mod_out = sb("mod_out", [NB, 4, D])
        mod_t0 = sb("mod_t0", [NB, D])
        mod_t1 = sb("mod_t1", [NB, D])
        NBIAS = (E * DFF + E * D) // P
        bias_in = sb("bias_in", [P, NBIAS])
        bias_r = sb("bias_r", [P, NBIAS])
        bias_parts = sb("bias_parts", [P, PARTS, NBIAS], BF16)
        xin = sb("xin", [P, 2, NT, D])
        stats1 = sb("stats1", [P, NT, 6])
        mv1 = sb("mv1", [P, NT, 2])
        var1 = sb("var1", [P, NT])
        rstd1 = sb("rstd1", [P, NT])
        xhat = sb("xhat", [P, NT, D])
        hT = sb("hT", [P, 2, T])
        qk_f = sb("qk_f", [P, 2, T])
        qk_r = sb("qk_r", [P, 2, T])
        qk_parts = sb("qk_parts", [P, 2, PARTS, T], BF16)
        qst = [sb(f"qst{i}", [P, H, T], BF16) for i in range(2)]
        kst = [sb(f"kst{i}", [P, H, T], BF16) for i in range(2)]
        vaug = [sb(f"vaug{i}", [P, NT, H, DH + 1]) for i in range(2)]
        bmax = sb("bmax", [P, H // 2, 5, 4])
        rmax = sb("rmax", [P, NT, H])
        HH = H // 2
        neg_r = sb("neg_r", [P, 2, NT, HH])
        neg_parts = sb("neg_parts", [P, 2, NT, PARTS, HH], BF16)
        neg_T = sb("neg_T", [PARTS * HH, T], BF16)
        probs = [sb(f"probs{i}", [P, 10, T]) for i in range(2)]
        pvs = sb("pvs", [P, 2, T])
        rsum = sb("rsum", [P, NT, 4])
        attn = sb("attn", [P, NT, H, DH])
        attnT = sb("attnT", [P, T])
        wpg = sb("wpg", [P, D])
        xres = sb("xres", [P, 2, NT, D])
        modb = sb("modb", [P, 2, 3, D])
        pack = [sb(f"pack{i}", [P, NT, RW]) for i in range(2)]
        stats2 = sb("stats2", [P, NT, 6])
        mv2 = sb("mv2", [P, NT, 2])
        var2 = sb("var2", [P, NT])
        rstd2 = sb("rstd2", [P, NT])
        xhat2 = sb("xhat2", [P, NT, D])
        h2m = sb("h2m", [P, NT, D])
        h2T = sb("h2T", [P, T])
        logitT = sb("logitT", [P, P])
        logit = sb("logit", [P, NT, E])
        lmax = sb("lmax", [P, NT])
        first = sb("first", [P, NT, E])
        fmax = sb("fmax", [P, NT])
        onehot = sb("onehot", [P, NT, E], BF16)
        posm = sb("posm", [P, NT, E])
        pos = sb("pos", [P, NT])
        pos_u = sb("pos_u", [P, 2, NT], U32)
        base = sb("base", [P, E])
        e_cap = sb("e_cap", [1, E])
        m_128 = sb("m_128", [1, N // P])
        t_iota = sb("t_iota", [1, TILES])
        low_e = sb("low_e", [1, E, E])
        cnt = sb("cnt", [1, E])
        nt_cmp = qk_r[0:1, 0, :].rearrange("p (e n) -> p e n", e=E)[:, :, 0:N // P]
        nt_e = sb("nt_e", [1, E])
        nt_m = sb("nt_m", [1, E, E])
        nt_end = sb("nt_end", [1, E])
        t_ge = hT[0:1, :, :].rearrange("p a t -> p (a t)")[:, 0:TILES * E].rearrange("p (k e) -> p k e", e=E)
        t_gn = qk_f[0:1, :, :].rearrange("p a t -> p (a t)")[:, 0:TILES * E].rearrange("p (k e) -> p k e", e=E)
        t_e = sb("t_e", [1, TILES])
        t_b = sb("t_b", [1, TILES])
        t_row = sb("t_row", [1, TILES])
        t_row1 = sb("t_row1", [1, TILES])
        t_row_i = sb("t_row_i", [1, TILES], I32)
        t_e_i = sb("t_e_i", [1, TILES], I32)
        base_i = sb("base_i", [1, E], I32)
        pad = sb("pad", [P, RW])

        stack_f = qst[0][:, :, :].rearrange("p h t -> p (h t)").bitcast(F32)
        stack_g = qst[1][:, :, :].rearrange("p h t -> p (h t)").bitcast(F32)
        rows = [stack_f[:, i * RW:(i + 1) * RW] for i in range(RING)]
        h2T_b = [stack_f[:, 3200 + i * P:3200 + (i + 1) * P] for i in range(2)]
        ygb = [stack_f[:, 3584 + i * D:3584 + (i + 1) * D] for i in range(2)]
        hg = [stack_g[:, i * DFF:(i + 1) * DFF] for i in range(2)]
        hgT = [stack_g[:, 1024 + i * DFF:1024 + (i + 1) * DFF] for i in range(2)]
        y_b = [stack_g[:, 2048 + i * D:2048 + (i + 1) * D] for i in range(RING)]
        idx_u = sb("idx_u", [P, RING], U32)
        h_ps, gT_ps = sn_ps, st_ps
        y_ps = [sn_ps[:, 2, :], pv_ps[:, :]]
        hT_ps = [m0_ps, m1_ps]
        w2 = kst[0][:, :, :].rearrange("p h t -> p (h t)").bitcast(F32)[:, 0:E * FC * D]
        bias_rows = kst[1][:, :, :].rearrange("p h t -> p (h t)")
        b1p = bias_rows[0:PARTS, 0:E * DFF]
        b2p = bias_rows[0:PARTS, E * DFF:E * (DFF + D)]

        names = """passed const_done ident_done gate_w_zero w_loaded c_loaded c_exp_done silu_done cT_ready cT_done
            modps_ready modn_done modT_ready modT_done modout_done mod_stored bias_loaded bias_step
            bias_stored bias_rows_loaded stacks_zero stacks_ones vaug_ones pv_zero setup_dve
            pad_done wffn_loaded""".split()
        names += """x_loaded ln1_stat ln1_mv rstd1_add rstd1_done xhat_done xT_ready hT_done qk_ready qk_copied
            r1_done qm_done ql_done v_ready v_copied""".split()
        names += """sn_ready sn_read rmax_done neg_hi neg_rest neg_mid neg_done maxT_ready neg_copied
            """.split()
        names += """st_ready exp_done masked pv_ready pv_copied pvT_ready rsum_done pvn_done""".split()
        names += """res_loaded wpg_done aT_ready aT_copied proj_ready x1_done ln2_stat ln2_mv rstd2_add rstd2_done
            xhat2_done h2m_done h2_done h2T_ready h2T_copied lgT_ready lgT_copied lg_ready lg_read lmax_done
            first_done fmax_done onehot_done rank_ready posm_done posm_sel pos_done base_done pos_u_done idx_moved
            """.split()
        names += """base_i_done tab_step tab_done pads_stored tB_ready tB_copied hB_ready gelu_done gT_ready gT_copied yB_ready
            ygb_done y_done idx_done""".split()
        S = {n: sem(n) for n in names}
        parts_stored = [sem(f"parts_stored{i}") for i in range(2)]
        stack_loaded = [sem(f"stack_loaded{g}") for g in range(NG)]
        scattered = [sem(f"scattered{i}") for i in range(2)]
        max_loaded = [sem(f"max_loaded{i}") for i in range(2)]
        row_loaded = [sem(f"row_loaded{i}") for i in range(RING)]
        out_stored = [sem(f"out_stored{i}") for i in range(RING)]

        def after(eng, name, per, b, k):
            s = S[name] if isinstance(name, str) else name
            v = per * b + k
            if isinstance(v, int) and v <= 0:
                return
            eng.wait_ge(s, v)

        def stand(eng):
            eng.sem_inc(S["passed"], 1)

        def after_scatter(eng, b, par):
            after(eng, scattered[par], 32, b - par, 64)

        STACK_DMAS = 4
        block = ctx.enter_context(nc.Block())

        def steps(eng, step):
            for s in range(4):
                step(s, s % 2, s < NB, 1 <= s <= NB, s >= 2, s >= 3)
            with eng.Fori(2, NB // 2) as i:
                step(2 * i, 0, True, True, True, True)
                step(2 * i + 1, 1, True, True, True, True)
            for s in range(NB, NB + 3):
                step(s, s % 2, False, s <= NB, s <= NB + 1, True)

        @block.sync
        def _(sp):
            sp.dma_start(c_in[:, :], c).then_inc(S["c_loaded"], 16)
            sp.dma_start(wmod_sb[:, :], wmod).then_inc(S["c_loaded"], 16)
            sp.dma_start(xin[:, 0, :, :], x[0].rearrange("(t p) d -> p t d", p=P)).then_inc(S["x_loaded"], 16)
            sp.wait_ge(S["gate_w_zero"], 1)
            sp.dma_start(gate_w[:, 0:E], gate_W).then_inc(S["w_loaded"], 16)
            sp.dma_start(wqkv[:, :], Wqkv).then_inc(S["w_loaded"], 16)
            sp.dma_start(wproj[:, :], Wproj).then_inc(S["w_loaded"], 16)
            sp.dma_start(gate_bias[:, :], gate_b.partition_broadcast(P)).then_inc(S["w_loaded"], 16)
            nb1 = E * DFF // P
            sp.dma_start(bias_in[:, 0:nb1], b1.rearrange("e (a n) -> (e a) n", n=nb1)).then_inc(S["bias_loaded"], 16)
            sp.dma_start(bias_in[:, nb1:NBIAS], b2.rearrange("e (a n) -> (e a) n", n=E * D // P))\
                .then_inc(S["bias_loaded"], 16)
            sp.wait_ge(S["bias_step"], 5)
            sp.dma_start(b1_d.rearrange("i (p n) -> p i n", p=P), bias_parts[:, :, 0:nb1])\
                .then_inc(S["bias_stored"], 16)
            sp.dma_start(b2_d.rearrange("i (p n) -> p i n", p=P), bias_parts[:, :, nb1:NBIAS])\
                .then_inc(S["bias_stored"], 16)
            sp.wait_ge(S["modout_done"], 1)
            sp.dma_start(mod_d, mod_out[:, :, :]).then_inc(S["mod_stored"], 16)
            sp.wait_ge(S["mod_stored"], 16)

            def step(s, p, qkv, mx, soft, close):
                b = s
                if not isinstance(s, int) or s + 1 < NB:
                    after(sp, "xhat_done", NT, b - 1, NT)
                    nxt = s + 1 if isinstance(s, int) or p == 0 else (s + 1) % NB
                    after(sp, "x_loaded", 16, b, 16)
                    sp.dma_start(xin[:, 1 - p, :, :], xt_d(nxt)).then_inc(S["x_loaded"], 16)
                if soft:
                    load_max(s - 2, p, 1)
                if qkv:
                    for i in range(2):
                        for g in range(NG):
                            after(sp, stack_loaded[g], 16 * STACK_DMAS, b - 1, 16 * STACK_DMAS) if i == 0 else None
                        after(sp, "ql_done", 2, b, i + 1)
                        for j in range(PARTS):
                            sp.dma_start(parts_d[i, j].rearrange("d h n -> h d n"), qk_parts[:, i, j, :])\
                                .then_inc(parts_stored[i], 16)
                    for i in range(2):
                        after(sp, parts_stored[i], 16 * PARTS, b, 16 * PARTS)
                    if isinstance(s, int) and s == 0:
                        sp.wait_ge(S["stacks_zero"], 8)
                for g in range(NG):
                    if g == NG - 1 and mx:
                            load_max(s - 1, 1 - p, 0)
                    if qkv:
                        after(sp, "st_ready", SLOTS, b - 2, GROUP_SLOTS * (g + 1))
                        q_d = parts_d[0].rearrange("i d h n -> (i d) (h n)")[:, 4 * g * T:4 * (g + 1) * T]
                        k_d = parts_d[1].rearrange("i d h n -> i d (h n)")[:, :, 4 * g * T:4 * (g + 1) * T]
                        rows_q = PARTS * DH
                        sp.dma_start(qst[p][0:ROWS, 4 * g:4 * g + 4, :],
                                     q_d.unsqueeze(0).to_broadcast([PARTS, rows_q, 4 * T]))\
                            .then_inc(stack_loaded[g], 16)
                        for j in range(PARTS):
                            sp.dma_start(kst[p][j * rows_q:(j + 1) * rows_q, 4 * g:4 * g + 4, :],
                                         k_d[j].unsqueeze(0).to_broadcast([PARTS, DH, 4 * T]))\
                                .then_inc(stack_loaded[g], 16)
                if soft and (not isinstance(s, int) or s - 2 < NB):
                    cb = s - 2
                    after(sp, "res_loaded", 48, cb - 1, 48)
                    after(sp, "x1_done", 1, cb - 2, 1)
                    sp.dma_start(xres[:, p, :, :], xt_d(cb)).then_inc(S["res_loaded"], 16)
                    after(sp, "h2_done", 1, cb - 2, 1)
                    after(sp, "wpg_done", 1, cb - 2, 1)
                    sp.dma_start(modb[:, p, :, :], mod_row(cb)[0:3, :].partition_broadcast(P))\
                        .then_inc(S["res_loaded"], 16)
                    after_scatter(sp, cb - 2, p)
                    sp.dma_start(pack[p][:, :, 2 * D:3 * D],
                                 mod_row(cb)[3, :].partition_broadcast(P).unsqueeze(1).to_broadcast([P, NT, D]))\
                        .then_inc(S["res_loaded"], 16)

            def load_max(b, par, half):
                after(sp, "neg_copied", 2, b, half + 1)
                sp.dma_start(qst[par][MAX_ROW:MAX_ROW + PARTS, HH * half:HH * (half + 1), :], neg_T[:, :])\
                    .then_inc(max_loaded[half], 16)

            def xt_d(b):
                return x[b].rearrange("(t p) d -> p t d", p=P)

            def mod_row(b):
                return mod_d[b]

            sp.dma_start(w1[:, :].rearrange("p (e f) -> p e f", e=E), W1.rearrange("e p f -> p e f"))\
                .then_inc(S["wffn_loaded"], 16)

            steps(sp, step)

            sp.wait_ge(S["st_ready"], SLOTS * (NB - 1))
            sp.dma_start(w2.rearrange("p (e c d) -> p e c d", e=E, c=FC),
                         W2.rearrange("e (c p) d -> p e c d", p=P)).then_inc(S["wffn_loaded"], 16)

            sp.wait_ge(S["st_ready"], SLOTS * NB)
            sp.wait_ge(S["bias_stored"], 32)
            sp.dma_start(b1p, b1_d).then_inc(S["bias_rows_loaded"], 16)
            sp.dma_start(b2p, b2_d).then_inc(S["bias_rows_loaded"], 16)

            sp.wait_ge(S["base_i_done"], 1)
            sp.wait_ge(S["pad_done"], 1)
            for e in range(E):
                row = sp.value_load(base_i[0:1, e:e + 1], min_val=0, max_val=SPARE - P)
                sp.dma_start(rows_d[bass.ds(row, P), :], pad[:, :]).then_inc(S["pads_stored"], 16)
            sp.dma_start(rows_d[SPARE:SPARE + P, :], pad[:, :]).then_inc(S["pads_stored"], 16)
            sp.wait_ge(S["tab_done"], 1)
            for i in range(2):
                after_scatter(sp, NB - 2 + i, i)
            sp.wait_ge(S["pads_stored"], 16 * (E + 1))

            def load(k, r):
                if not isinstance(k, int):
                    after(sp, "y_done", 1, k, 1 - RING)
                    after(sp, "idx_done", 1, k, 1 - RING)
                row = sp.value_load(t_row_i[0:1, bass.ds(k, 1)], min_val=0, max_val=SPARE)
                sp.dma_start(rows[r], rows_d[bass.ds(row, P), :]).then_inc(row_loaded[r], 16)

            for r in range(RING):
                load(r, r)
            with sp.Fori(1, TILES // RING) as n:
                for r in range(RING):
                    load(RING * n + r, r)

        @block.gpsimd
        def _(pool):
            g = nc.gpsimd

            for m in (ident, ident_b):
                g.memset(m[:, :], 0.0).then_inc(S["ident_done"], 1)
            g.memset(causal[:, :], 0.0).then_inc(S["ident_done"], 1)
            g.memset(before[:, :], 1.0).then_inc(S["ident_done"], 1)
            g.memset(gate_w[:, :], 0.0).then_inc(S["gate_w_zero"], 1)
            pool.wait_ge(S["ident_done"], 4)
            for m in (ident, ident_b):
                g.affine_select(out=m[:, :], in_=m[:, :], compare_op=ALU.not_equal, fill=1.0, base=0,
                                pattern=[[-1, P]], channel_multiplier=1).then_inc(S["const_done"], 1)
            g.affine_select(out=causal[:, :], in_=causal[:, :], compare_op=ALU.is_ge, fill=NEG, base=0,
                            pattern=[[-1, P]], channel_multiplier=1).then_inc(S["const_done"], 1)
            g.affine_select(out=before[:, :], in_=before[:, :], compare_op=ALU.is_gt, fill=0.0, base=0,
                            pattern=[[1, P]], channel_multiplier=-1).then_inc(S["const_done"], 1)
            g.memset(ones_b[:, :], 1.0).then_inc(S["const_done"], 1)
            g.memset(ones3[:, :], 1.0).then_inc(S["const_done"], 1)
            g.memset(eps[:, :], EPS).then_inc(S["const_done"], 1)
            g.memset(half[:, :], -0.5).then_inc(S["const_done"], 1)
            g.iota(rank_of_e[:, :], pattern=[[-1, E]], base=E, channel_multiplier=0,
                   allow_small_or_imprecise_dtypes=True).then_inc(S["const_done"], 1)
            g.iota(base[:, :], pattern=[[CAP, E]], base=0, channel_multiplier=0,
                   allow_small_or_imprecise_dtypes=True).then_inc(S["const_done"], 1)
            g.iota(e_cap[:, :], pattern=[[CAP, E]], base=0, channel_multiplier=0,
                   allow_small_or_imprecise_dtypes=True).then_inc(S["const_done"], 1)
            g.iota(m_128[:, :], pattern=[[P, N // P]], base=0, channel_multiplier=0,
                   allow_small_or_imprecise_dtypes=True).then_inc(S["const_done"], 1)
            g.iota(t_iota[:, :], pattern=[[1, TILES]], base=0, channel_multiplier=0,
                   allow_small_or_imprecise_dtypes=True).then_inc(S["const_done"], 1)
            g.memset(low_e[:, :, :], 1.0).then_inc(S["ident_done"], 1)
            pool.wait_ge(S["ident_done"], 5)
            g.affine_select(out=low_e[:, :, :], in_=low_e[:, :, :], compare_op=ALU.is_ge, fill=0.0, base=0,
                            pattern=[[1, E], [-1, E]], channel_multiplier=0).then_inc(S["const_done"], 1)
            for i in range(2):
                g.memset(pack[i][:, :, IDX:RW], 0.0).then_inc(S["ident_done"], 1)
                pool.wait_ge(S["ident_done"], 6 + i)
                g.iota(pack[i][:, :, IDX:IDX + 1], pattern=[[P, NT], [0, 1]], base=(i - 2) * T, channel_multiplier=1,
                       allow_small_or_imprecise_dtypes=True).then_inc(S["const_done"], 1)
            g.memset(pad[:, :], 0.0).then_inc(S["ident_done"], 1)
            pool.wait_ge(S["ident_done"], 8)
            g.memset(pad[:, IDX:IDX + 1], NO_TOKEN).then_inc(S["pad_done"], 1)
            for i in range(2):
                g.memset(vaug[i][:, :, :, DH:DH + 1], 1.0).then_inc(S["vaug_ones"], 1)
            pool.wait_ge(S["const_done"], 16)

            def rstd(mv, var, r, add, done, b):
                g.tensor_tensor(var[:, :], mv[:, :, 1], eps[:, :], op=ALU.add).then_inc(S[add], 1)
                after(pool, add, 1, b, 1)
                g.tensor_tensor(r[:, :], var[:, :], half[:, :], op=ALU.pow).then_inc(S[done], 1)

            def split(b, i):
                after(pool, "qk_copied", 4, b, 2 * i + 2)
                g.tensor_tensor(qk_r[:, i, :], qk_f[:, i, :], qk_parts[:, i, 0, :], op=ALU.subtract)\
                    .then_inc(S["r1_done"], 1)

            def split_last(b, i):
                after(pool, "qm_done", 2, b, i + 1)
                g.tensor_tensor(qk_parts[:, i, 2, :], qk_r[:, i, :], qk_parts[:, i, 1, :], op=ALU.subtract)\
                    .then_inc(S["ql_done"], 1)

            def mask(b, pair):
                after(pool, "exp_done", SLOTS, b, 5 * (pair + 1))
                stand(pool)
                v = probs[pair // 2 % 2][:, 5 * (pair % 2):5 * (pair % 2) + 5, :]
                for blocks, n in ((v[:, 0:4:2, 0:P], (2, 1)),
                                  (v[:, 1:5:2, 0:2 * P].rearrange("p a (b n) -> p a b n", b=2), (2, 2)),
                                  (v[:, 4, :].rearrange("p (a n) -> p a n", a=2)[:, :, 0:P], (2, 1))):
                    pat = [[0, n[0]], [0, n[1]], [1, P]] if n[1] > 1 else [[0, n[0]], [1, P]]
                    last = g.affine_select(out=blocks, in_=blocks, compare_op=ALU.is_ge, fill=0.0, base=0,
                                           pattern=pat, channel_multiplier=-1)
                last.then_inc(S["masked"], 1)

            def step(s, p, qkv, mx, soft, close):
                for q in range(SLOTS):
                    if soft and q % 5 == 1 and q > 1:
                        mask(s - 2, q // 5 - 1)
                    if qkv and q == 2:
                        after(pool, "ln1_mv", NT, s, NT)
                        after(pool, "xhat_done", NT, s - 1, NT)
                        rstd(mv1, var1, rstd1, "rstd1_add", "rstd1_done", s)
                    if close and q == 3:
                        b = s - 3
                        after(pool, "res_loaded", 48, b, 48)
                        after(pool, "proj_ready", 1, b - 1, 1)
                        g.tensor_tensor(wpg[:, :], wproj[:, :], modb[:, 1 - p, 0, :], op=ALU.mult)\
                            .then_inc(S["wpg_done"], 1)
                        after_scatter(pool, b - 2, 1 - p)
                        stand(pool)
                        col = pack[1 - p][:, :, IDX:IDX + 1]
                        g.tensor_scalar(col, col, float(2 * T), None, op0=ALU.add).then_inc(S["idx_moved"], 1)
                    if qkv and q == PE_Q + 3:
                        split(s, 0)
                    if qkv and q == PE_Q + 5:
                        split_last(s, 0)
                    if qkv and q == PE_K + 3:
                        split(s, 1)
                    if qkv and q == PE_K + 5:
                        split_last(s, 1)
                    if close and q == PE_PROJ + 5:
                        after(pool, "ln2_mv", NT, s - 3, NT)
                        after(pool, "xhat2_done", NT, s - 4, NT)
                        rstd(mv2, var2, rstd2, "rstd2_add", "rstd2_done", s - 3)
                    if close and q == PE_PROJ + 8:
                        b = s - 3
                        mb = modb[:, 1 - p, :, :]
                        after(pool, "xhat2_done", NT, b, NT)
                        g.tensor_tensor(h2m[:, :, :], xhat2[:, :, :],
                                        mb[:, 1, :].unsqueeze(1).to_broadcast([P, NT, D]), op=ALU.mult)\
                            .then_inc(S["h2m_done"], 1)
                        after(pool, "h2m_done", 1, b, 1)
                        g.tensor_tensor(pack[1 - p][:, :, 0:D], h2m[:, :, :],
                                        mb[:, 2, :].unsqueeze(1).to_broadcast([P, NT, D]), op=ALU.add)\
                            .then_inc(S["h2_done"], 1)
                if soft:
                    mask(s - 2, 7)
                if close:
                    b = s - 3
                    after(pool, "pos_u_done", 1, b, 1)
                    after(pool, "x1_done", 1, b, 1)
                    after(pool, "h2_done", 1, b, 1)
                    after(pool, "idx_moved", 1, b, 1)
                    stand(pool)
                    for t in range(NT):
                        g.indirect_dma_start(
                            out=rows_d, out_offset=bass.IndirectOffsetOnAxis(ap=pos_u[:, 1 - p, t:t + 1], axis=0),
                            in_=pack[1 - p][:, t, :], in_offset=None, bounds_check=E * CAP - 1, oob_is_err=False)\
                            .then_inc(scattered[1 - p], 16)

            steps(pool, step)

            def store(k, r, n):
                after(pool, row_loaded[r], 16, n, 16)
                after(pool, out_stored[r], 16, n - 1, 16)
                stand(pool)
                g.tensor_copy(idx_u[:, r:r + 1], rows[r][:, IDX:IDX + 1]).then_inc(S["idx_done"], 1)
                pool.wait_ge(S["idx_done"], k + 1)
                pool.wait_ge(S["y_done"], k + 1)
                stand(pool)
                g.indirect_dma_start(
                    out=out.rearrange("b t d -> (b t) d"),
                    out_offset=bass.IndirectOffsetOnAxis(ap=idx_u[:, r:r + 1], axis=0),
                    in_=y_b[r], in_offset=None, bounds_check=N - 1, oob_is_err=False).then_inc(out_stored[r], 16)

            for r in range(RING):
                store(r, r, 0)
            with pool.Fori(1, TILES // RING) as n:
                for r in range(RING):
                    store(RING * n + r, r, n)
            for r in range(RING):
                pool.wait_ge(out_stored[r], 16 * (TILES // RING))

        @block.scalar
        def _(act):
            a = nc.scalar
            act.wait_ge(S["c_loaded"], 32)
            a.activation(c_exp[:, :], c_in[:, :], ACT.Exp, scale=-1.0).then_inc(S["c_exp_done"], 1)
            act.wait_ge(S["modT_done"], 2)

            def copy_out(dst, src, name):
                a.activation(dst, src, ACT.Copy).then_inc(S[name], 1)

            def exp(b, q):
                gr = q // GROUP_SLOTS
                if q % GROUP_SLOTS == 0:
                    after(act, "pv_ready", NG, b, gr - 1)
                after(act, "st_ready", SLOTS, b, q + 1)
                a.activation(probs[gr % 2][:, q % GROUP_SLOTS, :], st_ps[:, q % 2, :], ACT.Exp, scale=SCALE)\
                    .then_inc(S["exp_done"], 1)

            def pv_copy(b, gr):
                after(act, "pv_ready", NG, b, gr + 1)
                after(act, "pvT_ready", NG, b, gr - 1)
                copy_out(pvs[:, gr % 2, :], pv_ps[:, :], "pv_copied")

            def step(s, p, qkv, mx, soft, close):
                for q in range(SLOTS):
                    if close and q == 0:
                        pv_copy(s - 3, 2)
                    if close and q == 10:
                        pv_copy(s - 3, 3)
                    if soft and q == 20:
                        pv_copy(s - 2, 0)
                    if soft and q == 30:
                        pv_copy(s - 2, 1)
                    if qkv and q == PE_XT + 1:
                        after(act, "xT_ready", 1, s, 1)
                        after(act, "v_ready", 1, s - 2, 1)
                        a.activation(hT[:, p, :], m0_ps[:, :], ACT.Identity, bias=modT[:, 0, bass.ds(s, 1)],
                                     scale=modT[:, 1, bass.ds(s, 1)]).then_inc(S["hT_done"], 1)
                    for i, at in ((0, PE_Q + 1), (1, PE_K + 1)):
                        if qkv and q == at:
                            after(act, "qk_ready", 2, s, i + 1)
                            copy_out(qk_f[:, i, :], m0_ps[:, :], "qk_copied")
                        if qkv and q == at + 1:
                            after(act, parts_stored[i], 16 * PARTS, s - 1, 16 * PARTS)
                            copy_out(qk_parts[:, i, 0, :], m0_ps[:, :], "qk_copied")
                    if mx and q == PE_V + 2:
                        b = s - 1
                        after(act, "v_ready", 1, b, 1)
                        after(act, "pv_ready", NG, b - 2, NG)
                        a.activation(vaug[1 - p][:, :, :, 0:DH],
                                     m1_ps[:, :].rearrange("p (t h d) -> p t h d", t=NT, h=H), ACT.Copy)\
                            .then_inc(S["v_copied"], 1)
                    for half, there, b in ((0, mx, s - 1), (1, soft, s - 2)):
                        if there and q == PE_MAX_T[half] + 1 + (half == 0):
                            after(act, "maxT_ready", 2, b, half + 1)
                            after(act, max_loaded[1 - half], 16, b - (1 - half), 16)
                            copy_out(neg_T[:, :], m1_ps[0:PARTS * HH, :].bitcast(BF16)[:, 0:T], "neg_copied")
                    if close and q == PE_AT + 1:
                        after(act, "aT_ready", 1, s - 3, 1)
                        after(act, "proj_ready", 1, s - 4, 1)
                        copy_out(attnT[:, :], m0_ps[:, :], "aT_copied")
                    if close and q == PE_H2T + 1:
                        after(act, "h2T_ready", 1, s - 3, 1)
                        after(act, "lgT_ready", 1, s - 4, 1)
                        copy_out(h2T[:, :], m0_ps[:, :], "h2T_copied")
                    if close and q == PE_LOGIT + 1:
                        after(act, "lgT_ready", 1, s - 3, 1)
                        after(act, "lg_ready", 1, s - 4, 1)
                        copy_out(logitT[:, :], m0_ps[:, 0:P], "lgT_copied")
                    if soft:
                        exp(s - 2, q)

            steps(act, step)

            def gelu(k, r):
                act.wait_ge(S["hB_ready"], k + 1)
                if not (isinstance(k, int) and k < 2):
                    after(act, "gT_ready", 1, k, -1)
                a.activation(hg[r], h_ps[:, r, :], ACT.Gelu).then_inc(S["gelu_done"], 1)

            gelu(0, 0)
            gelu(1, 1)
            with act.Fori(1, TILES // 2) as n:
                gelu(2 * n, 0)
                gelu(2 * n + 1, 1)

        @block.tensor
        def _(pe):
            t_ = nc.tensor

            def mm(o, l, r, start=True, stop=True):
                return t_.matmul(o, l, r, start=start, stop=stop, skip_group_check=True)

            pe.wait_ge(S["const_done"], 16)
            pe.wait_ge(S["silu_done"], 1)
            t_.transpose(m0_ps[:, 0:NB], c_silu[:, :], ident[0:NB, 0:NB]).then_inc(S["cT_ready"], 1)
            pe.wait_ge(S["cT_done"], 1)
            mm(m0_ps[0:NB, :], c_T[:, :], wmod_sb[:, 0:BANK])
            mm(m1_ps[0:NB, 0:6 * D - BANK], c_T[:, :], wmod_sb[:, BANK:6 * D]).then_inc(S["modps_ready"], 1)
            for i in range(6):
                last = mm(pv_ps[:, i * NB:(i + 1) * NB], wmod_sb[:, i * D:(i + 1) * D], c_T[:, :])
            last.then_inc(S["modT_ready"], 1)
            pe.wait_ge(S["modn_done"], 2)
            pe.wait_ge(S["modT_done"], 2)
            pe.wait_ge(S["w_loaded"], 64)
            pe.wait_ge(S["stacks_zero"], 8)
            pe.wait_ge(S["stacks_ones"], 2)
            pe.wait_ge(S["vaug_ones"], 2)
            pe.wait_ge(S["pv_zero"], 1)

            def sn_unit(b, par, u):
                gr, pair, k = u // GROUP_SLOTS, u // 5, u % 5
                if u % GROUP_SLOTS == 0:
                    after(pe, stack_loaded[gr], 16 * STACK_DMAS, b, 16 * STACK_DMAS)
                after(pe, "sn_read", 2 * SLOTS, b, 2 * max(u - 2, 0))
                o = sn_ps[:, u % 3, :]
                parts = {0: [(0, 3, 0)], 1: [(0, 0, 0), (0, 2, P)], 2: [(1, 3, 0)], 3: [(1, 0, 0), (1, 2, P)],
                         4: [(0, 1, 0), (1, 1, 2 * P)]}[k]
                for hd, t, col in parts:
                    h = 2 * pair + hd
                    mm(o[:, col:col + (t + 1) * P], qst[par][0:ROWS, h, t * P:(t + 1) * P],
                       kst[par][0:ROWS, h, 0:(t + 1) * P], stop=False)
                    last = mm(o[:, col + t * P:col + (t + 1) * P], ident_b[:, :], causal[:, :], start=False)
                last.then_inc(S["sn_ready"], 1)

            def st_unit(b, par, u):
                pair, k = u // 5, u % 5
                if u % (SLOTS // 2) == 0:
                    after(pe, max_loaded[u // (SLOTS // 2)], 16, b, 16)
                after(pe, "exp_done", SLOTS, b, u - 1)
                o = st_ps[:, u % 2, :]
                parts = {0: [(0, 0, 0)], 1: [(0, 3, 0), (0, 1, P)], 2: [(1, 0, 0)], 3: [(1, 3, 0), (1, 1, P)],
                         4: [(0, 2, 0), (1, 2, 2 * P)]}[k]
                for hd, t, col in parts:
                    h = 2 * pair + hd
                    last = mm(o[:, col:col + T - t * P], kst[par][:, h, t * P:(t + 1) * P],
                              qst[par][:, h, t * P:T])
                last.then_inc(S["st_ready"], 1)

            def pv(b, par, gr, j):
                if j == 0:
                    after(pe, "masked", H // 2, b, 2 * gr + 2)
                    after(pe, "pv_copied", NG, b, gr)
                    after(pe, "v_copied", 1, b, 1)
                for hd in range(4):
                    base_u, X = 5 * (hd // 2), hd % 2
                    u, col = {0: (2 * X, 0), 1: (2 * X + 1, P), 2: (4, 2 * P * X), 3: (2 * X + 1, 0)}[j]
                    last = mm(pv_ps[32 * hd:32 * hd + DH + 1, j * P:T], vaug[par][:, j, 4 * gr + hd, :],
                              probs[gr % 2][:, base_u + u, col:col + T - j * P], start=j == 0, stop=j == NT - 1)
                if j == NT - 1:
                    last.then_inc(S["pv_ready"], 1)

            def pv_transpose(b, gr):
                after(pe, "pv_copied", NG, b, gr + 1)
                for t in range(NT):
                    last = t_.transpose(m1_ps[:, t * P:(t + 1) * P], pvs[:, gr % 2, t * P:(t + 1) * P], ident[:, :])
                last.then_inc(S["pvT_ready"], 1)

            def four_transposes(ps, src, name):
                for t in range(NT):
                    last = t_.transpose(ps[:, t * P:(t + 1) * P], src[:, t, :], ident[:, :])
                last.then_inc(S[name], 1)

            def step(s, p, qkv, mx, soft, close):
                for q in range(SLOTS):
                    later = not isinstance(s, int)
                    if close and q == 2:
                        after(pe, "pvn_done", NG, s - 3, 2)
                        pv_transpose(s - 3, 2)
                    if close and q == 12:
                        if later or s - 2 < NB:
                            after(pe, "neg_copied", 2, s - 2, 2)
                        after(pe, "pvn_done", NG, s - 3, 3)
                        pv_transpose(s - 3, 3)
                    if soft and q == 22:
                        if later or s - 1 < NB:
                            after(pe, "v_copied", 1, s - 1, 1)
                        after(pe, "neg_copied", 2, s - 2, 2)
                        after(pe, "pvn_done", NG, s - 3, NG)
                        pv_transpose(s - 2, 0)
                    if soft and q == 32:
                        if later or s - 1 < NB:
                            after(pe, "neg_copied", 2, s - 1, 1)
                        after(pe, "pvn_done", NG, s - 2, 1)
                        pv_transpose(s - 2, 1)
                    if qkv and q == PE_XT:
                        after(pe, "xhat_done", NT, s, NT)
                        after(pe, "qk_copied", 4, s - 1, 4)
                        after(pe, "base_done", 1, s - 4, 1)
                        four_transposes(m0_ps, xhat, "xT_ready")
                    for i, at in ((0, PE_Q), (1, PE_K)):
                        if qkv and q == at:
                            after(pe, "hT_done", 1, s, 1)
                            after(pe, "qk_copied", 4, s, 2 * i)
                            if i == 1:
                                after(pe, "aT_copied", 1, s - 3, 1)
                            mm(m0_ps[:, :], wqkv[:, i * D:(i + 1) * D], hT[:, p, :]).then_inc(S["qk_ready"], 1)
                    if mx and q == PE_V:
                        after(pe, "hT_done", 1, s - 1, 1)
                        after(pe, "neg_copied", 2, s - 2, 2)
                        after(pe, "pvn_done", NG, s - 3, NG)
                        for t in range(NT):
                            last = mm(m1_ps[:, t * P:(t + 1) * P], hT[:, 1 - p, t * P:(t + 1) * P],
                                      wqkv[:, 2 * D:3 * D])
                        last.then_inc(S["v_ready"], 1)
                    for half, there, b in ((0, mx, s - 1), (1, soft, s - 2)):
                        if there and q == PE_MAX_T[half]:
                            if half == 0:
                                after(pe, "v_copied", 1, b, 1)
                                after(pe, "pvn_done", NG, b - 1, 1)
                            else:
                                after(pe, "neg_copied", 2, b, 1)
                                after(pe, "pvn_done", NG, b - 1, 3)
                            after(pe, "neg_done", 2, b, half + 1)
                            for t in range(NT):
                                last = t_.transpose(
                                    m1_ps[0:PARTS * HH, :].bitcast(BF16)[:, t * P:(t + 1) * P],
                                    neg_parts[:, half, t, :, :].rearrange("p i h -> p (i h)"), ident_b[:, :])
                            last.then_inc(S["maxT_ready"], 1)
                    if close:
                        b = s - 3
                        if q == PE_AT:
                            after(pe, "pvn_done", NG, b, NG)
                            if qkv:
                                after(pe, "qk_copied", 4, s, 2)
                            else:
                                after(pe, "base_done", 1, b - 1, 1)
                            four_transposes(m0_ps, attn[:, :, :, :].rearrange("p t h d -> p t (h d)"), "aT_ready")
                        if q == PE_PROJ:
                            after(pe, "aT_copied", 1, b, 1)
                            after(pe, "wpg_done", 1, b, 1)
                            if qkv:
                                after(pe, "qk_copied", 4, s, 4)
                            for t in range(NT):
                                last = mm(m0_ps[:, t * P:(t + 1) * P], attnT[:, t * P:(t + 1) * P], wpg[:, :])
                            last.then_inc(S["proj_ready"], 1)
                        if q == PE_H2T:
                            after(pe, "x1_done", 1, b, 1)
                            after(pe, "h2_done", 1, b, 1)
                            four_transposes(m0_ps, pack[1 - p][:, :, 0:D], "h2T_ready")
                        if q == PE_LOGIT:
                            after(pe, "h2T_copied", 1, b, 1)
                            for t in range(NT):
                                last = mm(m0_ps[32 * t:32 * t + 32, 0:P], gate_w[:, :], h2T[:, t * P:(t + 1) * P])
                            last.then_inc(S["lgT_ready"], 1)
                        if q == PE_LOGIT_T:
                            after(pe, "lgT_copied", 1, b, 1)
                            t_.transpose(m0_ps[:, 0:P], logitT[:, :], ident[:, :]).then_inc(S["lg_ready"], 1)
                        if q == PE_RANK:
                            after(pe, "onehot_done", 1, b, 1)
                            after(pe, "lg_read", 1, b, 1)
                            for t in range(NT + 1):
                                o = m0_ps[:, t * E:(t + 1) * E]
                                for u in range(min(t, NT)):
                                    last = mm(o, ones_b[:, :], onehot[:, u, :], start=u == 0, stop=u == NT - 1)
                                if t < NT:
                                    last = mm(o, before[:, :], onehot[:, t, :], start=t == 0)
                            last.then_inc(S["rank_ready"], 1)
                    if mx:
                        sn_unit(s - 1, 1 - p, q)
                    if soft:
                        st_unit(s - 2, p, q)
                    if q % GROUP_SLOTS in PV_SLOTS:
                        j = PV_SLOTS.index(q % GROUP_SLOTS)
                        gr = q // GROUP_SLOTS - 1
                        if gr < 0 and close:
                            pv(s - 3, 1 - p, 3, j)
                        if gr >= 0 and soft:
                            pv(s - 2, p, gr, j)

            steps(pe, step)

            pe.wait_ge(S["wffn_loaded"], 32)
            pe.wait_ge(S["bias_rows_loaded"], 32)
            pe.wait_ge(S["tab_done"], 1)

            def load_expert(k):
                return pe.value_load(t_e_i[0:1, bass.ds(k, 1)], min_val=0, max_val=E - 1)

            def turn(k, rb, n):
                r = rb % 2
                after(pe, row_loaded[rb], 16, n, 16)
                if not (isinstance(k, int) and k < 2):
                    after(pe, "tB_copied", 1, k, -1)
                t_.transpose(hT_ps[r][:, 0:P], rows[rb][:, 0:D], ident[:, :]).then_inc(S["tB_ready"], 1)

            def up(k, r):
                e = load_expert(k)
                if not (isinstance(k, int) and k < 2):
                    after(pe, "gelu_done", 1, k, -1)
                mm(h_ps[:, r, :], ones3[:, :], b1p[:, bass.ds(e * DFF, DFF)], stop=False)
                after(pe, "tB_copied", 1, k, 1)
                mm(h_ps[:, r, :], h2T_b[r], w1[:, bass.ds(e * DFF, DFF)], start=False).then_inc(S["hB_ready"], 1)

            def turn_hidden(k, r):
                after(pe, "gelu_done", 1, k, 1)
                if not (isinstance(k, int) and k < 2):
                    after(pe, "gT_copied", 1, k, -1)
                for f in range(FC):
                    last = t_.transpose(gT_ps[:, r, f * P:(f + 1) * P], hg[r][:, f * P:(f + 1) * P], ident[:, :])
                last.then_inc(S["gT_ready"], 1)

            def down(k, r):
                e = load_expert(k)
                if not (isinstance(k, int) and k < 2):
                    after(pe, "ygb_done", 1, k, -1)
                mm(y_ps[r][:, 0:D], ones3[:, :], b2p[:, bass.ds(e * D, D)], stop=False)
                after(pe, "gT_copied", 1, k, 1)
                for f in range(FC):
                    last = mm(y_ps[r][:, 0:D], hgT[r][:, f * P:(f + 1) * P],
                              w2[:, bass.ds(e * (FC * D) + f * D, D)], start=False, stop=f == FC - 1)
                last.then_inc(S["yB_ready"], 1)

            for k in range(RING):
                turn(k, k, 0)
                if k >= 2:
                    up(k - 2, k % 2)
                if k >= 3:
                    turn_hidden(k - 3, (k - 3) % 2)
                if k >= 4:
                    down(k - 4, k % 2)
            with pe.Fori(1, TILES // RING) as n:
                for r in range(RING):
                    turn(RING * n + r, r, n)
                    up(RING * n + r - 2, r % 2)
                    turn_hidden(RING * n + r - 3, (r + 1) % 2)
                    down(RING * n + r - 4, r % 2)
            for k in range(TILES, TILES + 4):
                if k < TILES + 2:
                    up(k - 2, k % 2)
                if k < TILES + 3:
                    turn_hidden(k - 3, (k - 3) % 2)
                down(k - 4, k % 2)

        @block.vector
        def _(dve):
            v = nc.vector

            for i in range(2):
                v.memset(qst[i][64:P, :, :].rearrange("p h t -> p (h t)").bitcast(U32), 0).then_inc(S["stacks_zero"], 2)
                v.memset(kst[i][64:P, :, :].rearrange("p h t -> p (h t)").bitcast(U32), 0).then_inc(S["stacks_zero"], 2)
            dve.wait_ge(S["stacks_zero"], 8)
            for i in range(2):
                v.memset(kst[i][MAX_ROW:MAX_ROW + PARTS, :, :], 1.0).then_inc(S["stacks_ones"], 1)
            dve.wait_ge(S["c_exp_done"], 1)
            dve.wait_ge(S["c_loaded"], 32)
            v.tensor_scalar(c_exp[:, :], c_exp[:, :], 1.0, None, op0=ALU.add).then_inc(S["setup_dve"], 1)
            dve.wait_ge(S["setup_dve"], 1)
            v.reciprocal(c_exp[:, :], c_exp[:, :]).then_inc(S["setup_dve"], 1)
            dve.wait_ge(S["setup_dve"], 2)
            v.tensor_tensor(c_silu[:, :], c_in[:, :], c_exp[:, :], op=ALU.mult).then_inc(S["silu_done"], 1)
            dve.wait_ge(S["cT_ready"], 1)
            v.tensor_copy(c_T[:, :], m0_ps[:, 0:NB]).then_inc(S["cT_done"], 1)
            dve.wait_ge(S["modps_ready"], 1)
            flat = mod_n[:, :, :].rearrange("b s d -> b (s d)")
            v.tensor_copy(flat[:, 0:BANK], m0_ps[0:NB, :]).then_inc(S["modn_done"], 1)
            v.tensor_copy(flat[:, BANK:6 * D], m1_ps[0:NB, 0:6 * D - BANK]).then_inc(S["modn_done"], 1)
            dve.wait_ge(S["modT_ready"], 1)
            v.tensor_copy(modT[:, :, :].rearrange("p s b -> p (s b)"), pv_ps[:, 0:6 * NB])\
                .then_inc(S["modT_done"], 1)
            dve.wait_ge(S["modT_done"], 1)
            v.tensor_scalar(modT[:, 1, :], modT[:, 1, :], 1.0, None, op0=ALU.add).then_inc(S["modT_done"], 1)
            v.memset(pv_ps[:, :], 0.0).then_inc(S["pv_zero"], 1)
            dve.wait_ge(S["modn_done"], 2)
            n0 = 2
            for src, dst in ((2, 0), (5, 3)):
                v.tensor_scalar(mod_t0[:, :], mod_n[:, src, :], 0.0, 2.0, op0=ALU.is_ge, op1=ALU.mult)\
                    .then_inc(S["setup_dve"], 1)
                v.scalar_tensor_tensor(out=mod_t1[:, :], in0=mod_n[:, src, :], scalar=-1.0, in1=mod_n[:, src, :],
                                       op0=ALU.mult, op1=ALU.max).then_inc(S["setup_dve"], 1)
                n0 += 2
                dve.wait_ge(S["setup_dve"], n0)
                v.tensor_scalar(mod_t1[:, :], mod_t1[:, :], 0.25, None, op0=ALU.max).then_inc(S["setup_dve"], 1)
                n0 += 1
                dve.wait_ge(S["setup_dve"], n0)
                v.scalar_tensor_tensor(out=mod_out[:, dst, :], in0=mod_t0[:, :], scalar=-1.0, in1=mod_t1[:, :],
                                       op0=ALU.add, op1=ALU.mult).then_inc(S["setup_dve"], 1)
                n0 += 1
                dve.wait_ge(S["setup_dve"], n0)
            v.tensor_scalar(mod_out[:, 1, :], mod_n[:, 4, :], 1.0, None, op0=ALU.add).then_inc(S["setup_dve"], 1)
            v.tensor_copy(mod_out[:, 2, :], mod_n[:, 3, :]).then_inc(S["setup_dve"], 1)
            dve.wait_ge(S["setup_dve"], n0 + 2)
            v.tensor_copy(mod_t0[:, :], mod_out[:, 2, :]).then_inc(S["modout_done"], 1)
            dve.wait_ge(S["bias_loaded"], 32)
            v.tensor_copy(bias_parts[:, 0, :], bias_in[:, :]).then_inc(S["bias_step"], 1)
            dve.wait_ge(S["bias_step"], 1)
            v.tensor_tensor(bias_r[:, :], bias_in[:, :], bias_parts[:, 0, :], op=ALU.subtract)\
                .then_inc(S["bias_step"], 1)
            dve.wait_ge(S["bias_step"], 2)
            v.tensor_copy(bias_parts[:, 1, :], bias_r[:, :]).then_inc(S["bias_step"], 1)
            dve.wait_ge(S["bias_step"], 3)
            v.tensor_tensor(bias_parts[:, 2, :], bias_r[:, :], bias_parts[:, 1, :], op=ALU.subtract)\
                .then_inc(S["bias_step"], 2)
            dve.wait_ge(S["const_done"], 16)
            dve.wait_ge(S["w_loaded"], 64)

            def layer_stats(src, tiles, stats, stat):
                for t in tiles:
                    v.bn_stats(stats[:, t, :], src(t)).then_inc(S[stat], 1)

            def layer_mv(stats, mv, stat, mvd, b):
                after(dve, stat, NT, b, NT)
                stand(dve)
                for t in range(NT):
                    v.bn_aggr(mv[:, t, :], stats[:, t, :]).then_inc(S[mvd], 1)

            def normalise(dst, src, tiles, mv, r, name):
                for t in tiles:
                    v.tensor_scalar(dst[:, t, :], src(t), mv[:, t, 0:1], r[:, t:t + 1],
                                    op0=ALU.subtract, op1=ALU.mult).then_inc(S[name], 1)

            def divide(b, gr):
                after(dve, "pvT_ready", NG, b, gr + 1)
                m = m1_ps[:, :].rearrange("p (t h d) -> p t h d", t=NT, h=4)
                v.reciprocal(rsum[:, :, :], m[:, :, :, DH]).then_inc(S["rsum_done"], 1)
                after(dve, "rsum_done", NG, b, gr + 1)
                if gr == 0:
                    after(dve, "aT_ready", 1, b - 1, 1)
                v.tensor_tensor(attn[:, :, 4 * gr:4 * gr + 4, :], m[:, :, :, 0:DH],
                                rsum[:, :, :].unsqueeze(3).to_broadcast([P, NT, 4, DH]), op=ALU.mult)\
                    .then_inc(S["pvn_done"], 1)

            def row_maxima(b, half):
                after(dve, "sn_read", 2 * SLOTS, b, SLOTS * (half + 1))
                by_head = rmax[:, :, HH * half:HH * (half + 1)].rearrange("p t (a x) -> p t a x", x=2)
                bm = bmax[:, 4 * half:4 * half + 4, :, :]
                v.tensor_reduce(by_head[:, 3, :, :], bm[:, :, 0:4:2, :], axis=AX_X, op=ALU.max)\
                    .then_inc(S["rmax_done"], 1)
                v.tensor_reduce(by_head[:, 2, :, :], bm[:, :, 1:5:2, 1:4], axis=AX_X, op=ALU.max)\
                    .then_inc(S["rmax_done"], 1)
                v.tensor_reduce(by_head[:, 1, :, :], bm[:, :, 4, :].rearrange("p a (x k) -> p a x k", x=2),
                                axis=AX_X, op=ALU.max).then_inc(S["rmax_done"], 1)
                v.tensor_copy(by_head[:, 0, :, :], bm[:, :, 1:5:2, 0]).then_inc(S["rmax_done"], 1)

            def negate(b, half):
                m, r, parts = rmax[:, :, HH * half:HH * (half + 1)], neg_r[:, half, :, :], neg_parts[:, half, :, :, :]
                after(dve, "rmax_done", 8, b, 4 * half + 4)
                after(dve, "maxT_ready", 2, b - 1, half + 1)
                v.tensor_scalar(parts[:, :, 0, :], m, -1.0, None, op0=ALU.mult).then_inc(S["neg_hi"], 1)
                after(dve, "neg_hi", 2, b, half + 1)
                v.scalar_tensor_tensor(out=r, in0=m, scalar=-1.0, in1=parts[:, :, 0, :],
                                       op0=ALU.mult, op1=ALU.subtract).then_inc(S["neg_rest"], 1)
                after(dve, "neg_rest", 2, b, half + 1)
                v.tensor_copy(parts[:, :, 1, :], r).then_inc(S["neg_mid"], 1)
                after(dve, "neg_mid", 2, b, half + 1)
                v.tensor_tensor(parts[:, :, 2, :], r, parts[:, :, 1, :], op=ALU.subtract)\
                    .then_inc(S["neg_done"], 1)

            def choose(b):
                after(dve, "lg_ready", 1, b, 1)
                m = m0_ps[:, 0:P].rearrange("p (t e) -> p t e", t=NT)[:, :, 0:E]
                v.tensor_tensor(logit[:, :, :], m, gate_bias[:, :].unsqueeze(1).to_broadcast([P, NT, E]), op=ALU.add)\
                    .then_inc(S["lg_read"], 1)
                after(dve, "lg_read", 1, b, 1)
                v.tensor_reduce(lmax[:, :], logit[:, :, :], axis=AX_X, op=ALU.max).then_inc(S["lmax_done"], 1)
                after(dve, "lmax_done", 1, b, 1)
                v.tensor_tensor(first[:, :, :], logit[:, :, :], lmax[:, :].unsqueeze(2).to_broadcast([P, NT, E]),
                                op=ALU.is_ge).then_inc(S["first_done"], 1)
                after(dve, "first_done", 2, b, 1)
                v.tensor_tensor(first[:, :, :], first[:, :, :], rank_of_e[:, :].unsqueeze(1).to_broadcast([P, NT, E]),
                                op=ALU.mult).then_inc(S["first_done"], 1)
                after(dve, "first_done", 2, b, 2)
                v.tensor_reduce(fmax[:, :], first[:, :, :], axis=AX_X, op=ALU.max).then_inc(S["fmax_done"], 1)
                after(dve, "fmax_done", 1, b, 1)
                after(dve, "rank_ready", 1, b - 1, 1)
                v.tensor_tensor(onehot[:, :, :], rank_of_e[:, :].unsqueeze(1).to_broadcast([P, NT, E]),
                                fmax[:, :].unsqueeze(2).to_broadcast([P, NT, E]), op=ALU.is_equal)\
                    .then_inc(S["onehot_done"], 1)

            def place(b, par):
                after(dve, "rank_ready", 1, b, 1)
                m = m0_ps[:, 0:(NT + 1) * E].rearrange("p (t e) -> p t e", t=NT + 1)
                after(dve, "base_done", 1, b - 1, 1)
                v.tensor_tensor(posm[:, :, :], m[:, 0:NT, :], base[:, :].unsqueeze(1).to_broadcast([P, NT, E]),
                                op=ALU.add).then_inc(S["posm_done"], 1)
                after(dve, "posm_done", 1, b, 1)
                v.tensor_tensor(base[:, :], m[:, NT, :], base[:, :], op=ALU.add).then_inc(S["base_done"], 1)
                v.tensor_tensor(posm[:, :, :], posm[:, :, :], onehot[:, :, :], op=ALU.mult).then_inc(S["posm_sel"], 1)
                after(dve, "posm_sel", 1, b, 1)
                v.tensor_reduce(pos[:, :], posm[:, :, :], axis=AX_X, op=ALU.add).then_inc(S["pos_done"], 1)
                after(dve, "pos_done", 1, b, 1)
                after_scatter(dve, b - 2, par)
                v.tensor_copy(pos_u[:, par, :], pos[:, :]).then_inc(S["pos_u_done"], 1)

            def step(s, p, qkv, mx, soft, close):
                b = s - 3
                xs = lambda t: xin[:, p, t, :]
                x1s = lambda t: pack[1 - p][:, t, D:2 * D]
                for q in range(SLOTS):
                    if qkv and q == 0:
                        after(dve, "x_loaded", 16, s, 16)
                        after(dve, "rstd1_add", 1, s - 1, 1)
                    if qkv and q < 2:
                        layer_stats(xs, (2 * q, 2 * q + 1), stats1, "ln1_stat")
                    if qkv and q == 2:
                        layer_mv(stats1, mv1, "ln1_stat", "ln1_mv", s)
                    if qkv and q == 5:
                        after(dve, "rstd1_done", 1, s, 1)
                        after(dve, "xT_ready", 1, s - 1, 1)
                    if qkv and q in (5, 6):
                        normalise(xhat, xs, (2 * q - 10, 2 * q - 9), mv1, rstd1, "xhat_done")
                    for i, at in ((0, PE_Q + 4), (1, PE_K + 4)):
                        if qkv and q == at:
                            after(dve, "r1_done", 2, s, i + 1)
                            v.tensor_copy(qk_parts[:, i, 1, :], qk_r[:, i, :]).then_inc(S["qm_done"], 1)
                    if q % GROUP_SLOTS == 3:
                        gr = (q // GROUP_SLOTS - 2) % NG
                        if gr >= 2 and close:
                            divide(b, gr)
                        if gr < 2 and soft:
                            divide(s - 2, gr)
                    if close and q == PE_PROJ + 1:
                        after(dve, "proj_ready", 1, b, 1)
                        after(dve, "res_loaded", 48, b, 48)
                        after_scatter(dve, b - 2, 1 - p)
                        v.tensor_tensor(pack[1 - p][:, :, D:2 * D], m0_ps[:, :].rearrange("p (t d) -> p t d", t=NT),
                                        xres[:, 1 - p, :, :], op=ALU.add).then_inc(S["x1_done"], 1)
                    if close and q == PE_PROJ + 2:
                        after(dve, "x1_done", 1, b, 1)
                        after(dve, "rstd2_add", 1, b - 1, 1)
                    if close and q in (PE_PROJ + 2, PE_PROJ + 3):
                        t = 2 * (q - PE_PROJ - 2)
                        layer_stats(x1s, (t, t + 1), stats2, "ln2_stat")
                    if close and q == PE_PROJ + 4:
                        layer_mv(stats2, mv2, "ln2_stat", "ln2_mv", b)
                    if close and q == PE_PROJ + 6:
                        after(dve, "rstd2_done", 1, b, 1)
                        after(dve, "h2m_done", 1, b - 1, 1)
                    if close and q in (PE_PROJ + 6, PE_PROJ + 7):
                        t = 2 * (q - PE_PROJ - 6)
                        normalise(xhat2, x1s, (t, t + 1), mv2, rstd2, "xhat2_done")
                    if mx:
                        after(dve, "sn_ready", SLOTS, s - 1, q + 1)
                        v.tensor_reduce(bmax[:, q // 5, q % 5, :],
                                        sn_ps[:, q % 3, :].rearrange("p (k n) -> p k n", k=4),
                                        axis=AX_X, op=ALU.max).then_inc(S["sn_read"], 2)
                    for half, there, mb in ((0, mx, s - 1), (1, soft, s - 2)):
                        if there and q == PE_MAX_T[half] - 5:
                            row_maxima(mb, half)
                        if there and q == PE_MAX_T[half] - 2:
                            negate(mb, half)
                    if close and q == PE_LOGIT_T + 1:
                        choose(b)
                    if close and q == PE_RANK + 1:
                        place(b, 1 - p)

            steps(dve, step)

            dve.wait_ge(S["base_done"], NB)
            dve.wait_ge(S["const_done"], 16)
            n = [0]

            def link(ins):
                n[0] += 1
                ins.then_inc(S["tab_step"], 1)
                dve.wait_ge(S["tab_step"], n[0])

            v.tensor_copy(base_i[:, :], base[0:1, :]).then_inc(S["base_i_done"], 1)
            link(v.tensor_tensor(cnt[:, :], base[0:1, :], e_cap[:, :], op=ALU.subtract))
            link(v.tensor_tensor(nt_cmp[:, :, :], cnt[:, :].unsqueeze(2).to_broadcast([1, E, N // P]),
                                 m_128[:, :].unsqueeze(1).to_broadcast([1, E, N // P]), op=ALU.is_gt))
            link(v.tensor_reduce(nt_e[:, :], nt_cmp[:, :, :], axis=AX_X, op=ALU.add))
            link(v.tensor_tensor(nt_m[:, :, :], low_e[:, :, :], nt_e[:, :].unsqueeze(1).to_broadcast([1, E, E]),
                                 op=ALU.mult))
            link(v.tensor_reduce(nt_end[:, :], nt_m[:, :, :], axis=AX_X, op=ALU.add))
            link(v.tensor_tensor(t_ge[:, :, :], t_iota[:, :].unsqueeze(2).to_broadcast([1, TILES, E]),
                                 nt_end[:, :].unsqueeze(1).to_broadcast([1, TILES, E]), op=ALU.is_ge))
            link(v.tensor_tensor(t_gn[:, :, :], t_ge[:, :, :], nt_e[:, :].unsqueeze(1).to_broadcast([1, TILES, E]),
                                 op=ALU.mult))
            link(v.tensor_reduce(t_e[:, :], t_ge[:, :, :], axis=AX_X, op=ALU.add))
            link(v.tensor_reduce(t_b[:, :], t_gn[:, :, :], axis=AX_X, op=ALU.add))
            link(v.tensor_tensor(t_row[:, :], t_iota[:, :], t_b[:, :], op=ALU.subtract))
            link(v.tensor_scalar(t_row[:, :], t_row[:, :], float(P), None, op0=ALU.mult))
            link(v.scalar_tensor_tensor(out=t_row1[:, :], in0=t_e[:, :], scalar=float(CAP), in1=t_row[:, :],
                                        op0=ALU.mult, op1=ALU.add))
            link(v.tensor_scalar(t_row_i[:, :], t_row1[:, :], float(SPARE), None, op0=ALU.min))
            link(v.tensor_scalar(t_e_i[:, :], t_e[:, :], float(E - 1), None, op0=ALU.min))
            v.tensor_copy(t_b[:, :], t_e[:, :]).then_inc(S["tab_done"], 1)

            def tile_in(k, r):
                dve.wait_ge(S["tB_ready"], k + 1)
                if not (isinstance(k, int) and k < 2):
                    after(dve, "hB_ready", 1, k, -1)
                v.tensor_copy(h2T_b[r], hT_ps[r][:, 0:P]).then_inc(S["tB_copied"], 1)

            def tile_hidden(k, r):
                dve.wait_ge(S["gT_ready"], k + 1)
                if not (isinstance(k, int) and k < 2):
                    after(dve, "yB_ready", 1, k, -1)
                v.tensor_copy(hgT[r], gT_ps[:, r, :]).then_inc(S["gT_copied"], 1)

            def tile_close(k, rb, n):
                r = rb % 2
                dve.wait_ge(S["yB_ready"], k + 1)
                after(dve, row_loaded[rb], 16, n, 16)
                v.tensor_tensor(ygb[r], y_ps[r][:, 0:D], rows[rb][:, 2 * D:3 * D], op=ALU.mult)\
                    .then_inc(S["ygb_done"], 1)
                dve.wait_ge(S["ygb_done"], k + 1)
                if not (isinstance(n, int) and n == 0):
                    after(dve, out_stored[rb], 16, n - 1, 16)
                v.tensor_tensor(y_b[rb], ygb[r], rows[rb][:, D:2 * D], op=ALU.add).then_inc(S["y_done"], 1)

            for k in range(RING):
                tile_in(k, k % 2)
                if k >= 3:
                    tile_hidden(k - 3, (k - 3) % 2)
                if k >= 4:
                    tile_close(k - 4, k - 4, 0)
            with dve.Fori(1, TILES // RING) as n:
                for r in range(RING):
                    tile_in(RING * n + r, r % 2)
                    tile_hidden(RING * n + r - 3, (r + 1) % 2)
                    tile_close(RING * n + r - 4, (r - 4) % RING, n if r >= 4 else n - 1)
            for k in range(TILES, TILES + 4):
                if k < TILES + 3:
                    tile_hidden(k - 3, (k - 3) % 2)
                tile_close(k - 4, (k - 4) % RING, TILES // RING - 1)


_INS = ["L0_attn_x", "L0_attn_Wqkv", "L0_attn_Wproj", "L0_ffn_gate_W", "L0_ffn_gate_b", "L0_ffn_W1", "L0_ffn_b1",
        "L0_ffn_W2", "L0_ffn_b2", "L0_c", "L0_wmod"]


def kernel(**inputs):
    import numpy as _np
    import concourse.bacc as _bacc
    from concourse import mybir as _mybir
    from concourse.bass_utils import run_bass_kernel_spmd as _run

    nc = _bacc.Bacc("TRN2", target_bir_lowering=False, num_devices=1)
    arrays, args = {}, []
    for name in _INS:
        a = _np.ascontiguousarray(inputs[name])
        arrays[f"in_{name}_dram"] = a
        args.append(nc.dram_tensor(f"in_{name}_dram", a.shape, _mybir.dt.from_np(a.dtype), kind="ExternalInput").ap())
    shape = inputs["L0_attn_x"].shape
    args.append(nc.dram_tensor("out_0_dram", shape, F32, kind="ExternalOutput").ap())
    block_kernel(nc, *args)
    r = _run(nc, [arrays], core_ids=[0])
    return r.results[0]["out_0_dram"]
```

```python
from contextlib import ExitStack

import concourse.bass as bass
from concourse import mybir

ALU = mybir.AluOpType
ACT = mybir.ActivationFunctionType
F32 = mybir.dt.float32
BF16 = mybir.dt.bfloat16
I32 = mybir.dt.int32
U32 = mybir.dt.uint32
AX_X = mybir.AxisListType.X

P = 128
PARTS = 3
NEG = -1e30
BANK = 512
EPS = 1e-5

SLOTS = 40
GROUP_SLOTS = 10
AT = {
    "xT": 9, "q": 11, "k": 14, "aT": 17, "v": 21, "proj": 20,
    "h2T": 31, "logit": 35, "logit_T": 36, "rank": 39, "max_T": (30, 8), "pv": (4, 6, 7, 9),
    "pv_T": 2,
    "pv_copy": 0,
    "hT": 9, "q_f": 11, "q_hi": 11, "k_f": 13, "k_hi": 13, "q_mid": 13, "k_mid": 19,
    "aT_copy": 18, "v_copy": 20, "neg_copy": (29, 8),
    "h2T_copy": 31, "logit_copy": 35,
    "stats1": (1, 1, 3, 3), "mv1": 6, "xhat": (10, 11, 12, 12), "divide": (8, 9), "x1": 40,
    "stats2": (42, 42, 44, 44), "mv2": 45, "xhat2": (50, 50, 52, 52), "row_maxima": (44, 0),
    "negate": ((49, 50, 51, 52), (7, 8, 9, 10)),
    "choose": (71, 71, 72, 73, 74, 75), "place": (78, 78, 79, 79),
    "rstd1": 2, "wpg": 4, "scatter": (20, 22, 32, 34), "q_rest": 13, "q_lo": 15, "k_rest": 17, "k_lo": 20,
    "rstd2": 25, "h2": 26,
    "tile": (11, 15, 19, 23, 27, 31, 35, 39),
}


def block_kernel(nc, x, Wqkv, Wproj, gate_W, gate_b, W1, b1, W2, b2, c, wmod, out):
    NB, T, D = x.shape
    E = gate_W.shape[1]
    DFF = W1.shape[2]
    H = 16
    DH = D // H
    NT = T // P
    NG = H // 4
    N = NB * T
    SCALE = float(DH) ** -0.5
    ROWS = PARTS * PARTS * DH
    ROWS_MAX = ROWS + PARTS
    CAP = N + P
    SPARE = E * CAP
    RW = 388
    IDX = 3 * D
    TILES = N // P + E
    FC = DFF // P
    UP = DFF + FC
    RING = 8
    EARLY = ((NB - 2) * T - E * (P - 1)) // P // RING * RING
    NO_TOKEN = float(2 * N)
    assert T == BANK and D == P and NT == 4 and NG == 4 and NB % 2 == 0 and NB >= 8 and TILES % RING == 0
    assert EARLY > 3 * RING and E == RING

    parts_d = nc.dram_tensor("parts_d", [2, PARTS, DH, H, T], BF16).ap()
    mod_d = nc.dram_tensor("mod_d", [NB, 4, D], F32).ap()
    rows_d = nc.dram_tensor("rows_d", [E * CAP + P, RW], F32).ap()
    b2_d = nc.dram_tensor("b2_d", [PARTS, E * D], BF16).ap()

    ctx = ExitStack()
    with ctx:
        def sb(name, shape, dt=F32):
            return ctx.enter_context(nc.sbuf_tensor(name, shape, dt))

        def psum(name, shape, dt=F32):
            return ctx.enter_context(nc.psum_tensor(name, shape, dt))

        def sem(name):
            return ctx.enter_context(nc.semaphore(name))

        sn_ps = psum("sn_ps", [P, 3, BANK])
        st_ps = psum("st_ps", [P, 2, BANK])
        pv_ps = psum("pv_ps", [P, BANK])
        m0_ps = psum("m0_ps", [P, BANK])
        m1_ps = psum("m1_ps", [P, BANK])

        ident = sb("ident", [P, P])
        ident_b = sb("ident_b", [P, P], BF16)
        causal = sb("causal", [P, P], BF16)
        before = sb("before", [P, P], BF16)
        ones_b = sb("ones_b", [P, P], BF16)
        wqkv = sb("wqkv", [P, 3 * D])
        wproj = sb("wproj", [P, D])
        gate_w = sb("gate_w", [P, 32])
        gate_bias = sb("gate_bias", [P, E])
        rank_of_e = sb("rank_of_e", [P, E])
        w1 = sb("w1", [P, E * UP])
        ones3 = sb("ones3", [PARTS, P], BF16)
        eps = sb("eps", [P, NT])
        half = sb("half", [P, NT])
        modT = sb("modT", [P, 6, NB])
        c_in = sb("c_in", [NB, D])
        c_exp = sb("c_exp", [NB, D])
        c_silu = sb("c_silu", [NB, D])
        c_T = sb("c_T", [P, NB])
        wmod_sb = sb("wmod_sb", [P, 6 * D])
        mod_n = sb("mod_n", [NB, 6, D])
        mod_out = sb("mod_out", [NB, 4, D])
        mod_t0 = sb("mod_t0", [NB, D])
        mod_t1 = sb("mod_t1", [NB, D])
        NBIAS = E * D // P
        b1_in = sb("b1_in", [E * FC, P])
        bias_in = sb("bias_in", [P, NBIAS])
        bias_r = sb("bias_r", [P, NBIAS])
        bias_parts = sb("bias_parts", [P, PARTS, NBIAS], BF16)
        xin = sb("xin", [P, 2, NT, D])
        stats1 = sb("stats1", [P, NT, 6])
        mv1 = sb("mv1", [P, NT, 2])
        var1 = sb("var1", [P, NT])
        rstd1 = sb("rstd1", [P, NT])
        xhat = sb("xhat", [P, NT, D])
        hT = sb("hT", [P, 2, T])
        qk_f = sb("qk_f", [P, 2, T])
        qk_r = sb("qk_r", [P, 2, T])
        qk_parts = sb("qk_parts", [P, 2, PARTS, T], BF16)
        qst = [sb(f"qst{i}", [P, H, T], BF16) for i in range(2)]
        kst = [sb(f"kst{i}", [P, H, T], BF16) for i in range(2)]
        vaug = [sb(f"vaug{i}", [P, NT, H, DH + 1]) for i in range(2)]
        bmax = sb("bmax", [P, H // 2, 5, 4])
        rmax = sb("rmax", [P, NT, H])
        HH = H // 2
        neg_r = sb("neg_r", [P, 2, NT, HH])
        neg_parts = sb("neg_parts", [P, 2, NT, PARTS, HH], BF16)
        neg_T = sb("neg_T", [PARTS * HH, T], BF16)
        probs = [sb(f"probs{i}", [P, 10, T]) for i in range(2)]
        pvs = sb("pvs", [P, 2, T])
        rsum = sb("rsum", [P, NT, 4])
        attn = sb("attn", [P, NT, H, DH])
        attnT = sb("attnT", [P, T])
        wpg = sb("wpg", [P, D])
        xres = sb("xres", [P, 2, NT, D])
        modb = sb("modb", [P, 2, 3, D])
        pack = [sb(f"pack{i}", [P, NT, RW]) for i in range(2)]
        stats2 = sb("stats2", [P, NT, 6])
        mv2 = sb("mv2", [P, NT, 2])
        var2 = sb("var2", [P, NT])
        rstd2 = sb("rstd2", [P, NT])
        xhat2 = sb("xhat2", [P, NT, D])
        h2m = sb("h2m", [P, NT, D])
        h2T = sb("h2T", [P, T])
        logitT = sb("logitT", [P, P])
        logit = sb("logit", [P, NT, E])
        lmax = sb("lmax", [P, NT])
        first = sb("first", [P, NT, E])
        fmax = sb("fmax", [P, NT])
        onehot = sb("onehot", [P, NT, E], BF16)
        posm = sb("posm", [P, NT, E])
        pos = sb("pos", [P, NT])
        pos_u = sb("pos_u", [P, 2, NT], U32)
        base = sb("base", [P, E])
        e_cap = sb("e_cap", [1, E])
        m_128 = sb("m_128", [1, N // P])
        t_iota = sb("t_iota", [1, TILES])
        low_e = sb("low_e", [1, E, E])
        cnt = sb("cnt", [1, E])
        nt_cmp = qk_r[0:1, 0, :].rearrange("p (e n) -> p e n", e=E)[:, :, 0:N // P]
        nt_e = sb("nt_e", [1, E])
        taken = sb("taken", [1, E + 1])
        nt_rest = sb("nt_rest", [1, E])
        nt_step = sb("nt_step", [1, E])
        nt_m = sb("nt_m", [1, E, E])
        nt_end = sb("nt_end", [1, E])
        t_ge = hT[0:1, :, :].rearrange("p a t -> p (a t)")[:, 0:TILES * E].rearrange("p (k e) -> p k e", e=E)
        t_gn = qk_f[0:1, :, :].rearrange("p a t -> p (a t)")[:, 0:TILES * E].rearrange("p (k e) -> p k e", e=E)
        t_e = sb("t_e", [1, TILES])
        t_b = sb("t_b", [1, TILES])
        t_row = sb("t_row", [1, TILES])
        t_row1 = sb("t_row1", [1, TILES])
        t_row_i = sb("t_row_i", [1, TILES], I32)
        t_e_i = sb("t_e_i", [1, TILES], I32)
        base_i = sb("base_i", [1, E], I32)
        pad = sb("pad", [P, RW])

        stack_f = qst[0][:, :, :].rearrange("p h t -> p (h t)").bitcast(F32)
        stack_g = qst[1][:, :, :].rearrange("p h t -> p (h t)").bitcast(F32)
        rows = [stack_f[:, i * RW:(i + 1) * RW] for i in range(RING)]
        h2T_b = [stack_f[:, 3200 + i * P:3200 + (i + 1) * P] for i in range(2)]
        ygb = [stack_f[:, 3584 + i * D:3584 + (i + 1) * D] for i in range(2)]
        hgT = [stack_g[:, i * DFF:(i + 1) * DFF] for i in range(2)]
        w1_b = [stack_g[:, 1024 + i * UP:1024 + (i + 1) * UP] for i in range(2)]
        y_b = [stack_g[:, 2176 + i * D:2176 + (i + 1) * D] for i in range(RING)]
        idx_u = sb("idx_u", [P, RING], U32)
        h_ps, y_ps = sn_ps, st_ps
        hT_ps = [sn_ps[:, 2, :], pv_ps]
        w2 = kst[0][:, :, :].rearrange("p h t -> p (h t)").bitcast(F32)[:, 0:E * FC * D]
        b2p = kst[1][:, :, :].rearrange("p h t -> p (h t)")[0:PARTS, 0:E * D]

        names = """passed const_done ident_done gate_w_zero w_loaded c_loaded c_exp_done silu_done cT_ready cT_done
            modps_ready modn_done modT_ready modT_done modout_done mod_stored bias_loaded bias_step
            bias_stored bias_rows_loaded b1_loaded b1T_ready b1_placed stacks_ones vaug_ones pv_zero setup_dve
            pad_done wffn_loaded""".split()
        names += """x_loaded ln1_stat ln1_mv rstd1_add rstd1_done xhat_done xT_ready hT_done qk_ready qk_copied
            r1_done qm_done ql_done v_ready v_copied""".split()
        names += """sn_ready sn_read rmax_done neg_hi neg_rest neg_mid neg_done maxT_ready neg_copied
            """.split()
        names += """st_ready exp_done masked pv_ready pv_copied pvT_ready rsum_done pvn_done""".split()
        names += """res_loaded wpg_done aT_ready aT_copied proj_ready x1_done ln2_stat ln2_mv rstd2_add rstd2_done
            xhat2_done h2m_done h2_done h2T_ready h2T_copied lgT_ready lgT_copied lg_ready lg_read lmax_done
            first_done fmax_done onehot_done rank_ready posm_done posm_sel pos_done base_done pos_u_done idx_moved
            """.split()
        names += """base_i_done tab_step tab_early_done tab_done w1_copied spare_stored pads_stored tB_ready tB_copied hB_ready gelu_done yB_ready
            ygb_done y_done idx_done""".split()
        S = {n: sem(n) for n in names}
        parts_stored = [sem(f"parts_stored{i}") for i in range(2)]
        stack_loaded = [sem(f"stack_loaded{g}") for g in range(NG)]
        scattered = [sem(f"scattered{i}") for i in range(2)]
        max_loaded = [sem(f"max_loaded{i}") for i in range(2)]
        row_loaded = [sem(f"row_loaded{i}") for i in range(RING)]
        out_stored = [sem(f"out_stored{i}") for i in range(RING)]

        def after(eng, name, per, b, k):
            s = S[name] if isinstance(name, str) else name
            v = per * b + k
            if isinstance(v, int) and v <= 0:
                return
            eng.wait_ge(s, v)

        def stand(eng):
            eng.sem_inc(S["passed"], 1)

        def after_scatter(eng, b, par):
            after(eng, scattered[par], 32, b - par, 64)

        STACK_DMAS = 4
        block = ctx.enter_context(nc.Block())

        def steps(eng, step):
            for s in range(6):
                step(s, s % 2, s < NB, 1 <= s <= NB, s >= 2, s >= 3)
            with eng.Fori(3, NB // 2) as i:
                step(2 * i, 0, True, True, True, True)
                step(2 * i + 1, 1, True, True, True, True)
            for s in range(NB, NB + 3):
                step(s, s % 2, False, s <= NB, s <= NB + 1, True)

        def tile_of(s, q):
            if isinstance(s, int) and s == NB + 2 and q in AT["tile"]:
                return AT["tile"].index(q)

        @block.sync
        def _(sp):
            sp.dma_start(c_in[:, :], c).then_inc(S["c_loaded"], 16)
            sp.dma_start(wmod_sb[:, :], wmod).then_inc(S["c_loaded"], 16)
            sp.dma_start(xin[:, 0, :, :], x[0].rearrange("(t p) d -> p t d", p=P)).then_inc(S["x_loaded"], 16)
            sp.wait_ge(S["gate_w_zero"], 1)
            sp.dma_start(gate_w[:, 0:E], gate_W).then_inc(S["w_loaded"], 16)
            sp.dma_start(wqkv[:, :], Wqkv).then_inc(S["w_loaded"], 16)
            sp.dma_start(wproj[:, :], Wproj).then_inc(S["w_loaded"], 16)
            sp.dma_start(gate_bias[:, :], gate_b.partition_broadcast(P)).then_inc(S["w_loaded"], 16)
            sp.dma_start(b1_in[:, :], b1.rearrange("e (c p) -> (e c) p", p=P)).then_inc(S["b1_loaded"], 16)
            sp.dma_start(bias_in[:, :], b2.rearrange("e (a n) -> (e a) n", n=NBIAS)).then_inc(S["bias_loaded"], 16)
            sp.wait_ge(S["const_done"], 16)
            for i in range(2):
                sp.dma_start(kst[i][ROWS:ROWS_MAX, :, :].rearrange("r h (a n) -> r (h a) n", n=P),
                             ones3[:, :].unsqueeze(1).to_broadcast([PARTS, H * NT, P])).then_inc(S["stacks_ones"], 16)

            def store_setup():
                sp.wait_ge(S["modout_done"], 1)
                sp.dma_start(mod_d, mod_out[:, :, :]).then_inc(S["mod_stored"], 16)
                sp.wait_ge(S["bias_step"], 5)
                sp.dma_start(b2_d.rearrange("i (p n) -> p i n", p=P), bias_parts[:, :, :])\
                    .then_inc(S["bias_stored"], 16)
                sp.wait_ge(S["mod_stored"], 16)

            def load_for_phase_b():
                sp.dma_start(w1[:, :].rearrange("p (e f) -> p e f", e=E)[:, :, 0:DFF], W1.rearrange("e p f -> p e f"))\
                    .then_inc(S["wffn_loaded"], 16)
                sp.wait_ge(S["pad_done"], 1)
                sp.dma_start(rows_d[SPARE:SPARE + P, :], pad[:, :]).then_inc(S["spare_stored"], 16)

            def step(s, p, qkv, mx, soft, close):
                b = s
                if isinstance(s, int) and s == NB + 1:
                    sp.wait_ge(S["st_ready"], SLOTS * (NB - 1))
                    sp.dma_start(w2.rearrange("p (e c d) -> p e c d", e=E, c=FC),
                                 W2.rearrange("e (c p) d -> p e c d", p=P)).then_inc(S["wffn_loaded"], 16)
                if not isinstance(s, int) or s + 1 < NB:
                    after(sp, "xhat_done", NT, b - 1, NT)
                    nxt = s + 1 if isinstance(s, int) or p == 0 else (s + 1) % NB
                    after(sp, "x_loaded", 16, b, 16)
                    sp.dma_start(xin[:, 1 - p, :, :], xt_d(nxt)).then_inc(S["x_loaded"], 16)
                if soft:
                    load_max(s - 2, p, 1)
                if qkv:
                    for i in range(2):
                        if i == 0:
                            for g in range(NG):
                                after(sp, stack_loaded[g], 16 * STACK_DMAS, b - 1, 16 * STACK_DMAS)
                        after(sp, "ql_done", 2, b, i + 1)
                        for j in range(PARTS):
                            sp.dma_start(parts_d[i, j].rearrange("d h n -> h d n"), qk_parts[:, i, j, :])\
                                .then_inc(parts_stored[i], 16)
                    for i in range(2):
                        after(sp, parts_stored[i], 16 * PARTS, b, 16 * PARTS)
                for g in range(NG):
                    if g == NG - 1 and mx:
                        load_max(s - 1, 1 - p, 0)
                    if qkv:
                        after(sp, "st_ready", SLOTS, b - 2, GROUP_SLOTS * (g + 1))
                        q_d = parts_d[0].rearrange("i d h n -> (i d) (h n)")[:, 4 * g * T:4 * (g + 1) * T]
                        k_d = parts_d[1].rearrange("i d h n -> i d (h n)")[:, :, 4 * g * T:4 * (g + 1) * T]
                        rows_q = PARTS * DH
                        sp.dma_start(qst[p][0:ROWS, 4 * g:4 * g + 4, :],
                                     q_d.unsqueeze(0).to_broadcast([PARTS, rows_q, 4 * T]))\
                            .then_inc(stack_loaded[g], 16)
                        for j in range(PARTS):
                            sp.dma_start(kst[p][j * rows_q:(j + 1) * rows_q, 4 * g:4 * g + 4, :],
                                         k_d[j].unsqueeze(0).to_broadcast([PARTS, DH, 4 * T]))\
                                .then_inc(stack_loaded[g], 16)
                if isinstance(s, int) and s == 0:
                    store_setup()
                if isinstance(s, int) and s == 1:
                    load_for_phase_b()
                if soft and (not isinstance(s, int) or s - 2 < NB):
                    cb = s - 2
                    after(sp, "res_loaded", 48, cb - 1, 48)
                    after(sp, "x1_done", 1, cb - 2, 1)
                    sp.dma_start(xres[:, p, :, :], xt_d(cb)).then_inc(S["res_loaded"], 16)
                    after(sp, "h2_done", 1, cb - 2, 1)
                    after(sp, "wpg_done", 1, cb - 2, 1)
                    sp.dma_start(modb[:, p, :, :], mod_row(cb)[0:3, :].partition_broadcast(P))\
                        .then_inc(S["res_loaded"], 16)
                    after_scatter(sp, cb - 2, p)
                    sp.dma_start(pack[p][:, :, 2 * D:3 * D],
                                 mod_row(cb)[3, :].partition_broadcast(P).unsqueeze(1).to_broadcast([P, NT, D]))\
                        .then_inc(S["res_loaded"], 16)

            def load_max(b, par, half):
                after(sp, "neg_copied", 2, b, half + 1)
                sp.dma_start(qst[par][ROWS:ROWS_MAX, HH * half:HH * (half + 1), :], neg_T[:, :])\
                    .then_inc(max_loaded[half], 16)

            def xt_d(b):
                return x[b].rearrange("(t p) d -> p t d", p=P)

            def mod_row(b):
                return mod_d[b]

            steps(sp, step)

            def load(k, r):
                if not isinstance(k, int) or k >= RING:
                    after(sp, "y_done", 1, k, 1 - RING)
                    after(sp, "idx_done", 1, k, 1 - RING)
                row = sp.value_load(t_row_i[0:1, bass.ds(k, 1)], min_val=0, max_val=SPARE)
                sp.dma_start(rows[r], rows_d[bass.ds(row, P), :]).then_inc(row_loaded[r], 16)

            sp.wait_ge(S["tab_early_done"], 1)
            for b in (NB - 4, NB - 3):
                after_scatter(sp, b, b % 2)
            for r in range(RING):
                load(r, r)
                if r == 2:
                    sp.wait_ge(S["st_ready"], SLOTS * NB)
                    sp.wait_ge(S["bias_stored"], 16)
                    sp.dma_start(b2p, b2_d).then_inc(S["bias_rows_loaded"], 16)
            for k in range(RING, 2 * RING):
                load(k, k % RING)
            for e in range(E):
                load(2 * RING + e, e)
                sp.wait_ge(S["base_i_done"], 1)
                row = sp.value_load(base_i[0:1, e:e + 1], min_val=0, max_val=SPARE - P)
                sp.dma_start(rows_d[bass.ds(row, P), :], pad[:, :]).then_inc(S["pads_stored"], 16)
            with sp.Fori(3, EARLY // RING) as n:
                for r in range(RING):
                    load(RING * n + r, r)

            sp.wait_ge(S["tab_done"], 1)
            for b in (NB - 2, NB - 1):
                after_scatter(sp, b, b % 2)
            sp.wait_ge(S["pads_stored"], 16 * E)
            sp.wait_ge(S["spare_stored"], 16)
            with sp.Fori(EARLY // RING, TILES // RING) as n:
                for r in range(RING):
                    load(RING * n + r, r)

        @block.gpsimd
        def _(pool):
            g = nc.gpsimd
            for m in (ident, ident_b):
                g.memset(m[:, :], 0.0).then_inc(S["ident_done"], 1)
            g.memset(causal[:, :], 0.0).then_inc(S["ident_done"], 1)
            g.memset(before[:, :], 1.0).then_inc(S["ident_done"], 1)
            g.memset(gate_w[:, :], 0.0).then_inc(S["gate_w_zero"], 1)
            pool.wait_ge(S["ident_done"], 4)
            for m in (ident, ident_b):
                g.affine_select(out=m[:, :], in_=m[:, :], compare_op=ALU.not_equal, fill=1.0, base=0,
                                pattern=[[-1, P]], channel_multiplier=1).then_inc(S["const_done"], 1)
            g.affine_select(out=causal[:, :], in_=causal[:, :], compare_op=ALU.is_ge, fill=NEG, base=0,
                            pattern=[[-1, P]], channel_multiplier=1).then_inc(S["const_done"], 1)
            g.affine_select(out=before[:, :], in_=before[:, :], compare_op=ALU.is_gt, fill=0.0, base=0,
                            pattern=[[1, P]], channel_multiplier=-1).then_inc(S["const_done"], 1)
            g.memset(ones_b[:, :], 1.0).then_inc(S["const_done"], 1)
            g.memset(ones3[:, :], 1.0).then_inc(S["const_done"], 1)
            g.memset(eps[:, :], EPS).then_inc(S["const_done"], 1)
            g.memset(half[:, :], -0.5).then_inc(S["const_done"], 1)
            g.iota(rank_of_e[:, :], pattern=[[-1, E]], base=E, channel_multiplier=0,
                   allow_small_or_imprecise_dtypes=True).then_inc(S["const_done"], 1)
            g.iota(base[:, :], pattern=[[CAP, E]], base=0, channel_multiplier=0,
                   allow_small_or_imprecise_dtypes=True).then_inc(S["const_done"], 1)
            g.iota(e_cap[:, :], pattern=[[CAP, E]], base=0, channel_multiplier=0,
                   allow_small_or_imprecise_dtypes=True).then_inc(S["const_done"], 1)
            g.iota(m_128[:, :], pattern=[[P, N // P]], base=0, channel_multiplier=0,
                   allow_small_or_imprecise_dtypes=True).then_inc(S["const_done"], 1)
            g.iota(t_iota[:, :], pattern=[[1, TILES]], base=0, channel_multiplier=0,
                   allow_small_or_imprecise_dtypes=True).then_inc(S["const_done"], 1)
            g.memset(low_e[:, :, :], 1.0).then_inc(S["ident_done"], 1)
            pool.wait_ge(S["ident_done"], 5)
            g.affine_select(out=low_e[:, :, :], in_=low_e[:, :, :], compare_op=ALU.is_ge, fill=0.0, base=0,
                            pattern=[[1, E], [-1, E]], channel_multiplier=0).then_inc(S["const_done"], 1)
            for i in range(2):
                g.memset(pack[i][:, :, IDX:RW], 0.0).then_inc(S["ident_done"], 1)
                pool.wait_ge(S["ident_done"], 6 + i)
                g.iota(pack[i][:, :, IDX:IDX + 1], pattern=[[P, NT], [0, 1]], base=(i - 2) * T, channel_multiplier=1,
                       allow_small_or_imprecise_dtypes=True).then_inc(S["const_done"], 1)
            g.memset(pad[:, :], 0.0).then_inc(S["ident_done"], 1)
            pool.wait_ge(S["ident_done"], 8)
            g.memset(pad[:, IDX:IDX + 1], NO_TOKEN).then_inc(S["pad_done"], 1)
            for i in range(2):
                g.memset(vaug[i][:, :, :, DH:DH + 1], 1.0).then_inc(S["vaug_ones"], 1)
            pool.wait_ge(S["const_done"], 16)

            def rstd(mv, var, r, add, done, b):
                g.tensor_tensor(var[:, :], mv[:, :, 1], eps[:, :], op=ALU.add).then_inc(S[add], 1)
                after(pool, add, 1, b, 1)
                g.tensor_tensor(r[:, :], var[:, :], half[:, :], op=ALU.pow).then_inc(S[done], 1)

            def split(b, i):
                after(pool, "qk_copied", 4, b, 2 * i + 2)
                g.tensor_tensor(qk_r[:, i, :], qk_f[:, i, :], qk_parts[:, i, 0, :], op=ALU.subtract)\
                    .then_inc(S["r1_done"], 1)

            def split_last(b, i):
                after(pool, "qm_done", 2, b, i + 1)
                g.tensor_tensor(qk_parts[:, i, 2, :], qk_r[:, i, :], qk_parts[:, i, 1, :], op=ALU.subtract)\
                    .then_inc(S["ql_done"], 1)

            def mask(b, pair):
                after(pool, "exp_done", SLOTS, b, 5 * (pair + 1))
                stand(pool)
                v = probs[pair // 2 % 2][:, 5 * (pair % 2):5 * (pair % 2) + 5, :]
                for blocks, n in ((v[:, 0:4:2, 0:P], (2, 1)),
                                  (v[:, 1:5:2, 0:2 * P].rearrange("p a (b n) -> p a b n", b=2), (2, 2)),
                                  (v[:, 4, :].rearrange("p (a n) -> p a n", a=2)[:, :, 0:P], (2, 1))):
                    pat = [[0, n[0]], [0, n[1]], [1, P]] if n[1] > 1 else [[0, n[0]], [1, P]]
                    last = g.affine_select(out=blocks, in_=blocks, compare_op=ALU.is_ge, fill=0.0, base=0,
                                           pattern=pat, channel_multiplier=-1)
                last.then_inc(S["masked"], 1)

            def store(k, r, n):
                after(pool, row_loaded[r], 16, n, 16)
                after(pool, out_stored[r], 16, n - 1, 16)
                stand(pool)
                g.tensor_copy(idx_u[:, r:r + 1], rows[r][:, IDX:IDX + 1]).then_inc(S["idx_done"], 1)
                pool.wait_ge(S["idx_done"], k + 1)
                pool.wait_ge(S["y_done"], k + 1)
                stand(pool)
                g.indirect_dma_start(
                    out=out.rearrange("b t d -> (b t) d"),
                    out_offset=bass.IndirectOffsetOnAxis(ap=idx_u[:, r:r + 1], axis=0),
                    in_=y_b[r], in_offset=None, bounds_check=N - 1, oob_is_err=False).then_inc(out_stored[r], 16)

            def scatter(b, par, t):
                if t == 0:
                    after(pool, "pos_u_done", 1, b, 1)
                    after(pool, "x1_done", 1, b, 1)
                    after(pool, "h2_done", 1, b, 1)
                    after(pool, "idx_moved", 1, b, 1)
                    stand(pool)
                g.indirect_dma_start(
                    out=rows_d, out_offset=bass.IndirectOffsetOnAxis(ap=pos_u[:, par, t:t + 1], axis=0),
                    in_=pack[par][:, t, :], in_offset=None, bounds_check=E * CAP - 1, oob_is_err=False)\
                    .then_inc(scattered[par], 16)

            def step(s, p, qkv, mx, soft, close):
                for q in range(SLOTS):
                    if (tile_of(s, q) or 0) >= 4:
                        store(tile_of(s, q) - 4, tile_of(s, q) - 4, 0)
                    if soft and q % 5 == 1 and q > 1:
                        mask(s - 2, q // 5 - 1)
                    if qkv and q == AT["rstd1"]:
                        after(pool, "ln1_mv", NT, s, NT)
                        after(pool, "xhat_done", NT, s - 1, NT)
                        rstd(mv1, var1, rstd1, "rstd1_add", "rstd1_done", s)
                    if close and q == AT["wpg"]:
                        b = s - 3
                        after(pool, "res_loaded", 48, b, 48)
                        after(pool, "proj_ready", 1, b - 1, 1)
                        g.tensor_tensor(wpg[:, :], wproj[:, :], modb[:, 1 - p, 0, :], op=ALU.mult)\
                            .then_inc(S["wpg_done"], 1)
                        after_scatter(pool, b - 2, 1 - p)
                        stand(pool)
                        col = pack[1 - p][:, :, IDX:IDX + 1]
                        g.tensor_scalar(col, col, float(2 * T), None, op0=ALU.add).then_inc(S["idx_moved"], 1)
                    if q in AT["scatter"] and (not isinstance(s, int) or s >= 4):
                        scatter(s - 4, p, AT["scatter"].index(q))
                    if qkv and q == AT["q_rest"]:
                        split(s, 0)
                    if qkv and q == AT["q_lo"]:
                        split_last(s, 0)
                    if qkv and q == AT["k_rest"]:
                        split(s, 1)
                    if qkv and q == AT["k_lo"]:
                        split_last(s, 1)
                    if close and q == AT["rstd2"]:
                        after(pool, "ln2_mv", NT, s - 3, NT)
                        after(pool, "xhat2_done", NT, s - 4, NT)
                        rstd(mv2, var2, rstd2, "rstd2_add", "rstd2_done", s - 3)
                    if close and q == AT["h2"]:
                        b = s - 3
                        mb = modb[:, 1 - p, :, :]
                        after(pool, "xhat2_done", NT, b, NT)
                        g.tensor_tensor(h2m[:, :, :], xhat2[:, :, :],
                                        mb[:, 1, :].unsqueeze(1).to_broadcast([P, NT, D]), op=ALU.mult)\
                            .then_inc(S["h2m_done"], 1)
                        after(pool, "h2m_done", 1, b, 1)
                        g.tensor_tensor(pack[1 - p][:, :, 0:D], h2m[:, :, :],
                                        mb[:, 2, :].unsqueeze(1).to_broadcast([P, NT, D]), op=ALU.add)\
                            .then_inc(S["h2_done"], 1)
                if soft:
                    mask(s - 2, 7)

            steps(pool, step)
            for t in range(NT):
                scatter(NB - 1, (NB - 1) % 2, t)

            for k in range(RING - 4, RING):
                store(k, k, 0)
            with pool.Fori(1, TILES // RING) as n:
                for r in range(RING):
                    store(RING * n + r, r, n)
            for r in range(RING):
                pool.wait_ge(out_stored[r], 16 * (TILES // RING))

        @block.scalar
        def _(act):
            a = nc.scalar
            act.wait_ge(S["c_loaded"], 32)
            a.activation(c_exp[:, :], c_in[:, :], ACT.Exp, scale=-1.0).then_inc(S["c_exp_done"], 1)
            act.wait_ge(S["modT_done"], 2)

            def copy_out(dst, src, name):
                a.activation(dst, src, ACT.Copy).then_inc(S[name], 1)

            def gelu(k, r):
                act.wait_ge(S["hB_ready"], k + 1)
                if not (isinstance(k, int) and k < 2):
                    after(act, "yB_ready", 1, k, -1)
                if not isinstance(k, int):
                    stand(act)
                for f in range(FC):
                    last = a.activation(hgT[r][:, f * P:(f + 1) * P], h_ps[:, r, f * P:(f + 1) * P], ACT.Gelu,
                                        bias=w1_b[r][:, DFF + f:DFF + f + 1])
                last.then_inc(S["gelu_done"], 1)

            def exp(b, q):
                gr = q // GROUP_SLOTS
                if q % GROUP_SLOTS == 0:
                    after(act, "pv_ready", NG, b, gr - 1)
                after(act, "st_ready", SLOTS, b, q + 1)
                a.activation(probs[gr % 2][:, q % GROUP_SLOTS, :], st_ps[:, q % 2, :], ACT.Exp, scale=SCALE)\
                    .then_inc(S["exp_done"], 1)

            def pv_copy(b, gr):
                after(act, "pv_ready", NG, b, gr + 1)
                after(act, "pvT_ready", NG, b, gr - 1)
                copy_out(pvs[:, gr % 2, :], pv_ps[:, :], "pv_copied")

            def step(s, p, qkv, mx, soft, close):
                for q in range(SLOTS):
                    if (tile_of(s, q) or 0) >= 2:
                        gelu(tile_of(s, q) - 2, tile_of(s, q) % 2)
                    if close and q == AT["pv_copy"]:
                        pv_copy(s - 3, 2)
                    if close and q == GROUP_SLOTS + AT["pv_copy"]:
                        pv_copy(s - 3, 3)
                    if soft and q == 2 * GROUP_SLOTS + AT["pv_copy"]:
                        pv_copy(s - 2, 0)
                    if soft and q == 3 * GROUP_SLOTS + AT["pv_copy"]:
                        pv_copy(s - 2, 1)
                    if qkv and q == AT["hT"]:
                        after(act, "xT_ready", 1, s, 1)
                        after(act, "v_ready", 1, s - 2, 1)
                        a.activation(hT[:, p, :], m0_ps[:, :], ACT.Identity, bias=modT[:, 0, bass.ds(s, 1)],
                                     scale=modT[:, 1, bass.ds(s, 1)]).then_inc(S["hT_done"], 1)
                    for i, n in enumerate("qk"):
                        if qkv and q == AT[n + "_f"]:
                            after(act, "qk_ready", 2, s, i + 1)
                            copy_out(qk_f[:, i, :], m0_ps[:, :], "qk_copied")
                        if qkv and q == AT[n + "_hi"]:
                            after(act, parts_stored[i], 16 * PARTS, s - 1, 16 * PARTS)
                            copy_out(qk_parts[:, i, 0, :], m0_ps[:, :], "qk_copied")
                        if qkv and q == AT[n + "_mid"]:
                            after(act, "r1_done", 2, s, i + 1)
                            after(act, parts_stored[i], 16 * PARTS, s - 1, 16 * PARTS)
                            copy_out(qk_parts[:, i, 1, :], qk_r[:, i, :], "qm_done")
                    if mx and q == AT["v_copy"]:
                        b = s - 1
                        after(act, "v_ready", 1, b, 1)
                        after(act, "pv_ready", NG, b - 2, NG)
                        a.activation(vaug[1 - p][:, :, :, 0:DH],
                                     m1_ps[:, :].rearrange("p (t h d) -> p t h d", t=NT, h=H), ACT.Copy)\
                            .then_inc(S["v_copied"], 1)
                    for half, there, b in ((0, mx, s - 1), (1, soft, s - 2)):
                        if there and q == AT["neg_copy"][half]:
                            after(act, "maxT_ready", 2, b, half + 1)
                            after(act, max_loaded[1 - half], 16, b - (1 - half), 16)
                            copy_out(neg_T[:, :], m1_ps[0:PARTS * HH, :].bitcast(BF16)[:, 0:T], "neg_copied")
                    if close and q == AT["aT_copy"]:
                        after(act, "aT_ready", 1, s - 3, 1)
                        after(act, "proj_ready", 1, s - 4, 1)
                        copy_out(attnT[:, :], m0_ps[:, :], "aT_copied")
                    if close and q == AT["h2T_copy"]:
                        after(act, "h2T_ready", 1, s - 3, 1)
                        after(act, "lgT_ready", 1, s - 4, 1)
                        copy_out(h2T[:, :], m0_ps[:, :], "h2T_copied")
                    if close and q == AT["logit_copy"]:
                        after(act, "lgT_ready", 1, s - 3, 1)
                        after(act, "lg_ready", 1, s - 4, 1)
                        copy_out(logitT[:, :], m0_ps[:, 0:P], "lgT_copied")
                    if soft:
                        exp(s - 2, q)

            steps(act, step)

            for k in range(RING - 2, RING):
                gelu(k, k % 2)
            with act.Fori(RING // 2, TILES // 2) as n:
                gelu(2 * n, 0)
                gelu(2 * n + 1, 1)

        @block.tensor
        def _(pe):
            t_ = nc.tensor

            def mm(o, l, r, start=True, stop=True):
                return t_.matmul(o, l, r, start=start, stop=stop, skip_group_check=True)

            pe.wait_ge(S["const_done"], 16)
            pe.wait_ge(S["silu_done"], 1)
            t_.transpose(m0_ps[:, 0:NB], c_silu[:, :], ident[0:NB, 0:NB]).then_inc(S["cT_ready"], 1)
            pe.wait_ge(S["cT_done"], 1)
            mm(m0_ps[0:NB, :], c_T[:, :], wmod_sb[:, 0:BANK])
            mm(m1_ps[0:NB, 0:6 * D - BANK], c_T[:, :], wmod_sb[:, BANK:6 * D]).then_inc(S["modps_ready"], 1)
            for i in range(6):
                last = mm(pv_ps[:, i * NB:(i + 1) * NB], wmod_sb[:, i * D:(i + 1) * D], c_T[:, :])
            last.then_inc(S["modT_ready"], 1)
            pe.wait_ge(S["modn_done"], 2)
            pe.wait_ge(S["modT_done"], 2)
            pe.wait_ge(S["b1_loaded"], 16)
            t_.transpose(m1_ps[:, 0:E * FC], b1_in[:, :], ident[0:E * FC, 0:E * FC]).then_inc(S["b1T_ready"], 1)
            pe.wait_ge(S["w_loaded"], 64)
            pe.wait_ge(S["stacks_ones"], 32)
            pe.wait_ge(S["vaug_ones"], 2)
            pe.wait_ge(S["pv_zero"], 1)

            def load_expert(k):
                return pe.value_load(t_e_i[0:1, bass.ds(k, 1)], min_val=0, max_val=E - 1)

            def turn(k, rb, n):
                r = rb % 2
                after(pe, row_loaded[rb], 16, n, 16)
                if isinstance(k, int) and k < 2:
                    pe.wait_ge(S["sn_read"], 2 * SLOTS * NB)
                    pe.wait_ge(S["pv_copied"], NG * NB)
                else:
                    after(pe, "tB_copied", 1, k, -1)
                t_.transpose(hT_ps[r][:, 0:P], rows[rb][:, 0:D], ident[:, :]).then_inc(S["tB_ready"], 1)

            def up(k, r):
                if not (isinstance(k, int) and k < 2):
                    after(pe, "gelu_done", 1, k, -1)
                after(pe, "tB_copied", 1, k, 1)
                for f in range(FC):
                    last = mm(h_ps[:, r, f * P:(f + 1) * P], w1_b[r][:, f * P:(f + 1) * P], h2T_b[r])
                last.then_inc(S["hB_ready"], 1)

            def down(k, r):
                if isinstance(k, int) and k == 0:
                    pe.wait_ge(S["tab_early_done"], 1)
                    pe.wait_ge(S["wffn_loaded"], 32)
                    pe.wait_ge(S["bias_rows_loaded"], 16)
                e = load_expert(k)
                if isinstance(k, int) and k < 2:
                    pe.wait_ge(S["exp_done"], SLOTS * NB)
                else:
                    after(pe, "ygb_done", 1, k, -1)
                mm(y_ps[:, r, 0:D], ones3[:, :], b2p[:, bass.ds(e * D, D)], stop=False)
                after(pe, "gelu_done", 1, k, 1)
                for f in range(FC):
                    last = mm(y_ps[:, r, 0:D], hgT[r][:, f * P:(f + 1) * P],
                              w2[:, bass.ds(e * (FC * D) + f * D, D)], start=False, stop=f == FC - 1)
                last.then_inc(S["yB_ready"], 1)

            def tile(k, rb, n):
                turn(k, rb, n)
                if not (isinstance(k, int) and k < 2):
                    up(k - 2, rb % 2)
                if not (isinstance(k, int) and k < 3):
                    down(k - 3, (rb + 1) % 2)

            def sn_unit(b, par, u):
                gr, pair, k = u // GROUP_SLOTS, u // 5, u % 5
                if u % GROUP_SLOTS == 0:
                    after(pe, stack_loaded[gr], 16 * STACK_DMAS, b, 16 * STACK_DMAS)
                after(pe, "sn_read", 2 * SLOTS, b, 2 * max(u - 2, 0))
                o = sn_ps[:, u % 3, :]
                parts = {0: [(0, 3, 0)], 1: [(0, 0, 0), (0, 2, P)], 2: [(1, 3, 0)], 3: [(1, 0, 0), (1, 2, P)],
                         4: [(0, 1, 0), (1, 1, 2 * P)]}[k]
                for hd, t, col in parts:
                    h = 2 * pair + hd
                    mm(o[:, col:col + (t + 1) * P], qst[par][0:ROWS, h, t * P:(t + 1) * P],
                       kst[par][0:ROWS, h, 0:(t + 1) * P], stop=False)
                    last = mm(o[:, col + t * P:col + (t + 1) * P], ident_b[:, :], causal[:, :], start=False)
                last.then_inc(S["sn_ready"], 1)

            def st_unit(b, par, u):
                pair, k = u // 5, u % 5
                if u % (SLOTS // 2) == 0:
                    after(pe, max_loaded[u // (SLOTS // 2)], 16, b, 16)
                after(pe, "exp_done", SLOTS, b, u - 1)
                o = st_ps[:, u % 2, :]
                parts = {0: [(0, 0, 0)], 1: [(0, 3, 0), (0, 1, P)], 2: [(1, 0, 0)], 3: [(1, 3, 0), (1, 1, P)],
                         4: [(0, 2, 0), (1, 2, 2 * P)]}[k]
                for hd, t, col in parts:
                    h = 2 * pair + hd
                    last = mm(o[:, col:col + T - t * P], kst[par][0:ROWS_MAX, h, t * P:(t + 1) * P],
                              qst[par][0:ROWS_MAX, h, t * P:T])
                last.then_inc(S["st_ready"], 1)

            def pv(b, par, gr, j):
                if j == 0:
                    after(pe, "masked", H // 2, b, 2 * gr + 2)
                    after(pe, "pv_copied", NG, b, gr)
                    after(pe, "v_copied", 1, b, 1)
                for hd in range(4):
                    base_u, X = 5 * (hd // 2), hd % 2
                    u, col = {0: (2 * X, 0), 1: (2 * X + 1, P), 2: (4, 2 * P * X), 3: (2 * X + 1, 0)}[j]
                    last = mm(pv_ps[32 * hd:32 * hd + DH + 1, j * P:T], vaug[par][:, j, 4 * gr + hd, :],
                              probs[gr % 2][:, base_u + u, col:col + T - j * P], start=j == 0, stop=j == NT - 1)
                if j == NT - 1:
                    last.then_inc(S["pv_ready"], 1)

            def pv_transpose(b, gr):
                after(pe, "pv_copied", NG, b, gr + 1)
                for t in range(NT):
                    last = t_.transpose(m1_ps[:, t * P:(t + 1) * P], pvs[:, gr % 2, t * P:(t + 1) * P], ident[:, :])
                last.then_inc(S["pvT_ready"], 1)

            def four_transposes(ps, src, name):
                for t in range(NT):
                    last = t_.transpose(ps[:, t * P:(t + 1) * P], src[:, t, :], ident[:, :])
                last.then_inc(S[name], 1)

            def step(s, p, qkv, mx, soft, close):
                for q in range(SLOTS):
                    later = not isinstance(s, int)
                    if tile_of(s, q) is not None:
                        tile(tile_of(s, q), tile_of(s, q), 0)
                    if close and q == AT["pv_T"]:
                        after(pe, "pvn_done", NG, s - 3, 2)
                        pv_transpose(s - 3, 2)
                    if close and q == GROUP_SLOTS + AT["pv_T"]:
                        if later or s - 2 < NB:
                            after(pe, "neg_copied", 2, s - 2, 2)
                        after(pe, "pvn_done", NG, s - 3, 3)
                        pv_transpose(s - 3, 3)
                    if soft and q == 2 * GROUP_SLOTS + AT["pv_T"]:
                        if later or s - 1 < NB:
                            after(pe, "v_copied", 1, s - 1, 1)
                        after(pe, "neg_copied", 2, s - 2, 2)
                        after(pe, "pvn_done", NG, s - 3, NG)
                        pv_transpose(s - 2, 0)
                    if soft and q == 3 * GROUP_SLOTS + AT["pv_T"]:
                        if later or s - 1 < NB:
                            after(pe, "neg_copied", 2, s - 1, 1)
                        after(pe, "pvn_done", NG, s - 2, 1)
                        pv_transpose(s - 2, 1)
                    if qkv and q == AT["xT"]:
                        after(pe, "xhat_done", NT, s, NT)
                        after(pe, "qk_copied", 4, s - 1, 4)
                        after(pe, "base_done", 1, s - 4, 1)
                        four_transposes(m0_ps, xhat, "xT_ready")
                    for i, n in enumerate("qk"):
                        if qkv and q == AT[n]:
                            after(pe, "hT_done", 1, s, 1)
                            after(pe, "qk_copied", 4, s, 2 * i)
                            mm(m0_ps[:, :], wqkv[:, i * D:(i + 1) * D], hT[:, p, :]).then_inc(S["qk_ready"], 1)
                    if mx and q == AT["v"]:
                        after(pe, "hT_done", 1, s - 1, 1)
                        after(pe, "neg_copied", 2, s - 2, 2)
                        after(pe, "pvn_done", NG, s - 3, NG)
                        for t in range(NT):
                            last = mm(m1_ps[:, t * P:(t + 1) * P], hT[:, 1 - p, t * P:(t + 1) * P],
                                      wqkv[:, 2 * D:3 * D])
                        last.then_inc(S["v_ready"], 1)
                    for half, there, b in ((0, mx, s - 1), (1, soft, s - 2)):
                        if there and q == AT["max_T"][half]:
                            if half == 0:
                                after(pe, "v_copied", 1, b, 1)
                                after(pe, "pvn_done", NG, b - 1, 1)
                            else:
                                after(pe, "neg_copied", 2, b, 1)
                                after(pe, "pvn_done", NG, b - 1, 3)
                            after(pe, "neg_done", 2, b, half + 1)
                            for t in range(NT):
                                last = t_.transpose(
                                    m1_ps[0:PARTS * HH, :].bitcast(BF16)[:, t * P:(t + 1) * P],
                                    neg_parts[:, half, t, :, :].rearrange("p i h -> p (i h)"), ident_b[:, :])
                            last.then_inc(S["maxT_ready"], 1)
                    if close:
                        b = s - 3
                        if q == AT["aT"]:
                            after(pe, "pvn_done", NG, b, NG)
                            if qkv:
                                after(pe, "qk_copied", 4, s, 4)
                            else:
                                after(pe, "base_done", 1, b - 1, 1)
                            four_transposes(m0_ps, attn[:, :, :, :].rearrange("p t h d -> p t (h d)"), "aT_ready")
                        if q == AT["proj"]:
                            after(pe, "aT_copied", 1, b, 1)
                            after(pe, "wpg_done", 1, b, 1)
                            for t in range(NT):
                                last = mm(m0_ps[:, t * P:(t + 1) * P], attnT[:, t * P:(t + 1) * P], wpg[:, :])
                            last.then_inc(S["proj_ready"], 1)
                        if q == AT["h2T"]:
                            after(pe, "x1_done", 1, b, 1)
                            after(pe, "h2_done", 1, b, 1)
                            four_transposes(m0_ps, pack[1 - p][:, :, 0:D], "h2T_ready")
                        if q == AT["logit"]:
                            after(pe, "h2T_copied", 1, b, 1)
                            for t in range(NT):
                                last = mm(m0_ps[32 * t:32 * t + 32, 0:P], gate_w[:, :], h2T[:, t * P:(t + 1) * P])
                            last.then_inc(S["lgT_ready"], 1)
                        if q == AT["logit_T"]:
                            after(pe, "lgT_copied", 1, b, 1)
                            t_.transpose(m0_ps[:, 0:P], logitT[:, :], ident[:, :]).then_inc(S["lg_ready"], 1)
                        if q == AT["rank"]:
                            after(pe, "onehot_done", 1, b, 1)
                            after(pe, "lg_read", 1, b, 1)
                            for t in range(NT + 1):
                                o = m0_ps[:, t * E:(t + 1) * E]
                                for u in range(min(t, NT)):
                                    last = mm(o, ones_b[:, :], onehot[:, u, :], start=u == 0, stop=u == NT - 1)
                                if t < NT:
                                    last = mm(o, before[:, :], onehot[:, t, :], start=t == 0)
                            last.then_inc(S["rank_ready"], 1)
                    if mx:
                        sn_unit(s - 1, 1 - p, q)
                    if soft:
                        st_unit(s - 2, p, q)
                    if q % GROUP_SLOTS in AT["pv"]:
                        j = AT["pv"].index(q % GROUP_SLOTS)
                        gr = q // GROUP_SLOTS - 1
                        if gr < 0 and close:
                            pv(s - 3, 1 - p, 3, j)
                        if gr >= 0 and soft:
                            pv(s - 2, p, gr, j)

            steps(pe, step)

            with pe.Fori(1, EARLY // RING) as n:
                for r in range(RING):
                    tile(RING * n + r, r, n)
            pe.wait_ge(S["tab_done"], 1)
            with pe.Fori(EARLY // RING, TILES // RING) as n:
                for r in range(RING):
                    tile(RING * n + r, r, n)
            for k in range(TILES, TILES + 3):
                if k < TILES + 2:
                    up(k - 2, k % 2)
                down(k - 3, (k + 1) % 2)

        @block.vector
        def _(dve):
            v = nc.vector

            dve.wait_ge(S["c_exp_done"], 1)
            dve.wait_ge(S["c_loaded"], 32)
            v.tensor_scalar(c_exp[:, :], c_exp[:, :], 1.0, None, op0=ALU.add).then_inc(S["setup_dve"], 1)
            dve.wait_ge(S["setup_dve"], 1)
            v.reciprocal(c_exp[:, :], c_exp[:, :]).then_inc(S["setup_dve"], 1)
            dve.wait_ge(S["setup_dve"], 2)
            v.tensor_tensor(c_silu[:, :], c_in[:, :], c_exp[:, :], op=ALU.mult).then_inc(S["silu_done"], 1)
            dve.wait_ge(S["cT_ready"], 1)
            v.tensor_copy(c_T[:, :], m0_ps[:, 0:NB]).then_inc(S["cT_done"], 1)
            dve.wait_ge(S["modps_ready"], 1)
            flat = mod_n[:, :, :].rearrange("b s d -> b (s d)")
            v.tensor_copy(flat[:, 0:BANK], m0_ps[0:NB, :]).then_inc(S["modn_done"], 1)
            v.tensor_copy(flat[:, BANK:6 * D], m1_ps[0:NB, 0:6 * D - BANK]).then_inc(S["modn_done"], 1)
            dve.wait_ge(S["modT_ready"], 1)
            v.tensor_copy(modT[:, :, :].rearrange("p s b -> p (s b)"), pv_ps[:, 0:6 * NB])\
                .then_inc(S["modT_done"], 1)
            dve.wait_ge(S["modT_done"], 1)
            v.tensor_scalar(modT[:, 1, :], modT[:, 1, :], 1.0, None, op0=ALU.add).then_inc(S["modT_done"], 1)
            v.memset(pv_ps[:, :], 0.0).then_inc(S["pv_zero"], 1)
            dve.wait_ge(S["const_done"], 16)
            dve.wait_ge(S["w_loaded"], 64)

            def setup_rest():
                dve.wait_ge(S["modn_done"], 2)
                n0 = 2
                for src, dst in ((2, 0), (5, 3)):
                    v.tensor_scalar(mod_t0[:, :], mod_n[:, src, :], 0.0, 2.0, op0=ALU.is_ge, op1=ALU.mult)\
                        .then_inc(S["setup_dve"], 1)
                    v.scalar_tensor_tensor(out=mod_t1[:, :], in0=mod_n[:, src, :], scalar=-1.0, in1=mod_n[:, src, :],
                                           op0=ALU.mult, op1=ALU.max).then_inc(S["setup_dve"], 1)
                    n0 += 2
                    dve.wait_ge(S["setup_dve"], n0)
                    v.tensor_scalar(mod_t1[:, :], mod_t1[:, :], 0.25, None, op0=ALU.max).then_inc(S["setup_dve"], 1)
                    n0 += 1
                    dve.wait_ge(S["setup_dve"], n0)
                    v.scalar_tensor_tensor(out=mod_out[:, dst, :], in0=mod_t0[:, :], scalar=-1.0, in1=mod_t1[:, :],
                                           op0=ALU.add, op1=ALU.mult).then_inc(S["setup_dve"], 1)
                    n0 += 1
                    dve.wait_ge(S["setup_dve"], n0)
                v.tensor_scalar(mod_out[:, 1, :], mod_n[:, 4, :], 1.0, None, op0=ALU.add).then_inc(S["setup_dve"], 1)
                v.tensor_copy(mod_out[:, 2, :], mod_n[:, 3, :]).then_inc(S["setup_dve"], 1)
                dve.wait_ge(S["setup_dve"], n0 + 2)
                v.tensor_copy(mod_t0[:, :], mod_out[:, 2, :]).then_inc(S["modout_done"], 1)
                dve.wait_ge(S["b1T_ready"], 1)
                v.tensor_copy(w1[:, :].rearrange("p (e f) -> p e f", e=E)[:, :, DFF:UP],
                              m1_ps[:, 0:E * FC].rearrange("p (e c) -> p e c", e=E)).then_inc(S["b1_placed"], 1)
                dve.wait_ge(S["bias_loaded"], 16)
                v.tensor_copy(bias_parts[:, 0, :], bias_in[:, :]).then_inc(S["bias_step"], 1)
                dve.wait_ge(S["bias_step"], 1)
                v.tensor_tensor(bias_r[:, :], bias_in[:, :], bias_parts[:, 0, :], op=ALU.subtract)\
                    .then_inc(S["bias_step"], 1)
                dve.wait_ge(S["bias_step"], 2)
                v.tensor_copy(bias_parts[:, 1, :], bias_r[:, :]).then_inc(S["bias_step"], 1)
                dve.wait_ge(S["bias_step"], 3)
                v.tensor_tensor(bias_parts[:, 2, :], bias_r[:, :], bias_parts[:, 1, :], op=ALU.subtract)\
                    .then_inc(S["bias_step"], 2)

            n_links = [0]

            def link(ins):
                n_links[0] += 1
                ins.then_inc(S["tab_step"], 1)
                dve.wait_ge(S["tab_step"], n_links[0])

            def count_full():
                link(v.tensor_tensor(cnt[:, :], base[0:1, :], e_cap[:, :], op=ALU.subtract))
                link(v.tensor_tensor(nt_cmp[:, :, :], cnt[:, :].unsqueeze(2).to_broadcast([1, E, N // P]),
                                     m_128[:, :].unsqueeze(1).to_broadcast([1, E, N // P]), op=ALU.is_ge))
                link(v.tensor_reduce(nt_e[:, :], nt_cmp[:, :, :], axis=AX_X, op=ALU.add))
                link(v.tensor_scalar(nt_e[:, :], nt_e[:, :], -1.0, None, op0=ALU.add))

            def take_early():
                link(v.memset(taken[:, E:E + 1], 0.0))
                link(v.tensor_tensor(taken[:, 0:E], nt_e[:, :], nt_end[:, :], op=ALU.subtract))
                link(v.tensor_scalar(taken[:, 0:E], taken[:, 0:E], float(EARLY), None, op0=ALU.add))
                link(v.scalar_tensor_tensor(out=taken[:, 0:E], in0=taken[:, 0:E], scalar=0.0, in1=nt_e[:, :],
                                            op0=ALU.max, op1=ALU.min))

            def count_all():
                link(v.tensor_tensor(cnt[:, :], base[0:1, :], e_cap[:, :], op=ALU.subtract))
                link(v.tensor_tensor(nt_cmp[:, :, :], cnt[:, :].unsqueeze(2).to_broadcast([1, E, N // P]),
                                     m_128[:, :].unsqueeze(1).to_broadcast([1, E, N // P]), op=ALU.is_gt))
                link(v.tensor_reduce(nt_e[:, :], nt_cmp[:, :, :], axis=AX_X, op=ALU.add))

            def count_rest():
                link(v.tensor_tensor(nt_rest[:, :], nt_e[:, :], taken[:, 0:E], op=ALU.subtract))
                link(v.tensor_tensor(nt_step[:, :], nt_e[:, :], taken[:, 1:E + 1], op=ALU.subtract))

            def end_tiles(per_e):
                link(v.tensor_tensor(nt_m[:, :, :], low_e[:, :, :], per_e[:, :].unsqueeze(1).to_broadcast([1, E, E]),
                                     op=ALU.mult))
                link(v.tensor_reduce(nt_end[:, :], nt_m[:, :, :], axis=AX_X, op=ALU.add))

            def list_tiles(n, step_e):
                link(v.tensor_tensor(t_ge[:, 0:n, :], t_iota[:, 0:n].unsqueeze(2).to_broadcast([1, n, E]),
                                     nt_end[:, :].unsqueeze(1).to_broadcast([1, n, E]), op=ALU.is_ge))
                link(v.tensor_tensor(t_gn[:, 0:n, :], t_ge[:, 0:n, :], step_e[:, :].unsqueeze(1).to_broadcast([1, n, E]),
                                     op=ALU.mult))
                link(v.tensor_reduce(t_e[:, 0:n], t_ge[:, 0:n, :], axis=AX_X, op=ALU.add))
                link(v.tensor_reduce(t_b[:, 0:n], t_gn[:, 0:n, :], axis=AX_X, op=ALU.add))

            def place_tiles(lo, n, first_tile, done):
                link(v.tensor_tensor(t_row[:, 0:n], t_iota[:, 0:n], t_b[:, 0:n], op=ALU.subtract))
                if first_tile is not None:
                    link(v.tensor_scalar(t_row[:, 0:n], t_row[:, 0:n], first_tile, None, op0=ALU.add))
                link(v.tensor_scalar(t_row[:, 0:n], t_row[:, 0:n], float(P), None, op0=ALU.mult))
                link(v.scalar_tensor_tensor(out=t_row1[:, 0:n], in0=t_e[:, 0:n], scalar=float(CAP), in1=t_row[:, 0:n],
                                            op0=ALU.mult, op1=ALU.add))
                link(v.tensor_scalar(t_row_i[:, lo:lo + n], t_row1[:, 0:n], float(SPARE), None, op0=ALU.min))
                v.tensor_scalar(t_e_i[:, lo:lo + n], t_e[:, 0:n], float(E - 1), None, op0=ALU.min)\
                    .then_inc(S[done], 1)

            def early_table():
                dve.wait_ge(S["base_done"], NB - 2)
                dve.wait_ge(S["ql_done"], 2 * NB)
                dve.wait_ge(S["v_ready"], NB)
                count_full()
                end_tiles(nt_e)
                list_tiles(EARLY, nt_e)
                take_early()
                place_tiles(0, EARLY, None, "tab_early_done")

            def tile_in(k, r):
                e = dve.value_load(t_e_i[0:1, bass.ds(k, 1)], min_val=0, max_val=E - 1)
                if not (isinstance(k, int) and k < 2):
                    after(dve, "hB_ready", 1, k, -1)
                    after(dve, "gelu_done", 1, k, -1)
                stand(dve)
                v.tensor_copy(w1_b[r], w1[:, bass.ds(e * UP, UP)]).then_inc(S["w1_copied"], 1)
                dve.wait_ge(S["tB_ready"], k + 1)
                dve.wait_ge(S["w1_copied"], k + 1)
                v.tensor_copy(h2T_b[r], hT_ps[r][:, 0:P]).then_inc(S["tB_copied"], 1)

            def tile_close(k, rb, n):
                r = rb % 2
                dve.wait_ge(S["yB_ready"], k + 1)
                after(dve, row_loaded[rb], 16, n, 16)
                v.tensor_tensor(ygb[r], y_ps[:, r, 0:D], rows[rb][:, 2 * D:3 * D], op=ALU.mult)\
                    .then_inc(S["ygb_done"], 1)
                dve.wait_ge(S["ygb_done"], k + 1)
                if not (isinstance(n, int) and n == 0):
                    after(dve, out_stored[rb], 16, n - 1, 16)
                v.tensor_tensor(y_b[rb], ygb[r], rows[rb][:, D:2 * D], op=ALU.add).then_inc(S["y_done"], 1)

            def tile(k, rb, n, n3):
                if isinstance(k, int) and k == 0:
                    dve.wait_ge(S["tab_early_done"], 1)
                    dve.wait_ge(S["wffn_loaded"], 32)
                    dve.wait_ge(S["b1_placed"], 1)
                    dve.wait_ge(S["st_ready"], SLOTS * NB)
                if isinstance(k, int) and k == EARLY:
                    dve.wait_ge(S["tab_done"], 1)
                tile_in(k, rb % 2)
                if not (isinstance(k, int) and k < 3):
                    tile_close(k - 3, (rb - 3) % RING, n3)

            def layer_stats(src, tiles, stats, stat):
                for t in tiles:
                    v.bn_stats(stats[:, t, :], src(t)).then_inc(S[stat], 1)

            def layer_mv(stats, mv, stat, mvd, b):
                after(dve, stat, NT, b, NT)
                stand(dve)
                for t in range(NT):
                    v.bn_aggr(mv[:, t, :], stats[:, t, :]).then_inc(S[mvd], 1)

            def normalise(dst, src, tiles, mv, r, name):
                for t in tiles:
                    v.tensor_scalar(dst[:, t, :], src(t), mv[:, t, 0:1], r[:, t:t + 1],
                                    op0=ALU.subtract, op1=ALU.mult).then_inc(S[name], 1)

            def divide(b, gr, i):
                m = m1_ps[:, :].rearrange("p (t h d) -> p t h d", t=NT, h=4)
                if i == 0:
                    after(dve, "pvT_ready", NG, b, gr + 1)
                    v.reciprocal(rsum[:, :, :], m[:, :, :, DH]).then_inc(S["rsum_done"], 1)
                if i == 1:
                    after(dve, "rsum_done", NG, b, gr + 1)
                    if gr == 0:
                        after(dve, "aT_ready", 1, b - 1, 1)
                    v.tensor_tensor(attn[:, :, 4 * gr:4 * gr + 4, :], m[:, :, :, 0:DH],
                                    rsum[:, :, :].unsqueeze(3).to_broadcast([P, NT, 4, DH]), op=ALU.mult)\
                        .then_inc(S["pvn_done"], 1)

            def row_maxima(b, half):
                after(dve, "sn_read", 2 * SLOTS, b, SLOTS * (half + 1))
                by_head = rmax[:, :, HH * half:HH * (half + 1)].rearrange("p t (a x) -> p t a x", x=2)
                bm = bmax[:, 4 * half:4 * half + 4, :, :]
                v.tensor_reduce(by_head[:, 3, :, :], bm[:, :, 0:4:2, :], axis=AX_X, op=ALU.max)\
                    .then_inc(S["rmax_done"], 1)
                v.tensor_reduce(by_head[:, 2, :, :], bm[:, :, 1:5:2, 1:4], axis=AX_X, op=ALU.max)\
                    .then_inc(S["rmax_done"], 1)
                v.tensor_reduce(by_head[:, 1, :, :], bm[:, :, 4, :].rearrange("p a (x k) -> p a x k", x=2),
                                axis=AX_X, op=ALU.max).then_inc(S["rmax_done"], 1)
                v.tensor_copy(by_head[:, 0, :, :], bm[:, :, 1:5:2, 0]).then_inc(S["rmax_done"], 1)

            def negate(b, half, i):
                m, r, parts = rmax[:, :, HH * half:HH * (half + 1)], neg_r[:, half, :, :], neg_parts[:, half, :, :, :]
                if i == 0:
                    after(dve, "rmax_done", 8, b, 4 * half + 4)
                    after(dve, "maxT_ready", 2, b - 1, half + 1)
                    v.tensor_scalar(parts[:, :, 0, :], m, -1.0, None, op0=ALU.mult).then_inc(S["neg_hi"], 1)
                if i == 1:
                    after(dve, "neg_hi", 2, b, half + 1)
                    v.scalar_tensor_tensor(out=r, in0=m, scalar=-1.0, in1=parts[:, :, 0, :],
                                           op0=ALU.mult, op1=ALU.subtract).then_inc(S["neg_rest"], 1)
                if i == 2:
                    after(dve, "neg_rest", 2, b, half + 1)
                    v.tensor_copy(parts[:, :, 1, :], r).then_inc(S["neg_mid"], 1)
                if i == 3:
                    after(dve, "neg_mid", 2, b, half + 1)
                    v.tensor_tensor(parts[:, :, 2, :], r, parts[:, :, 1, :], op=ALU.subtract)\
                        .then_inc(S["neg_done"], 1)

            def choose(b, i):
                ranks = rank_of_e[:, :].unsqueeze(1).to_broadcast([P, NT, E])
                if i == 0:
                    after(dve, "lg_ready", 1, b, 1)
                    m = m0_ps[:, 0:P].rearrange("p (t e) -> p t e", t=NT)[:, :, 0:E]
                    v.tensor_tensor(logit[:, :, :], m, gate_bias[:, :].unsqueeze(1).to_broadcast([P, NT, E]),
                                    op=ALU.add).then_inc(S["lg_read"], 1)
                if i == 1:
                    after(dve, "lg_read", 1, b, 1)
                    v.tensor_reduce(lmax[:, :], logit[:, :, :], axis=AX_X, op=ALU.max).then_inc(S["lmax_done"], 1)
                if i == 2:
                    after(dve, "lmax_done", 1, b, 1)
                    v.tensor_tensor(first[:, :, :], logit[:, :, :], lmax[:, :].unsqueeze(2).to_broadcast([P, NT, E]),
                                    op=ALU.is_ge).then_inc(S["first_done"], 1)
                if i == 3:
                    after(dve, "first_done", 2, b, 1)
                    v.tensor_tensor(first[:, :, :], first[:, :, :], ranks, op=ALU.mult).then_inc(S["first_done"], 1)
                if i == 4:
                    after(dve, "first_done", 2, b, 2)
                    v.tensor_reduce(fmax[:, :], first[:, :, :], axis=AX_X, op=ALU.max).then_inc(S["fmax_done"], 1)
                if i == 5:
                    after(dve, "fmax_done", 1, b, 1)
                    after(dve, "rank_ready", 1, b - 1, 1)
                    v.tensor_tensor(onehot[:, :, :], ranks, fmax[:, :].unsqueeze(2).to_broadcast([P, NT, E]),
                                    op=ALU.is_equal).then_inc(S["onehot_done"], 1)

            def place(b, par, i):
                m = m0_ps[:, 0:(NT + 1) * E].rearrange("p (t e) -> p t e", t=NT + 1)
                if i == 0:
                    after(dve, "rank_ready", 1, b, 1)
                    after(dve, "base_done", 1, b - 1, 1)
                    v.tensor_tensor(posm[:, :, :], m[:, 0:NT, :], base[:, :].unsqueeze(1).to_broadcast([P, NT, E]),
                                    op=ALU.add).then_inc(S["posm_done"], 1)
                if i == 1:
                    after(dve, "posm_done", 1, b, 1)
                    v.tensor_tensor(base[:, :], m[:, NT, :], base[:, :], op=ALU.add).then_inc(S["base_done"], 1)
                    v.tensor_tensor(posm[:, :, :], posm[:, :, :], onehot[:, :, :], op=ALU.mult)\
                        .then_inc(S["posm_sel"], 1)
                if i == 2:
                    after(dve, "posm_sel", 1, b, 1)
                    v.tensor_reduce(pos[:, :], posm[:, :, :], axis=AX_X, op=ALU.add).then_inc(S["pos_done"], 1)
                if i == 3:
                    after(dve, "pos_done", 1, b, 1)
                    after_scatter(dve, b - 2, par)
                    v.tensor_copy(pos_u[:, par, :], pos[:, :]).then_inc(S["pos_u_done"], 1)

            def step(s, p, qkv, mx, soft, close):
                b = s - 3
                xs = lambda t: xin[:, p, t, :]
                x1s = lambda t: pack[1 - p][:, t, D:2 * D]
                for h in range(2 * SLOTS):
                    q = h // 2
                    if h % 2 == 0 and tile_of(s, q) is not None:
                        tile(tile_of(s, q), tile_of(s, q), 0, 0)
                    if isinstance(s, int) and s == NB + 1 and h == 20:
                        early_table()
                    if qkv and h == AT["stats1"][0]:
                        after(dve, "x_loaded", 16, s, 16)
                        after(dve, "rstd1_add", 1, s - 1, 1)
                    for t in range(NT):
                        if qkv and h == AT["stats1"][t]:
                            layer_stats(xs, (t,), stats1, "ln1_stat")
                    if qkv and h == AT["mv1"]:
                        layer_mv(stats1, mv1, "ln1_stat", "ln1_mv", s)
                    if qkv and h == AT["xhat"][0]:
                        after(dve, "rstd1_done", 1, s, 1)
                        after(dve, "xT_ready", 1, s - 1, 1)
                    for t in range(NT):
                        if qkv and h == AT["xhat"][t]:
                            normalise(xhat, xs, (t,), mv1, rstd1, "xhat_done")
                    if isinstance(s, int) and s == 0 and h == AT["xhat"][NT - 1]:
                        setup_rest()
                    for i in range(2):
                        if h % (2 * GROUP_SLOTS) == AT["divide"][i]:
                            gr = (q // GROUP_SLOTS - 2) % NG
                            if gr >= 2 and close:
                                divide(b, gr, i)
                            if gr < 2 and soft:
                                divide(s - 2, gr, i)
                    if close and h == AT["x1"]:
                        after(dve, "proj_ready", 1, b, 1)
                        after(dve, "res_loaded", 48, b, 48)
                        after_scatter(dve, b - 2, 1 - p)
                        v.tensor_tensor(pack[1 - p][:, :, D:2 * D], m0_ps[:, :].rearrange("p (t d) -> p t d", t=NT),
                                        xres[:, 1 - p, :, :], op=ALU.add).then_inc(S["x1_done"], 1)
                    if close and h == AT["stats2"][0]:
                        after(dve, "x1_done", 1, b, 1)
                        after(dve, "rstd2_add", 1, b - 1, 1)
                    for t in range(NT):
                        if close and h == AT["stats2"][t]:
                            layer_stats(x1s, (t,), stats2, "ln2_stat")
                    if close and h == AT["mv2"]:
                        layer_mv(stats2, mv2, "ln2_stat", "ln2_mv", b)
                    if close and h == AT["xhat2"][0]:
                        after(dve, "rstd2_done", 1, b, 1)
                        after(dve, "h2m_done", 1, b - 1, 1)
                    for t in range(NT):
                        if close and h == AT["xhat2"][t]:
                            normalise(xhat2, x1s, (t,), mv2, rstd2, "xhat2_done")
                    for half, there, mb in ((0, mx, s - 1), (1, soft, s - 2)):
                        if there and h == AT["row_maxima"][half]:
                            row_maxima(mb, half)
                        for i in range(4):
                            if there and h == AT["negate"][half][i]:
                                negate(mb, half, i)
                    for i in range(6):
                        if close and h == AT["choose"][i]:
                            choose(b, i)
                    for i in range(4):
                        if close and h == AT["place"][i]:
                            place(b, 1 - p, i)
                    if mx and h % 2 == 0:
                        after(dve, "sn_ready", SLOTS, s - 1, q + 1)
                        v.tensor_reduce(bmax[:, q // 5, q % 5, :],
                                        sn_ps[:, q % 3, :].rearrange("p (k n) -> p k n", k=4),
                                        axis=AX_X, op=ALU.max).then_inc(S["sn_read"], 2)

            steps(dve, step)

            dve.wait_ge(S["base_done"], NB)
            v.tensor_copy(base_i[:, :], base[0:1, :]).then_inc(S["base_i_done"], 1)
            for k in range(RING, 2 * RING):
                tile(k, k % RING, 1, (k - 3) // RING)
                if k == RING:
                    count_all()
                if k == RING + 1:
                    count_rest()
                    end_tiles(nt_rest)
                if k == RING + 2:
                    list_tiles(TILES - EARLY, nt_step)
                if k == RING + 3:
                    place_tiles(EARLY, TILES - EARLY, taken[:, 0:1], "tab_done")
            dve.wait_ge(S["tab_done"], 1)
            with dve.Fori(2, TILES // RING) as n:
                for r in range(RING):
                    tile(RING * n + r, r, n, n if r >= 3 else n - 1)
            for k in range(TILES - 3, TILES):
                tile_close(k, k % RING, TILES // RING - 1)


_INS = ["L0_attn_x", "L0_attn_Wqkv", "L0_attn_Wproj", "L0_ffn_gate_W", "L0_ffn_gate_b", "L0_ffn_W1", "L0_ffn_b1",
        "L0_ffn_W2", "L0_ffn_b2", "L0_c", "L0_wmod"]


def kernel(**inputs):
    import numpy as _np
    import concourse.bacc as _bacc
    from concourse import mybir as _mybir
    from concourse.bass_utils import run_bass_kernel_spmd as _run

    nc = _bacc.Bacc("TRN2", target_bir_lowering=False, num_devices=1)
    arrays, args = {}, []
    for name in _INS:
        a = _np.ascontiguousarray(inputs[name])
        arrays[f"in_{name}_dram"] = a
        args.append(nc.dram_tensor(f"in_{name}_dram", a.shape, _mybir.dt.from_np(a.dtype), kind="ExternalInput").ap())
    shape = inputs["L0_attn_x"].shape
    args.append(nc.dram_tensor("out_0_dram", shape, F32, kind="ExternalOutput").ap())
    block_kernel(nc, *args)
    r = _run(nc, [arrays], core_ids=[0])
    return r.results[0]["out_0_dram"]
```
